# Optimizing a Trainium2 kernel written in Bass

```python
import numpy as np
import jax
import jax.numpy as jnp

def _softmax(x, axis=-1):
    return jax.nn.softmax(x, axis=axis)

def _gelu(x):
    return jax.nn.gelu(x, approximate=True)

def _silu(x):
    return jax.nn.silu(x)

def _sigmoid(x):
    return jax.nn.sigmoid(x)

def _layernorm(x, axis=-1, eps=1e-05):
    m = jnp.mean(x, axis=axis, keepdims=True)
    v = jnp.var(x, axis=axis, keepdims=True)
    return (x - m) / jnp.sqrt(v + eps)

def _scatter_add(tgt, idx, src, axis=0):
    return tgt.at[idx].add(src)

def _segment_sum(src, seg, n):
    return jax.ops.segment_sum(src, seg, n)
kernel_name = 'mk_adaln_d2_jaxref_r4_d1428e'

def setup_inputs(seed: int=0):
    np.random.seed(seed)
    _w = jnp.asarray

    def _L0_attn_setup():
        import jax, jax.numpy as jnp
        import numpy as np
        B, S, E, H, L = (2, 512, 512, 16, 128)
        HD = E // H

        def _reference_tuple_inner(x, Wq, Wdkv, Wuk, Wuv, ln_g, ln_b, Wo_h, Wo, bo):
            Bx, Sx, Ex = x.shape
            xh = x.reshape(Bx, Sx, H, HD).transpose(0, 2, 1, 3)
            c = jnp.einsum('bhsd,hld->bhsl', xh, Wdkv)
            mu = c.mean(-1, keepdims=True)
            var = c.var(-1, keepdims=True)
            c = (c - mu) * jax.lax.rsqrt(var + 1e-05)
            c = c * ln_g[None, :, None, :] + ln_b[None, :, None, :]
            absorbed = jnp.einsum('hij,hlj->hil', Wq, Wuk)
            q_lat = jnp.einsum('bhsd,hdl->bhsl', xh, absorbed)
            scores = jnp.einsum('bhsl,bhtl->bhst', q_lat, c)
            scores = scores * (1.0 / np.sqrt(L).astype(np.float32))
            mask = jnp.tril(jnp.ones((Sx, Sx), dtype=bool))
            scores = jnp.where(mask, scores, -jnp.inf)
            w = jax.nn.softmax(scores, axis=-1)
            v = jnp.einsum('bhsl,hld->bhsd', c, Wuv)
            oh = jnp.einsum('bhst,bhtd->bhsd', w, v)
            oh = jnp.einsum('bhsd,hed->bhse', oh, Wo_h)
            o = oh.transpose(0, 2, 1, 3).reshape(Bx, Sx, Ex)
            out = o @ Wo.T + bo
            return (out, c)
        key = jax.random.key(seed)
        ks = jax.random.split(key, 8)
        sd = 0.02
        return {'x': jax.random.normal(ks[0], (B, S, E), jnp.float32), 'Wq': jax.random.normal(ks[1], (H, HD, HD), jnp.float32) * sd, 'Wdkv': jax.random.normal(ks[2], (H, L, HD), jnp.float32) * sd, 'Wuk': jax.random.normal(ks[3], (H, L, HD), jnp.float32) * sd, 'Wuv': jax.random.normal(ks[4], (H, L, HD), jnp.float32) * sd, 'ln_g': jnp.ones((H, L), jnp.float32), 'ln_b': jnp.zeros((H, L), jnp.float32), 'Wo_h': jax.random.normal(ks[5], (H, HD, HD), jnp.float32) * sd, 'Wo': jax.random.normal(ks[6], (E, E), jnp.float32) * sd, 'bo': jnp.zeros((E,), jnp.float32)}
    _L0_attn_in = _L0_attn_setup()

    def _L0_ffn_setup():
        import jax, jax.numpy as jnp
        import numpy as np
        B, S, D = (4, 512, 512)
        E, K, M = (8, 2, 256)
        key = jax.random.key(seed)
        k0, k1, k2, k3, k4 = jax.random.split(key, 5)
        d_scale = D ** (-0.5)
        m_scale = M ** (-0.5)
        return {'x': jax.random.normal(k0, (B, S, D), jnp.float32), 'w_gate': jax.random.normal(k1, (D, E), jnp.float32) * d_scale, 'wi_0': jax.random.normal(k2, (E, D, M), jnp.float32) * d_scale, 'wi_1': jax.random.normal(k3, (E, D, M), jnp.float32) * d_scale, 'wo': jax.random.normal(k4, (E, M, D), jnp.float32) * m_scale}
    _L0_ffn_in = _L0_ffn_setup()
    _L0_c = _w((lambda *s: np.random.randn(*s).astype(np.float32) * 0.05)(2, 512))
    _L0_wmod = _w((lambda *s: np.random.randn(*s).astype(np.float32) * 0.05)(512, 6 * 512) * 512 ** (-0.5))

    def _L1_attn_setup():
        import jax, jax.numpy as jnp
        import numpy as np
        import math
        HIDDEN = 512
        NUM_HEADS = 16
        HEAD_SIZE = HIDDEN // NUM_HEADS
        BATCH = 2
        SEQ = 512
        key = jax.random.key(seed)
        k_x, k_wq, k_bq, k_wo, k_bo = jax.random.split(key, 5)
        scale_in = 1.0 / math.sqrt(HIDDEN)
        return {'x': jax.random.normal(k_x, (BATCH, SEQ, HIDDEN), dtype=jnp.float32), 'Wqkv': jax.random.normal(k_wq, (HIDDEN, 3 * HIDDEN), dtype=jnp.float32) * scale_in, 'bqkv': jax.random.normal(k_bq, (3 * HIDDEN,), dtype=jnp.float32) * 0.01, 'Wo': jax.random.normal(k_wo, (HIDDEN, HIDDEN), dtype=jnp.float32) * scale_in, 'bo': jax.random.normal(k_bo, (HIDDEN,), dtype=jnp.float32) * 0.01}
    _L1_attn_in = _L1_attn_setup()

    def _L1_ffn_setup():
        import jax, jax.numpy as jnp
        import numpy as np
        B, S, D, H = (4, 512, 512, 2048)

        def fwht(x):
            orig_shape = x.shape
            n = orig_shape[-1]
            x = x.reshape(-1, n)
            h = 1
            while h < n:
                xb = x.reshape(-1, n // (2 * h), 2, h)
                a = xb[:, :, 0, :]
                b = xb[:, :, 1, :]
                x = jnp.stack([a + b, a - b], axis=2).reshape(-1, n)
                h *= 2
            scale = jnp.asarray(1.0 / np.sqrt(n), dtype=x.dtype)
            return (x * scale).reshape(orig_shape)
        key = jax.random.key(seed)
        kx, k1, k2, k3 = jax.random.split(key, 4)
        x = jax.random.normal(kx, (B, S, D), dtype=jnp.float32)
        W1 = jax.random.normal(k1, (H, D), dtype=jnp.float32) * (1.0 / np.sqrt(D))
        W2 = jax.random.normal(k2, (D, H), dtype=jnp.float32) * (1.0 / np.sqrt(H))
        W3 = jax.random.normal(k3, (H, D), dtype=jnp.float32) * (1.0 / np.sqrt(D))
        return {'x': x, 'W1': W1, 'W2': W2, 'W3': W3}
    _L1_ffn_in = _L1_ffn_setup()
    _L1_c = _w((lambda *s: np.random.randn(*s).astype(np.float32) * 0.05)(2, 512))
    _L1_wmod = _w((lambda *s: np.random.randn(*s).astype(np.float32) * 0.05)(512, 6 * 512) * 512 ** (-0.5))
    _d = {'L0_attn_x': _L0_attn_in['x'], 'L0_attn_Wq': _L0_attn_in['Wq'], 'L0_attn_Wdkv': _L0_attn_in['Wdkv'], 'L0_attn_Wuk': _L0_attn_in['Wuk'], 'L0_attn_Wuv': _L0_attn_in['Wuv'], 'L0_attn_ln_g': _L0_attn_in['ln_g'], 'L0_attn_ln_b': _L0_attn_in['ln_b'], 'L0_attn_Wo_h': _L0_attn_in['Wo_h'], 'L0_attn_Wo': _L0_attn_in['Wo'], 'L0_attn_bo': _L0_attn_in['bo'], 'L0_ffn_w_gate': _L0_ffn_in['w_gate'], 'L0_ffn_wi_0': _L0_ffn_in['wi_0'], 'L0_ffn_wi_1': _L0_ffn_in['wi_1'], 'L0_ffn_wo': _L0_ffn_in['wo'], 'L0_c': _L0_c, 'L0_wmod': _L0_wmod, 'L1_attn_Wqkv': _L1_attn_in['Wqkv'], 'L1_attn_bqkv': _L1_attn_in['bqkv'], 'L1_attn_Wo': _L1_attn_in['Wo'], 'L1_attn_bo': _L1_attn_in['bo'], 'L1_ffn_W1': _L1_ffn_in['W1'], 'L1_ffn_W2': _L1_ffn_in['W2'], 'L1_ffn_W3': _L1_ffn_in['W3'], 'L1_c': _L1_c, 'L1_wmod': _L1_wmod}
    _x0 = _d['L0_attn_x']
    _d['L0_attn_x'] = jax.random.normal(jax.random.fold_in(jax.random.key(seed), 1), (2, 1024, 512), dtype=_x0.dtype)
    del _x0
    return _d

def reference(L0_attn_x, L0_attn_Wq, L0_attn_Wdkv, L0_attn_Wuk, L0_attn_Wuv, L0_attn_ln_g, L0_attn_ln_b, L0_attn_Wo_h, L0_attn_Wo, L0_attn_bo, L0_ffn_w_gate, L0_ffn_wi_0, L0_ffn_wi_1, L0_ffn_wo, L0_c, L0_wmod, L1_attn_Wqkv, L1_attn_bqkv, L1_attn_Wo, L1_attn_bo, L1_ffn_W1, L1_ffn_W2, L1_ffn_W3, L1_c, L1_wmod):

    def _L0_attn_ref(x, Wq, Wdkv, Wuk, Wuv, ln_g, ln_b, Wo_h, Wo, bo):
        import jax, jax.numpy as jnp
        import numpy as np
        B, S, E, H, L = (2, 512, 512, 16, 128)
        HD = E // H

        def _reference_tuple_inner(x, Wq, Wdkv, Wuk, Wuv, ln_g, ln_b, Wo_h, Wo, bo):
            Bx, Sx, Ex = x.shape
            xh = x.reshape(Bx, Sx, H, HD).transpose(0, 2, 1, 3)
            c = jnp.einsum('bhsd,hld->bhsl', xh, Wdkv)
            mu = c.mean(-1, keepdims=True)
            var = c.var(-1, keepdims=True)
            c = (c - mu) * jax.lax.rsqrt(var + 1e-05)
            c = c * ln_g[None, :, None, :] + ln_b[None, :, None, :]
            absorbed = jnp.einsum('hij,hlj->hil', Wq, Wuk)
            q_lat = jnp.einsum('bhsd,hdl->bhsl', xh, absorbed)
            scores = jnp.einsum('bhsl,bhtl->bhst', q_lat, c)
            scores = scores * (1.0 / np.sqrt(L).astype(np.float32))
            mask = jnp.tril(jnp.ones((Sx, Sx), dtype=bool))
            scores = jnp.where(mask, scores, -jnp.inf)
            w = jax.nn.softmax(scores, axis=-1)
            v = jnp.einsum('bhsl,hld->bhsd', c, Wuv)
            oh = jnp.einsum('bhst,bhtd->bhsd', w, v)
            oh = jnp.einsum('bhsd,hed->bhse', oh, Wo_h)
            o = oh.transpose(0, 2, 1, 3).reshape(Bx, Sx, Ex)
            out = o @ Wo.T + bo
            return (out, c)
        return _reference_tuple_inner(x, Wq, Wdkv, Wuk, Wuv, ln_g, ln_b, Wo_h, Wo, bo)[0]

    def _L0_ffn_ref(x, w_gate, wi_0, wi_1, wo):
        import jax, jax.numpy as jnp
        import numpy as np
        B, S, D = (4, 512, 512)
        E, K, M = (8, 2, 256)
        b, s, d = x.shape
        e = w_gate.shape[1]
        xf = x.reshape(-1, d)
        logits = jnp.dot(xf, w_gate)
        top_logits, top_idx = jax.lax.top_k(logits, K)
        weights = jax.nn.softmax(top_logits, axis=-1)
        flat_idx = top_idx.reshape(-1)
        sort_order = jnp.argsort(flat_idx)
        token_ids = sort_order // K
        sorted_x = jnp.take(xf, token_ids, axis=0)
        group_sizes = jnp.bincount(flat_idx, length=E).astype(jnp.int32)
        h0 = jax.lax.ragged_dot(sorted_x, wi_0, group_sizes)
        h1 = jax.lax.ragged_dot(sorted_x, wi_1, group_sizes)
        inter = jax.nn.silu(h0) * h1
        out_sorted = jax.lax.ragged_dot(inter, wo, group_sizes)
        unsort = jnp.argsort(sort_order)
        out = jnp.take(out_sorted, unsort, axis=0).reshape(-1, K, d)
        out = jnp.einsum('tkd,tk->td', out, weights)
        return out.reshape(b, s, d)

    def _L1_attn_ref(x, Wqkv, bqkv, Wo, bo):
        import jax, jax.numpy as jnp
        import numpy as np
        import math
        HIDDEN = 512
        NUM_HEADS = 16
        HEAD_SIZE = HIDDEN // NUM_HEADS
        BATCH = 2
        SEQ = 512
        b, s, _ = x.shape
        kqv = x @ Wqkv + bqkv
        kqv = kqv.reshape(b, s, 3, NUM_HEADS, HEAD_SIZE)
        q = kqv[:, :, 0]
        k = kqv[:, :, 1]
        v = kqv[:, :, 2]
        scores = jnp.einsum('bsnh,btnh->bnst', k, q) / math.sqrt(HEAD_SIZE)
        ones = jnp.ones_like(scores)
        scores = jnp.triu(scores) + -10000.0 * jnp.tril(ones, k=-1)
        attn = jax.nn.softmax(scores, axis=2)
        out = jnp.einsum('bnkq,bknh->bqnh', attn, v)
        out = out.reshape(b, s, NUM_HEADS * HEAD_SIZE)
        return out @ Wo + bo

    def _L1_ffn_ref(x, W1, W2, W3):
        import jax, jax.numpy as jnp
        import numpy as np
        B, S, D, H = (4, 512, 512, 2048)

        def fwht(x):
            orig_shape = x.shape
            n = orig_shape[-1]
            x = x.reshape(-1, n)
            h = 1
            while h < n:
                xb = x.reshape(-1, n // (2 * h), 2, h)
                a = xb[:, :, 0, :]
                b = xb[:, :, 1, :]
                x = jnp.stack([a + b, a - b], axis=2).reshape(-1, n)
                h *= 2
            scale = jnp.asarray(1.0 / np.sqrt(n), dtype=x.dtype)
            return (x * scale).reshape(orig_shape)
        up_gate = jnp.einsum('bsd,hd->bsh', x, W1)
        up_lin = jnp.einsum('bsd,hd->bsh', x, W3)
        hidden = jax.nn.silu(up_gate) * up_lin
        hidden = fwht(hidden)
        out = jnp.einsum('bsh,dh->bsd', hidden, W2)
        return out
    x = L0_attn_x
    mod = (_silu(L0_c) @ L0_wmod).reshape(L0_c.shape[0], 6, 1, -1)
    sa, ca, ga, sb, cb, gb = (mod[:, 0], mod[:, 1], mod[:, 2], mod[:, 3], mod[:, 4], mod[:, 5])
    ga = (2 * (ga >= 0) - 1) * jnp.maximum(jnp.abs(ga), 0.25)
    gb = (2 * (gb >= 0) - 1) * jnp.maximum(jnp.abs(gb), 0.25)
    h = _layernorm(x, axis=-1) * (1 + ca) + sa
    x = x + ga * _L0_attn_ref(h, L0_attn_Wq, L0_attn_Wdkv, L0_attn_Wuk, L0_attn_Wuv, L0_attn_ln_g, L0_attn_ln_b, L0_attn_Wo_h, L0_attn_Wo, L0_attn_bo)
    h = _layernorm(x, axis=-1) * (1 + cb) + sb
    x = x + gb * _L0_ffn_ref(h, L0_ffn_w_gate, L0_ffn_wi_0, L0_ffn_wi_1, L0_ffn_wo)
    mod = (_silu(L1_c) @ L1_wmod).reshape(L1_c.shape[0], 6, 1, -1)
    sa, ca, ga, sb, cb, gb = (mod[:, 0], mod[:, 1], mod[:, 2], mod[:, 3], mod[:, 4], mod[:, 5])
    ga = (2 * (ga >= 0) - 1) * jnp.maximum(jnp.abs(ga), 0.25)
    gb = (2 * (gb >= 0) - 1) * jnp.maximum(jnp.abs(gb), 0.25)
    h = _layernorm(x, axis=-1) * (1 + ca) + sa
    x = x + ga * _L1_attn_ref(h, L1_attn_Wqkv, L1_attn_bqkv, L1_attn_Wo, L1_attn_bo)
    h = _layernorm(x, axis=-1) * (1 + cb) + sb
    x = x + gb * _L1_ffn_ref(h, L1_ffn_W1, L1_ffn_W2, L1_ffn_W3)
    return x

_drawn_inputs = setup_inputs


def setup_inputs(seed=0):
    import zlib

    import numpy as np

    out = dict(_drawn_inputs(seed))
    spreads = {'L0_attn_ln_g': (1.0, 0.6), 'L0_attn_ln_b': (0.0, 0.8), 'L0_attn_bo': (0.0, 0.28)}
    factors = {'L0_attn_Wq': 8.0,
     'L0_attn_Wdkv': 8.0,
     'L0_attn_Wuk': 8.0,
     'L0_attn_Wuv': 8.0,
     'L0_attn_Wo_h': 8.0,
     'L0_attn_Wo': 8.0,
     'L1_attn_bqkv': 38.453,
     'L1_attn_bo': 38.911}
    for name, (base, spread) in spreads.items():
        noise = np.random.default_rng([zlib.crc32(name.encode()), seed]).standard_normal(out[name].shape)
        drawn = base * np.exp(spread * noise) if base else spread * noise
        out[name] = jnp.asarray(drawn.astype(out[name].dtype))
    for name, factor in factors.items():
        out[name] = (out[name] * factor).astype(out[name].dtype)
    return out
```

```python
from contextlib import ExitStack

import concourse.bass as bass
import numpy as np
from concourse import mybir

P = 128
B, S, D = 2, 1024, 512
TOK = B * S
NT = TOK // P
KC = D // P
H, HD, LAT = 16, 32, 128
HG = P // HD
QB = S // P
QC = 512
NH = S // QC
E, M = 8, 256
F = 2048
FC = F // P
EPS = 1e-5
NEG = -1e30

ALU = mybir.AluOpType
ACT = mybir.ActivationFunctionType
AX = mybir.AxisListType
F32 = mybir.dt.float32
FR = mybir.dt.float32r
BF16 = mybir.dt.bfloat16


class Shared:
    pass


C_ID, C_BLK, C_HAD, C_NEG, C_SEL = 0, P, 2 * P, 3 * P, 4 * P
C_END = C_SEL + E * P


def constant_table():
    t = np.zeros((P, C_END), np.float32)
    t[:, C_ID:C_ID + P] = np.eye(P)
    blk = np.arange(P) // HD
    t[:, C_BLK:C_BLK + P] = blk[:, None] == blk[None, :]
    had = np.ones((1, 1))
    while had.shape[0] < P:
        had = np.block([[had, had], [had, -had]])
    t[:, C_HAD:C_HAD + P] = had / np.sqrt(F)
    t[:, C_NEG:C_NEG + P] = np.where(np.arange(P)[None, :] > np.arange(P)[:, None], NEG, 0.0)
    for e in range(E):
        t[e, C_SEL + e * P:C_SEL + (e + 1) * P] = 1.0
    return t


def chained(eng, sem):
    count = [0]

    def link(ins):
        count[0] += 1
        ins.then_inc(sem, 1)
        eng.wait_ge(sem, count[0])
    return link


def spread(ap, shape):
    return ap.broadcast_to(shape)


def modulation(nc, ctx, t, sem, psum):
    cT = t.at("cT", [P, 2, KC, B], F32, 64)
    sT = t.at("sT", [P, 2 * KC * B], F32, 65)
    sB = t.at("sB", [P, 2 * KC * B, P], F32, 66)
    ring = [t.at(f"wmod_ring{i}", [P, KC, D], F32, 76 + 8 * i) for i in range(4)]
    t1 = t.at("gate_abs", [P, D], F32, 110)
    t2 = t.at("gate_sign", [P, D], F32, 112)
    s_const, s_c, s_w = sem("mod_const"), sem("mod_c"), [sem(f"mod_w{i}") for i in range(4)]
    s_silu, s_sb, s_ps, s_ev, s_chain = (sem(n) for n in
                                         ("mod_silu", "mod_sb", "mod_ps", "mod_ev", "mod_chain"))
    sections = [(layer, s) for layer in range(2) for s in range(6)]

    with nc.Block() as block:
        @block.sync
        def _(sp):
            sp.dma_start(t.const[:, :], t.d_const).then_inc(s_const, 16)
            for layer in range(2):
                for b in range(B):
                    src = t.d_c[layer][b, :].rearrange("(k p) -> p k", p=P)
                    sp.dma_start(cT[:, layer, :, b], src, allow_slow_non_contiguous=True).then_inc(s_c, 16)
            for n, (layer, s) in enumerate(sections):
                if n >= 4:
                    sp.wait_ge(s_ps, n - 3)
                src = t.d_wmod[layer].rearrange("(k p) n -> p k n", p=P)[:, :, s * D:(s + 1) * D]
                sp.dma_start(ring[n % 4][:, :, :], src).then_inc(s_w[n % 4], 16)

        @block.scalar
        def _(act):
            act.wait_ge(s_c, 64)
            nc.scalar.activation(sT[:, :], cT[:, :, :, :].rearrange("p l k b -> p (l k b)"),
                                 ACT.Silu).then_inc(s_silu, 1)

        @block.vector
        def _(dve):
            link = chained(dve, s_chain)
            dve.wait_ge(s_const, 16)
            link(nc.vector.tensor_copy(t.ident_bf[:, :], t.ident))
            link(nc.vector.tensor_copy(t.neg_bf[:, :], t.neg))
            link(nc.vector.memset(t.avg[:, :], 1.0 / P))
            dve.wait_ge(s_silu, 1)
            nc.vector.tensor_copy(sB[:, :, :], spread(sT[:, :].unsqueeze(2), [P, 2 * KC * B, P])).then_inc(s_sb, 1)
            for n, (layer, s) in enumerate(sections):
                dve.wait_ge(s_ps, n + 1)
                bank = psum[2 * (n % 2)]
                if s in (2, 5):
                    for b in range(B):
                        ps = psum[2 * (n % 2) + b]
                        link(nc.vector.tensor_scalar(t2[:, :], ps[:, :], 0.25, None, ALU.max))
                        link(nc.vector.scalar_tensor_tensor(out=t1[:, :], in0=ps[:, :], scalar=-1.0, in1=t2[:, :],
                                                            op0=ALU.mult, op1=ALU.max))
                        link(nc.vector.tensor_scalar(t2[:, :], ps[:, :], 0.0, 2.0, ALU.is_ge, ALU.mult))
                        ins = nc.vector.scalar_tensor_tensor(
                            out=t.gate[:, layer, s // 3, b, :], in0=t2[:, :], scalar=-1.0, in1=t1[:, :],
                            op0=ALU.add, op1=ALU.mult)
                        if b == 0:
                            link(ins)
                        else:
                            ins.then_inc(s_ev, 1)
                            dve.wait_ge(s_ev, n + 1)
                else:
                    one = 1.0 if s in (1, 4) else 0.0
                    nc.vector.tensor_scalar(
                        t.mod[:, layer, 2 * (s // 3) + s % 3, :], bank[:, 0:KC * B], one, None,
                        ALU.add).then_inc(s_ev, 1)

        @block.tensor
        def _(pe):
            pe.wait_ge(s_sb, 1)
            for n, (layer, s) in enumerate(sections):
                pe.wait_ge(s_w[n % 4], 16 * (n // 4 + 1))
                if n >= 2:
                    pe.wait_ge(s_ev, n - 1)
                w = ring[n % 4]
                if s in (2, 5):
                    for b in range(B):
                        for k in range(KC):
                            mm = nc.tensor.matmul(psum[2 * (n % 2) + b][:, :], sB[:, (layer * KC + k) * B + b, :],
                                                  w[:, k, :], start=(k == 0), stop=(k == KC - 1))
                else:
                    for j in range(KC):
                        for k in range(KC):
                            at = (layer * KC + k) * B
                            mm = nc.tensor.matmul(psum[2 * (n % 2)][:, j * B:(j + 1) * B],
                                                  w[:, k, j * P:(j + 1) * P], sT[:, at:at + B],
                                                  start=(k == 0), stop=(k == KC - 1))
                mm.then_inc(s_ps, 1)


def latent_weights(nc, ctx, t, sem, psum):
    W = {n: t.at("nat_" + n, [P, H * HD], F32, 116 + 2 * i) for i, n in enumerate(("dkv", "uk", "uv"))}
    S2 = {n: t.at("nat_" + n, [P, KC, HD], F32, 122 + i) for i, n in enumerate(("q", "o"))}
    lng = t.at("lngT", [P, H], F32, 124)
    lnb = t.at("lnbT", [P, H], F32, 125)
    wc = t.at("wc", [P, D], F32, 126)
    wg = t.at("wg", [P, D], F32, 128)
    mt = {n: t.at("mid_" + n, [P, D], F32, 130 + 2 * i) for i, n in enumerate(("uk", "uv"))}
    nat = {n: t.at("bdn_" + n, [P, D], F32, 134 + 2 * i) for i, n in enumerate(("q", "o"))}
    bdt = {n: t.at("bdt_" + n, [P, D], F32, 138 + 2 * i) for i, n in enumerate(("q", "o"))}
    own = t.at("own_head", [P, KC, HG], F32, 142)
    col = {n: t.at("col_" + n, [P, KC], F32, 143 + i) for i, n in enumerate(("uk", "uv"))}
    s_w, s_pe, s_dve, s_chain = sem("lat_w"), sem("lat_pe"), sem("lat_dve"), sem("lat_chain")
    pairs = (("uk", "q"), ("uv", "o"))

    def blk4(ap):
        return ap.rearrange("p (g c) -> p g c", g=KC)

    with nc.Block() as block:
        @block.sync
        def _(sp):
            for n, src in (("dkv", t.d_Wdkv), ("uk", t.d_Wuk), ("uv", t.d_Wuv)):
                sp.dma_start(W[n][:, :].rearrange("l (h d) -> l h d", h=H),
                             src.rearrange("h l d -> l h d")).then_inc(s_w, 16)
            for n, src in (("q", t.d_Wq), ("o", t.d_Woh)):
                sp.dma_start(S2[n][:, :, :], src.rearrange("(g a) i j -> (a i) g j", a=HG)).then_inc(s_w, 16)
            for dst, src in ((lng, t.d_lng), (lnb, t.d_lnb)):
                sp.dma_start(dst[:, :], src.rearrange("h l -> l h"),
                             allow_slow_non_contiguous=True).then_inc(s_w, 16)

        @block.tensor
        def _(pe):
            pe.wait_ge(s_w, 16 * 7)
            nc.tensor.matmul(psum[0][:, :], t.avg[:, :], W["dkv"][:, :], start=True, stop=True).then_inc(s_pe, 1)
            pe.wait_ge(s_dve, 1)
            for g in range(KC):
                c = slice(g * P, (g + 1) * P)
                nc.tensor.matmul(psum[1][:, c], wc[:, c], wc[:, c], start=True, stop=True)
                for i, (n, m) in enumerate(pairs):
                    nc.tensor.matmul(psum[2 + i][:, c], W[n][:, c], wg[:, c], start=True, stop=True)
                    nc.tensor.transpose(psum[4 + i][:, c], nat[m][:, c], t.ident)
                    mm = nc.tensor.matmul(psum[6][:, (i * KC + g) * HG:(i * KC + g + 1) * HG], W[n][:, c],
                                          lnb[:, g * HG:(g + 1) * HG], start=True, stop=True)
            mm.then_inc(s_pe, 1)
            pe.wait_ge(s_dve, 2)
            for i, (n, m) in enumerate(pairs):
                for g in range(KC):
                    c = slice(g * P, (g + 1) * P)
                    nc.tensor.matmul(psum[2 + i][:, c], mt[n][:, c], bdt[m][:, c], start=True, stop=True)
                    mm = nc.tensor.matmul(psum[7][:, i * KC + g:i * KC + g + 1], bdt[m][:, c],
                                          col[n][:, g:g + 1], start=True, stop=True)
            mm.then_inc(s_pe, 1)

        @block.vector
        def _(dve):
            link = chained(dve, s_chain)
            blk = t.blk.unsqueeze(1).broadcast_to([P, KC, P])
            dve.wait_ge(s_w, 16 * 7)
            dve.wait_ge(s_pe, 1)
            link(nc.vector.tensor_tensor(wc[:, :], W["dkv"][:, :], psum[0][:, :], ALU.subtract))
            link(nc.vector.tensor_tensor(wg[:, :].rearrange("l (h d) -> l h d", h=H),
                                         wc[:, :].rearrange("l (h d) -> l h d", h=H),
                                         lng[:, :].unsqueeze(2).broadcast_to([P, H, HD]), ALU.mult))
            for _, m in pairs:
                for g in range(KC):
                    ins = nc.vector.tensor_tensor(
                        nat[m][:, g * P:(g + 1) * P].rearrange("p (a j) -> p a j", a=HG),
                        S2[m][:, g, :].unsqueeze(1).broadcast_to([P, HG, HD]),
                        t.blk.rearrange("p (a j) -> p a j", a=HG), ALU.mult)
            ins.then_inc(s_dve, 1)
            dve.wait_ge(s_pe, 2)
            nc.vector.scalar_tensor_tensor(out=blk4(t.bd_m[:, :]), in0=blk4(psum[1][:, :]), scalar=1.0 / LAT,
                                           in1=blk, op0=ALU.mult, op1=ALU.mult)
            for i, (n, m) in enumerate(pairs):
                nc.vector.tensor_tensor(blk4(mt[n][:, :]), blk4(psum[2 + i][:, :]), blk, ALU.mult)
                nc.vector.tensor_copy(bdt[m][:, :], psum[4 + i][:, :])
                part = psum[6][:, i * KC * HG:(i + 1) * KC * HG].rearrange("p (g a) -> p g a", a=HG)
                link(nc.vector.tensor_tensor(own[:, :, :], part,
                                             t.blk4.unsqueeze(1).broadcast_to([P, KC, HG]), ALU.mult))
                link(nc.vector.tensor_reduce(col[n][:, :], own[:, :, :], AX.X, ALU.add))
            dve.wait_ge(s_chain, 6)
            nc.vector.memset(own[:, 0, 0:1], 0.0).then_inc(s_dve, 1)
            dve.wait_ge(s_pe, 3)
            scale = float(LAT) ** -0.5
            link(nc.vector.tensor_scalar(t.bd_k[:, :], psum[2][:, :], scale, None, ALU.mult))
            link(nc.vector.tensor_copy(t.bd_v[:, :], psum[3][:, :]))
            link(nc.vector.tensor_scalar(t.kb[:, :], psum[7][:, 0:KC], scale, None, ALU.mult))
            link(nc.vector.tensor_copy(t.vb[:, :], psum[7][:, KC:2 * KC]))


def layer_norm(nc, ctx, t, sem, psum, x, h, layer, half, name, load=None, save=None, tmp=128):
    xn = [t.at(f"{name}_xn{i}", [P, 4, D], F32, tmp + 8 * i) for i in range(2)]
    stats = t.at(f"{name}_stats", [P, NT, 6], F32, tmp + 16)
    mv = t.at(f"{name}_mv", [P, NT, 2], F32, tmp + 17)
    std = t.at(f"{name}_std", [P, NT], F32, tmp + 18)
    s_x, s_chain, s_var, s_std, s_xn, s_tr, s_ev, s_sv = (
        sem(f"{name}_{n}") for n in ("x", "chain", "var", "std", "xn", "tr", "ev", "sv"))
    GR = NT // 4
    with nc.Block() as block:
        @block.sync
        def _(sp):
            if load is not None:
                for g in range(GR):
                    sp.dma_start(x[:, 4 * g:4 * g + 4, :], load[:, 4 * g:4 * g + 4, :]).then_inc(s_x, 16)
            if save is not None:
                sp.dma_start(save, x[:, :, :]).then_inc(s_sv, 16)
                sp.wait_ge(s_sv, 16)

        @block.vector
        def _(dve):
            link = chained(dve, s_chain)
            if load is not None:
                dve.wait_ge(s_x, 16 * GR)
            for i in range(NT):
                ins = nc.vector.bn_stats(stats[:, i, :], x[:, i, :])
            link(ins)
            for i in range(NT):
                ins = nc.vector.bn_aggr(mv[:, i, :], stats[:, i, :])
            link(ins)
            nc.vector.tensor_scalar(std[:, :], mv[:, :, 1], EPS, None, ALU.add).then_inc(s_var, 1)
            dve.wait_ge(s_std, 1)
            link(nc.vector.reciprocal(std[:, :], std[:, :]))
            for g in range(GR):
                if g >= 2:
                    dve.wait_ge(s_tr, g - 1)
                for i in range(4):
                    n = 4 * g + i
                    ins = nc.vector.tensor_scalar(xn[g % 2][:, i, :], x[:, n, :], mv[:, n, 0:1], std[:, n:n + 1],
                                                  ALU.subtract, ALU.mult)
                ins.then_inc(s_xn, 1)

        @block.tensor
        def _(pe):
            for g in range(GR):
                pe.wait_ge(s_xn, g + 1)
                if g >= 2:
                    pe.wait_ge(s_ev, 4 * (g - 1))
                for k in range(KC):
                    for i in range(4):
                        mm = nc.tensor.transpose(psum[4 * (g % 2) + k][:, i * P:(i + 1) * P],
                                                 xn[g % 2][:, i, k * P:(k + 1) * P], t.ident)
                mm.then_inc(s_tr, 1)

        @block.scalar
        def _(act):
            act.wait_ge(s_var, 1)
            nc.scalar.activation(std[:, :], std[:, :], ACT.Sqrt).then_inc(s_std, 1)
            for g in range(GR):
                act.wait_ge(s_tr, g + 1)
                b = g // NH
                for k in range(KC):
                    at = k * B + b
                    dst = h[:, b, k, (g % NH) * QC:(g % NH + 1) * QC] if half == 0 else h[:, g, k, :]
                    nc.scalar.activation(dst, psum[4 * (g % 2) + k][:, :],
                                         ACT.Identity, scale=t.mod[:, layer, 2 * half + 1, at:at + 1],
                                         bias=t.mod[:, layer, 2 * half, at:at + 1]).then_inc(s_ev, 1)


def latent_keys_values(nc, ctx, t, sem, psum, h, k_all, v_all):
    prod = [t.at(f"lat_prod{i}", [P, S], F32, 128 + 4 * i) for i in range(2)]
    rstd = [t.at(f"lat_rstd{i}", [P, QC], F32, 136 + 2 * i) for i in range(2)]
    tmp = [t.at(f"lat_tmp{i}", [P, QC], F32, 140 + 2 * i) for i in range(2)]
    rt = t.at("lat_rt", [P, B * KC, QB, HG], F32, 144)
    s_y, s_prod, s_var, s_std, s_rec, s_kraw, s_mul, s_vt, s_chain, s_rt, s_v, s_vev, s_add, s_rtd = (
        sem(f"lkv_{n}") for n in ("y", "prod", "var", "std", "rec", "kraw", "mul", "vt", "chain", "rt", "v",
                                  "vev", "add", "rtd"))
    NI = B * KC
    PY, PV, PK = psum[0:2], psum[2:4], psum[4:6]
    VT = psum[6]
    with nc.Block() as block:
        @block.tensor
        def _(pe):
            def second(n):
                i, c = divmod(n, NH)
                b, g = divmod(i, KC)
                cs = slice(c * QC, (c + 1) * QC)
                gs = slice(g * P, (g + 1) * P)
                pe.wait_ge(s_prod, n + 1)
                if n >= 2:
                    pe.wait_ge(s_std, n - 1)
                nc.tensor.matmul(PV[n % 2][:, :], t.blk, prod[i % 2][:, cs], start=True, stop=True).then_inc(s_var, 1)
                for q in range(QC // P):
                    at = (i * QB + c * (QC // P) + q) * HG
                    mm = nc.tensor.matmul(VT[:, at:at + HG], prod[i % 2][:, c * QC + q * P:c * QC + (q + 1) * P],
                                          t.blk4, start=True, stop=True)
                mm.then_inc(s_vt, 1)
                if n >= 2:
                    pe.wait_ge(s_mul, n - 1)
                nc.tensor.matmul(PK[n % 2][:, :], t.bd_k[:, gs], h[:, b, g, cs], start=True,
                                 stop=True).then_inc(s_kraw, 1)

            for n in range(NI * NH):
                i, c = divmod(n, NH)
                b, g = divmod(i, KC)
                if n >= 2:
                    pe.wait_ge(s_prod, n - 1)
                nc.tensor.matmul(PY[n % 2][:, :], t.bd_m[:, g * P:(g + 1) * P], h[:, b, g, c * QC:(c + 1) * QC],
                                 start=True, stop=True).then_inc(s_y, 1)
                if n >= 1:
                    second(n - 1)
            second(NI * NH - 1)
            pe.wait_ge(s_mul, NI * NH)
            for n in range(NI * NH):
                i, c = divmod(n, NH)
                b, g = divmod(i, KC)
                if n >= 4:
                    pe.wait_ge(s_vev, n - 3)
                for q in range(QC // P):
                    at = c * QC + q * P
                    mm = nc.tensor.matmul(psum[n % 4][:, q * P:(q + 1) * P], h[:, b, g, at:at + P],
                                          t.bd_v[:, g * P:(g + 1) * P], start=True, stop=True)
                mm.then_inc(s_v, 1)

        @block.vector
        def _(dve):
            def keys(n):
                i, c = divmod(n, NH)
                b, g = divmod(i, KC)
                dve.wait_ge(s_std, n + 1)
                nc.vector.reciprocal(rstd[n % 2][:, :], rstd[n % 2][:, :]).then_inc(s_rec, 1)
                dve.wait_ge(s_rec, n + 1)
                dve.wait_ge(s_kraw, n + 1)
                if n >= 2:
                    dve.wait_ge(s_add, n - 1)
                nc.vector.tensor_tensor(tmp[n % 2][:, :], PK[n % 2][:, :], rstd[n % 2][:, :],
                                        ALU.mult).then_inc(s_mul, 1)

            for n in range(NI * NH):
                i, c = divmod(n, NH)
                b, g = divmod(i, KC)
                dve.wait_ge(s_y, n + 1)
                if n >= 4:
                    dve.wait_ge(s_vt, n - 3)
                nc.vector.tensor_tensor(prod[i % 2][:, c * QC:(c + 1) * QC], PY[n % 2][:, :],
                                        h[:, b, g, c * QC:(c + 1) * QC], ALU.mult).then_inc(s_prod, 1)
                if n >= 1:
                    keys(n - 1)
            keys(NI * NH - 1)
            dve.wait_ge(s_vt, NI * NH)
            nc.vector.tensor_scalar(rt[:, :, :, :].rearrange("p i q a -> p (i q a)"), VT[:, 0:NI * QB * HG], EPS,
                                    None, ALU.add).then_inc(s_rt, 1)
            dve.wait_ge(s_rtd, 1)
            nc.vector.reciprocal(rt[:, :, :, :], rt[:, :, :, :]).then_inc(s_rt, 1)
            dve.wait_ge(s_rt, 2)
            for n in range(NI * NH):
                i, c = divmod(n, NH)
                dve.wait_ge(s_v, n + 1)
                q = slice(c * (QC // P), (c + 1) * (QC // P))
                nc.vector.tensor_tensor(
                    v_all[:, i, q, :].rearrange("p q (a d) -> p (q a) d", a=HG),
                    psum[n % 4][:, :].rearrange("p (c d) -> p c d", d=HD),
                    rt[:, i, q, :].rearrange("p q a -> p (q a)").unsqueeze(2).broadcast_to([P, QC // HD, HD]),
                    ALU.mult).then_inc(s_vev, 1)

        @block.scalar
        def _(act):
            for n in range(NI * NH):
                act.wait_ge(s_var, n + 1)
                if n >= 2:
                    act.wait_ge(s_mul, n - 1)
                nc.scalar.activation(rstd[n % 2][:, :], PV[n % 2][:, :], ACT.Sqrt, bias=t.eps[:, 0:1]).then_inc(s_std, 1)
            act.wait_ge(s_rt, 1)
            nc.scalar.activation(rt[:, :, :, :], rt[:, :, :, :], ACT.Sqrt).then_inc(s_rtd, 1)

        @block.gpsimd
        def _(pool):
            for n in range(NI * NH):
                i, c = divmod(n, NH)
                pool.wait_ge(s_mul, n + 1)
                nc.gpsimd.tensor_scalar(k_all[:, i, c * QC:(c + 1) * QC], tmp[n % 2][:, :],
                                        t.kb[:, i % KC:i % KC + 1], None, ALU.add).then_inc(s_add, 1)


def project_qkv(nc, ctx, t, sem, psum, h, q_all, k_all, v_all):
    w = t.at("wqkv", [P, KC, 3 * D], F32, 128)
    bias = t.at("bqkv", [P, 3 * KC], F32, 152)
    s_w, s_ps, s_ev, s_b, s_chain = (sem(f"qkv_{n}") for n in ("w", "ps", "ev", "b", "chain"))
    NG = B * KC * NH
    with nc.Block() as block:
        @block.sync
        def _(sp):
            for k in range(KC):
                sp.dma_start(w[:, k, :], t.d_Wqkv[k * P:(k + 1) * P, :]).then_inc(s_w, 16)
            sp.dma_start(bias[:, :], t.d_bqkv.rearrange("(c p) -> p c", p=P),
                         allow_slow_non_contiguous=True).then_inc(s_b, 16)

        @block.tensor
        def _(pe):
            pe.wait_ge(s_w, 16 * KC)
            n = 0
            for i in range(B * KC):
                b, g = divmod(i, KC)
                for c in range(NH):
                    for part in range(2):
                        if n >= 8:
                            pe.wait_ge(s_ev, n - 7)
                        for k in range(KC):
                            mm = nc.tensor.matmul(psum[n % 8][:, :],
                                                  w[:, k, part * D + g * P:part * D + (g + 1) * P],
                                                  h[:, b, k, c * QC:(c + 1) * QC],
                                                  start=(k == 0), stop=(k == KC - 1))
                        mm.then_inc(s_ps, 1)
                        n += 1
            for tile in range(NT):
                b, q = divmod(tile, QB)
                pe.wait_ge(s_ev, n - 7)
                for k in range(KC):
                    mm = nc.tensor.matmul(psum[n % 8][:, :], h[:, b, k, q * P:(q + 1) * P], w[:, k, 2 * D:3 * D],
                                          start=(k == 0), stop=(k == KC - 1))
                mm.then_inc(s_ps, 1)
                n += 1

        @block.vector
        def _(dve):
            scale = float(HD) ** -0.5
            dve.wait_ge(s_b, 16)
            nc.vector.tensor_copy(t.vb[:, :], bias[:, 2 * KC:3 * KC]).then_inc(s_chain, 1)
            n = 0
            for i in range(B * KC):
                g = i % KC
                for c in range(NH):
                    for part, dst in enumerate((q_all, k_all)):
                        dve.wait_ge(s_ps, n + 1)
                        nc.vector.tensor_scalar(dst[:, i, c * QC:(c + 1) * QC], psum[n % 8][:, :],
                                                bias[:, part * KC + g:part * KC + g + 1],
                                                scale if part == 0 else 1.0, ALU.add, ALU.mult).then_inc(s_ev, 1)
                        n += 1
            for tile in range(NT):
                b, q = divmod(tile, QB)
                dve.wait_ge(s_ps, n + 1)
                nc.vector.tensor_copy(v_all[:, b * KC:(b + 1) * KC, q, :],
                                      psum[n % 8][:, :].rearrange("p (g c) -> p g c", g=KC)).then_inc(s_ev, 1)
                n += 1


HP = 2
STEPS = [(c, tb) for c in range(NH) for tb in range(4 * c + 4)]
NSTEP = len(STEPS)
S1_UNITS = [[(q, 0, a) for q in range(4) for a in range(HP)],
            [(q, c, a) for q in range(4, QB) for c in range(NH) for a in range(HP)]]
N_S1 = len(S1_UNITS[0]) + len(S1_UNITS[1])
N_S2 = NSTEP * HP
DIAG = [tb >= 4 * c for c, tb in STEPS]
S1_FROM = NSTEP - 8
PTS = 3


def attention(nc, ctx, t, sem, psum, q_all, k_all, v_all, o_all, stack_at, name):
    TAIL = 128
    qs = [[t.at(f"{name}_qs{p}{a}", [P, S], FR, stack_at + 16 * p + 8 * a) for a in range(HP)] for p in range(2)]
    ks = [[t.at(f"{name}_ks{p}{a}", [P, S], FR, stack_at + 16 * p + 8 * a + 4) for a in range(HP)] for p in range(2)]
    qh, ql, kh, kl = (t.at(f"{name}_{n}", [P, S], FR, TAIL + 4 * i) for i, n in enumerate(("qh", "ql", "kh", "kl")))
    ve = [t.at(f"{name}_ve{p}", [P, QB, HP, 2 * HD], F32, TAIL + 16 + 4 * p) for p in range(2)]
    pt = [t.at(f"{name}_pt{p}", [P, HP, QC], F32, TAIL + 24 + 4 * p) for p in range(PTS)]
    nm = [t.at(f"{name}_nm{p}", [P, 4, 4, HD], F32, TAIL + 36 + 2 * p) for p in range(2)]
    raw = t.at(f"{name}_raw", [P, 2, N_S1], F32, TAIL + 40)
    neg = t.at(f"{name}_negmax", [P, 2, 4, HP], F32, TAIL + 41)
    rden = t.at(f"{name}_rden", [P, QC], F32, TAIL + 42)
    PS1, PS2, POD, PMT = psum[0:2], psum[2:5], psum[5:7], psum[7]
    s_st = [sem(f"{name}_stack{p}") for p in range(2)]
    (s_seen, s_split, s_ve, s_init, s_s1, s_max, s_nm, s_mt, s_row, s_s2, s_exp, s_msk, s_pv, s_norm, s_nch,
     s_rch) = (sem(f"{name}_{n}") for n in (
         "seen", "split", "ve", "init", "s1", "max", "nm", "mt", "row", "s2", "exp", "msk", "pv", "norm", "nch", "rch"))
    NI = B * KC
    N_MSK = sum(DIAG)
    DMAS = 6 * HP

    def item_base(i, p, per):
        return i * (2 * per) + p * per

    with nc.Block() as block:
        @block.sync
        def _(sp):
            def stack(i, p):
                sp.wait_ge(s_split, i * 4 + 4)
                for a in range(HP):
                    src = slice(64 * p + HD * a, 64 * p + HD * a + HD)
                    for r, (x, y) in enumerate(((qh, kh), (qh, kl), (ql, kh))):
                        sp.dma_start(qs[p][a][HD * r:HD * r + HD, :].bitcast(F32), x[src, :].bitcast(F32)).then_inc(s_st[p], 16)
                        sp.dma_start(ks[p][a][HD * r:HD * r + HD, :].bitcast(F32), y[src, :].bitcast(F32)).then_inc(s_st[p], 16)

            stack(0, 0)
            stack(0, 1)
            with nc.sync.Fori(1, NI) as i:
                for p in range(2):
                    sp.wait_ge(s_s2, item_base(i, p, N_S2) - N_S2)
                    stack(i, p)

        @block.gpsimd
        def _(pool):
            def held():
                nc.gpsimd.sem_inc(s_seen, 1)

            def split(i):
                held()
                for x, hi, lo in ((q_all, qh, ql), (k_all, kh, kl)):
                    nc.gpsimd.tensor_copy(hi[:, :], x[:, i, :]).then_inc(s_split, 1)
                pool.wait_ge(s_split, i * 4 + 2)
                held()
                for x, hi, lo in ((q_all, qh, ql), (k_all, kh, kl)):
                    nc.gpsimd.tensor_tensor(lo[:, :], x[:, i, :], hi[:, :].bitcast(F32),
                                            ALU.subtract).then_inc(s_split, 1)

            def values(i, p):
                held()
                for a in range(HP):
                    at = 64 * p + HD * a
                    ins = nc.gpsimd.tensor_copy(ve[p][:, :, a, 0:HD], v_all[:, i, :, at:at + HD])
                ins.then_inc(s_ve, 1)

            def mask(i, p, s):
                c, tb = STEPS[s]
                at = tb * P - c * QC
                m = sum(DIAG[:s])
                pool.wait_ge(s_exp, item_base(i, p, N_S2) + HP * s + HP)
                held()
                nc.gpsimd.affine_select(out=pt[s % PTS][:, :, at:at + P], in_=pt[s % PTS][:, :, at:at + P],
                                        compare_op=ALU.is_ge, fill=0.0, base=0,
                                        pattern=[[0, HP], [1, P]], channel_multiplier=-1).then_inc(s_msk, 1)

            for p in range(2):
                nc.gpsimd.memset(ve[p][:, :, :, HD:2 * HD], 1.0).then_inc(s_init, 1)
                nc.gpsimd.memset(nm[p][:, :, :, :], 0.0).then_inc(s_init, 1)
            split(0)
            values(0, 0)

            def body(i, last):
                for p in range(2):
                    for s in range(NSTEP):
                        if s == 4:
                            if not (last and p == 1):
                                if p == 0:
                                    if not isinstance(i, int) or i > 0:
                                        pool.wait_ge(s_pv, item_base(i, 0, NSTEP))
                                    values(i, 1)
                                else:
                                    pool.wait_ge(s_pv, item_base(i, 1, NSTEP))
                                    values(i + 1, 0)
                            if p == 0 and not last:
                                for q in range(2):
                                    pool.wait_ge(s_st[q], i * (16 * DMAS) + 16 * DMAS)
                                split(i + 1)
                        if DIAG[s]:
                            mask(i, p, s)

            body(0, False)
            with nc.gpsimd.Fori(1, NI - 1) as i:
                body(i, False)
            body(NI - 1, True)

        @block.tensor
        def _(pe):
            def score1(i, p, u0, u1):
                units = S1_UNITS[0] + S1_UNITS[1]
                for u in range(u0, u1):
                    q, c, a = units[u]
                    n = min(QC, (q + 1) * P - c * QC)
                    diag = c == q // 4
                    pe.wait_ge(s_max, item_base(i, p, N_S1) + u - 1)
                    mm = nc.tensor.matmul(PS1[u % 2][:, 0:n], qs[p][a][0:3 * HD, q * P:(q + 1) * P],
                                          ks[p][a][0:3 * HD, c * QC:c * QC + n], start=True, stop=not diag)
                    if diag:
                        mm = nc.tensor.matmul(PS1[u % 2][:, n - P:n], t.ident_bf[:, :], t.neg_bf[:, :],
                                              start=False, stop=True)
                    mm.then_inc(s_s1, 1)

            def turn(i, p, hf):
                pe.wait_ge(s_nm, item_base(i, p, 2) + hf + 1)
                if hf or not isinstance(i, int) or i or p:
                    pe.wait_ge(s_row, item_base(i, p, 2) + hf)
                for q in range(4):
                    mm = nc.tensor.transpose(PMT[:, q * P:(q + 1) * P],
                                             nm[hf][:, q, :, :].rearrange("p a c -> p (a c)"), t.ident)
                mm.then_inc(s_mt, 1)

            def pv(i, p, s):
                c, tb = STEPS[s]
                at = max(0, tb * P - c * QC)
                if tb == 0:
                    if c == 0:
                        pe.wait_ge(s_ve, item_base(i, p, 1) + 1)
                    if not (isinstance(i, int) and i == 0 and p == 0):
                        pe.wait_ge(s_norm, item_base(i, p, 2) + c - 1)
                if DIAG[s]:
                    pe.wait_ge(s_msk, item_base(i, p, N_MSK) + sum(DIAG[:s + 1]))
                else:
                    pe.wait_ge(s_exp, item_base(i, p, N_S2) + HP * s + HP)
                for a in range(HP):
                    mm = nc.tensor.matmul(POD[c][64 * a:64 * a + 64, at:QC], ve[p][:, tb, a, :],
                                          pt[s % PTS][:, a, at:QC], start=(tb == 0), stop=(tb == 4 * c + 3))
                mm.then_inc(s_pv, 1)

            def item(i, p, nxt):
                for s, (c, tb) in enumerate(STEPS):
                    at = max(0, tb * P - c * QC)
                    if tb == 0:
                        pe.wait_ge(s_row, item_base(i, p, 2) + c + 1)
                    for a in range(HP):
                        u = HP * s + a
                        if u >= 3 or not (isinstance(i, int) and i == 0 and p == 0):
                            pe.wait_ge(s_exp, item_base(i, p, N_S2) + u - 2)
                        nc.tensor.matmul(PS2[u % 3][:, at:QC], ks[p][a][:, tb * P:(tb + 1) * P],
                                         qs[p][a][:, c * QC + at:(c + 1) * QC], start=True,
                                         stop=True).then_inc(s_s2, 1)
                    if s == 2:
                        turn(i, p, 1)
                    if nxt is not None and s >= S1_FROM:
                        if s == S1_FROM:
                            pe.wait_ge(s_st[nxt[1]], nxt[0] * (16 * DMAS) + 16 * DMAS)
                        k = (s - S1_FROM) * N_S1 // 8
                        score1(*nxt, k, k + N_S1 // 8)
                        if s == S1_FROM + 5:
                            turn(*nxt, 0)
                    if s >= 1:
                        pv(i, p, s - 1)
                pv(i, p, NSTEP - 1)

            pe.wait_ge(s_init, 8)
            pe.wait_ge(s_st[0], 16 * DMAS)
            for u, (q, c, a) in enumerate((S1_UNITS[0] + S1_UNITS[1])[:2]):
                nc.tensor.matmul(PS1[u][:, 0:P], qs[0][a][0:3 * HD, 0:P], ks[0][a][0:3 * HD, 0:P],
                                 start=True, stop=False)
                nc.tensor.matmul(PS1[u][:, 0:P], t.ident_bf[:, :], t.neg_bf[:, :], start=False,
                                 stop=True).then_inc(s_s1, 1)
            score1(0, 0, 2, N_S1)
            turn(0, 0, 0)

            def body(i, last):
                item(i, 0, (i, 1))
                item(i, 1, None if last else (i + 1, 0))

            body(0, False)
            with nc.tensor.Fori(1, NI - 1) as i:
                body(i, False)
            body(NI - 1, True)

        @block.scalar
        def _(act):
            def rows(i, p, hf):
                act.wait_ge(s_mt, item_base(i, p, 2) + hf + 1)
                for a in range(HP):
                    ins = nc.scalar.activation(qs[p][a][3 * HD:P, hf * QC:(hf + 1) * QC],
                                               PMT[64 + HD * a:64 + HD * a + HD, :], ACT.Copy)
                ins.then_inc(s_row, 1)

            def item(i, p, nxt):
                for s, (c, tb) in enumerate(STEPS):
                    at = max(0, tb * P - c * QC)
                    if s >= PTS or not (isinstance(i, int) and i == 0 and p == 0):
                        act.wait_ge(s_pv, item_base(i, p, NSTEP) + s - PTS + 1)
                    for a in range(HP):
                        u = HP * s + a
                        act.wait_ge(s_s2, item_base(i, p, N_S2) + u + 1)
                        nc.scalar.activation(pt[s % PTS][:, a, at:QC], PS2[u % 3][:, at:QC],
                                             ACT.Exp).then_inc(s_exp, 1)
                    if s == 2:
                        rows(i, p, 1)
                    if nxt is not None and s == S1_FROM + 5:
                        rows(*nxt, 0)

            rows(0, 0, 0)

            def body(i, last):
                item(i, 0, (i, 1))
                item(i, 1, None if last else (i + 1, 0))

            body(0, False)
            with nc.scalar.Fori(1, NI - 1) as i:
                body(i, False)
            body(NI - 1, True)

        @block.vector
        def _(dve):
            def maxima(i, p, u0, u1):
                units = S1_UNITS[0] + S1_UNITS[1]
                for u in range(u0, u1):
                    q, c, a = units[u]
                    n = min(QC, (q + 1) * P - c * QC)
                    dve.wait_ge(s_s1, item_base(i, p, N_S1) + u + 1)
                    nc.vector.tensor_reduce(raw[:, p, u:u + 1], PS1[u % 2][:, 0:n], AX.X, ALU.max,
                                            negate=True).then_inc(s_max, 1)
                    for hf, end in enumerate((8, 24)):
                        if u + 1 == end:
                            parts(i, p, hf)

            def parts(i, p, hf):
                dve.wait_ge(s_max, item_base(i, p, N_S1) + (8, 24)[hf])
                if hf == 0:
                    m = raw[:, p, 0:8].rearrange("p (q a) -> p q a", a=HP)
                else:
                    m = neg[:, p, :, :]
                    both = raw[:, p, 8:24].rearrange("p (q c a) -> p q c a", c=NH, a=HP)
                    nc.vector.tensor_tensor(m, both[:, :, 0, :], both[:, :, 1, :], ALU.min).then_inc(s_nch, 1)
                    dve.wait_ge(s_nch, item_base(i, p, 3) + 2)
                if not (isinstance(i, int) and i == 0 and p == 0):
                    dve.wait_ge(s_mt, item_base(i, p, 2) + hf - 1)
                hi, lo = nm[hf][:, :, 2:4, 0], nm[hf][:, :, 2:4, 1]
                nc.vector.tensor_copy(hi.bitcast(FR), m).then_inc(s_nch, 1)
                dve.wait_ge(s_nch, item_base(i, p, 3) + (1, 3)[hf])
                nc.vector.tensor_tensor(lo, m, hi, ALU.subtract).then_inc(s_nm, 1)

            def norm(i, p, c):
                dve.wait_ge(s_pv, item_base(i, p, NSTEP) + (4, 12)[c])
                if c or not (isinstance(i, int) and i == 0 and p == 0):
                    dve.wait_ge(s_norm, item_base(i, p, 2) + c)
                nc.vector.reciprocal(rden[:, :], POD[c][:, :]).then_inc(s_rch, 1)
                dve.wait_ge(s_rch, item_base(i, p, 2) + c + 1)
                for a in range(HP):
                    at = 64 * p + HD * a
                    ins = nc.vector.tensor_tensor(o_all[at:at + HD, i, c * QC:(c + 1) * QC],
                                                  POD[c][64 * a:64 * a + HD, :], rden[64 * a + HD:64 * a + 64, :],
                                                  ALU.mult)
                ins.then_inc(s_norm, 1)

            def item(i, p, nxt):
                for s in range(NSTEP):
                    if s == 5:
                        norm(i, p, 0)
                    if nxt is not None and s >= S1_FROM:
                        k = (s - S1_FROM) * N_S1 // 8
                        maxima(*nxt, k, k + N_S1 // 8)
                norm(i, p, 1)

            for p in range(2):
                for a in range(HP):
                    nc.vector.memset(ks[p][a][3 * HD:P, :].bitcast(F32), 1.0).then_inc(s_init, 1)
            dve.wait_ge(s_init, 8)
            maxima(0, 0, 0, N_S1)

            def body(i, last):
                item(i, 0, (i, 1))
                item(i, 1, None if last else (i + 1, 0))

            body(0, False)
            with nc.vector.Fori(1, NI - 1) as i:
                body(i, False)
            body(NI - 1, True)


def output_projection(nc, ctx, t, sem, psum, o_all, x, x_src, layer, d_Wo, d_bo, name):
    wo = t.at(f"{name}_wo", [P, KC, D], F32, 160)
    bo = t.at(f"{name}_bo", [P, D], F32, 168)
    bg = t.at(f"{name}_bg", [P, B, D], F32, 170)
    vbb = t.at(f"{name}_vbb", [P, KC, P], F32, 174)
    tmp = [t.at(f"{name}_tmp{i}", [P, D], F32, 176 + 2 * i) for i in range(2)]
    nat = t.at(f"{name}_nat", [P, KC, D], F32, 128) if layer == 0 else None
    s_w, s_x, s_tr, s_ev, s_vbb, s_bp, s_bg, s_xb, s_ps, s_tmp, s_add, s_chain = (
        sem(f"{name}_{n}") for n in ("w", "x", "tr", "ev", "vbb", "bp", "bg", "xb", "ps", "tmp", "add", "chain"))
    with nc.Block() as block:
        @block.sync
        def _(sp):
            sp.dma_start((nat if layer == 0 else wo)[:, :, :],
                         d_Wo.rearrange("(k p) n -> p k n", p=P)).then_inc(s_w, 16)
            sp.dma_start(bo[:, :], d_bo.rearrange("(o n) -> o n", o=1).broadcast_to([P, D])).then_inc(s_w, 16)
            for g in range(NT // 4):
                sp.dma_start(x[:, 4 * g:4 * g + 4, :], x_src[:, 4 * g:4 * g + 4, :]).then_inc(s_x, 16)

        @block.tensor
        def _(pe):
            pe.wait_ge(s_w, 32)
            if layer == 0:
                for k in range(KC):
                    for j in range(KC):
                        mm = nc.tensor.transpose(psum[k][:, j * P:(j + 1) * P], nat[:, j, k * P:(k + 1) * P],
                                                 t.ident)
                    mm.then_inc(s_tr, 1)
                pe.wait_ge(s_ev, KC)
            pe.wait_ge(s_vbb, 1)
            for k in range(KC):
                mm = nc.tensor.matmul(psum[4][:, :], vbb[:, k, :], wo[:, k, :], start=(k == 0), stop=(k == KC - 1))
            mm.then_inc(s_bp, 1)
            for n in range(NT):
                b, q = divmod(n, QB)
                if n >= 4:
                    pe.wait_ge(s_tmp, n - 3)
                for k in range(KC):
                    mm = nc.tensor.matmul(psum[n % 4][:, :], o_all[:, b * KC + k, q * P:(q + 1) * P], wo[:, k, :],
                                          start=(k == 0), stop=(k == KC - 1))
                mm.then_inc(s_ps, 1)

        @block.scalar
        def _(act):
            if layer == 0:
                for k in range(KC):
                    act.wait_ge(s_tr, k + 1)
                    nc.scalar.activation(wo[:, k, :], psum[k][:, :], ACT.Copy).then_inc(s_ev, 1)

        @block.vector
        def _(dve):
            nc.vector.tensor_copy(vbb[:, :, :], t.vb[:, :].unsqueeze(2).broadcast_to([P, KC, P])).then_inc(s_vbb, 1)
            dve.wait_ge(s_bp, 1)
            dve.wait_ge(s_w, 32)
            nc.vector.tensor_tensor(tmp[0][:, :], psum[4][:, :], bo[:, :], ALU.add).then_inc(s_chain, 1)
            dve.wait_ge(s_chain, 1)
            for b in range(B):
                ins = nc.vector.tensor_tensor(bg[:, b, :], tmp[0][:, :], t.gate[:, layer, 0, b, :], ALU.mult)
            ins.then_inc(s_bg, 1)
            dve.wait_ge(s_bg, 1)
            for n in range(NT):
                dve.wait_ge(s_ps, n + 1)
                if n >= 2:
                    dve.wait_ge(s_add, n - 1)
                nc.vector.tensor_tensor(tmp[n % 2][:, :], psum[n % 4][:, :], t.gate[:, layer, 0, n // QB, :],
                                        ALU.mult).then_inc(s_tmp, 1)

        @block.gpsimd
        def _(pool):
            pool.wait_ge(s_bg, 1)
            pool.wait_ge(s_x, 16 * (NT // 4))
            for n in range(NT):
                ins = nc.gpsimd.tensor_tensor(x[:, n, :], x[:, n, :], bg[:, n // QB, :], ALU.add)
            ins.then_inc(s_xb, 1)
            pool.wait_ge(s_xb, 1)
            for n in range(NT):
                pool.wait_ge(s_tmp, n + 1)
                nc.gpsimd.tensor_tensor(x[:, n, :], x[:, n, :], tmp[n % 2][:, :], ALU.add).then_inc(s_add, 1)


def route(nc, ctx, t, sem, psum, h, d_wgate, d_gates):
    wg = t.at("rt_wg", [P, KC, E], F32, 160)
    lg = t.at("rt_logits", [P, NT, E], F32, 161)
    cmp_ = t.at("rt_cmp", [P, NT, E], F32, 162)
    rank = t.at("rt_rank", [P, NT, E], F32, 163)
    second = t.at("rt_second", [P, NT, E], F32, 164)
    m1, m2, ex, w1 = (t.at(f"rt_{n}", [P, NT], F32, 165 + 0.25 * i) for i, n in enumerate(("m1", "m2", "ex", "w1")))
    gt = t.at("rt_gt", [P, P], F32, 166)
    s_w, s_lg, s_d, s_e, s_g, s_t, s_gt, s_out, s_chain = (
        sem(f"rt_{n}") for n in ("w", "lg", "d", "e", "g", "t", "gt", "out", "chain"))
    with nc.Block() as block:
        @block.sync
        def _(sp):
            sp.dma_start(wg[:, :, :], d_wgate.rearrange("(k p) e -> p k e", p=P)).then_inc(s_w, 16)
            sp.wait_ge(s_gt, 1)
            sp.dma_start(d_gates.rearrange("n e q -> (n e) q"), gt[:, :]).then_inc(s_out, 16)
            sp.wait_ge(s_out, 16)

        @block.tensor
        def _(pe):
            pe.wait_ge(s_w, 16)
            for n in range(NT):
                for k in range(KC):
                    mm = nc.tensor.matmul(psum[0][:, n * E:(n + 1) * E],
                                          h[:, n // 4, k, (n % 4) * P:(n % 4 + 1) * P], wg[:, k, :],
                                          start=(k == 0), stop=(k == KC - 1))
            mm.then_inc(s_lg, 1)
            pe.wait_ge(s_g, 1)
            nc.tensor.transpose(psum[1][:, 0:P], rank[:, :, :].rearrange("p n e -> p (n e)"), t.ident).then_inc(s_t, 1)

        @block.scalar
        def _(act):
            act.wait_ge(s_d, 1)
            nc.scalar.activation(ex[:, :], m2[:, :], ACT.Exp).then_inc(s_e, 1)

        @block.vector
        def _(dve):
            link = chained(dve, s_chain)
            tt, v = nc.vector.tensor_tensor, nc.vector
            dve.wait_ge(s_lg, 1)
            link(v.tensor_copy(lg[:, :, :].rearrange("p n e -> p (n e)"), psum[0][:, 0:NT * E]))
            link(v.memset(rank[:, :, :], 0.0))
            for e in range(E):
                one = lg[:, :, e:e + 1]
                ins = tt(cmp_[:, :, 0:e + 1], one.broadcast_to([P, NT, e + 1]), lg[:, :, 0:e + 1], ALU.is_gt)
                if e + 1 < E:
                    ins = tt(cmp_[:, :, e + 1:E], one.broadcast_to([P, NT, E - e - 1]), lg[:, :, e + 1:E], ALU.is_ge)
                link(ins)
                link(tt(rank[:, :, :], rank[:, :, :], cmp_[:, :, :], ALU.add))
            link(v.tensor_scalar(second[:, :, :], rank[:, :, :], 1.0, None, ALU.is_equal))
            link(v.tensor_scalar(rank[:, :, :], rank[:, :, :], 0.0, None, ALU.is_equal))
            link(v.tensor_reduce(m1[:, :], lg[:, :, :], AX.X, ALU.max))
            link(tt(cmp_[:, :, :], lg[:, :, :], second[:, :, :], ALU.mult))
            link(v.tensor_reduce(m2[:, :], cmp_[:, :, :], AX.X, ALU.add))
            tt(m2[:, :], m2[:, :], m1[:, :], ALU.subtract).then_inc(s_d, 1)
            dve.wait_ge(s_e, 1)
            link(v.tensor_scalar(w1[:, :], ex[:, :], 1.0, None, ALU.add))
            link(v.reciprocal(w1[:, :], w1[:, :]))
            link(tt(ex[:, :], ex[:, :], w1[:, :], ALU.mult))
            link(tt(rank[:, :, :], rank[:, :, :], w1[:, :].unsqueeze(2).broadcast_to([P, NT, E]), ALU.mult))
            link(tt(second[:, :, :], second[:, :, :], ex[:, :].unsqueeze(2).broadcast_to([P, NT, E]), ALU.mult))
            tt(rank[:, :, :], rank[:, :, :], second[:, :, :], ALU.add).then_inc(s_g, 1)
            dve.wait_ge(s_t, 1)
            v.tensor_copy(gt[:, :], psum[1][:, 0:P]).then_inc(s_gt, 1)


def feed_forward(nc, ctx, t, sem, psum, h, x, w_up0, w_up1, w_down, layer, name, loads=(), d_gates=None):
    act_t = [t.at(f"{name}_act{i}", [P, QC], F32, 160 + 2 * i) for i in range(2)]
    hid = [t.at(f"{name}_hid{i}", [P, QC], F32, 164 + 2 * i) for i in range(2)]
    gb = [t.at(f"{name}_gb{i}", [P, QC], F32, 168 + 2 * i) for i in range(4)] if d_gates is not None else None
    tmp = t.at(f"{name}_tmp", [P, 2, D], F32, 176)
    s_w, s_h, s_act, s_mul, s_hid, s_down, s_tmp, s_xa = (
        sem(f"{name}_{n}") for n in ("w", "h", "act", "mul", "hid", "down", "tmp", "xa"))
    s_g = [sem(f"{name}_g{i}") for i in range(4)]
    UP0, UP1, ACC = psum[0:2], psum[2:4], psum[4:8]
    gated = d_gates is not None
    SUB = QC // P
    CR = 8

    with nc.Block() as block:
        @block.sync
        def _(sp):
            for dst, src in loads:
                sp.dma_start(dst, src).then_inc(s_w, 16)
            if gated:
                with nc.sync.Fori(0, B) as b:
                    for half in range(NH):
                        T = 2 * b + half
                        for e in range(E):
                            sp.wait_ge(s_hid, T * FC + (2 * e - 8 + CR + 2))
                            sp.dma_start(gb[e % 4][:, :].rearrange("p (n q) -> p n q", n=SUB),
                                         d_gates.rearrange("(t n) e q -> t e n q", n=SUB)[T, e:e + 1, :, :]
                                         .broadcast_to([P, SUB, P])).then_inc(s_g[e % 4], 16)

        @block.tensor
        def _(pe):
            def down(T, c):
                pe.wait_ge(s_hid, T * FC + (c + 1 + CR))
                if c == 0:
                    pe.wait_ge(s_tmp, T * SUB + CR)
                for sub in range(SUB):
                    mm = nc.tensor.matmul(ACC[sub][:, :], hid[c % 2][:, sub * P:(sub + 1) * P], w_down[:, c, :],
                                          start=(c == 0), stop=(c == FC - 1))
                mm.then_inc(s_down, 1)

            if loads:
                pe.wait_ge(s_w, 16 * len(loads))
            nc.tensor.sem_inc(s_down, CR)
            with nc.tensor.Fori(0, B) as b:
                for half in range(NH):
                    T = 2 * b + half
                    for c in range(FC):
                        pe.wait_ge(s_mul, T * FC + (c - 1 + CR))
                        for up, w in ((UP0, w_up0), (UP1, w_up1)):
                            for k in range(KC):
                                mm = nc.tensor.matmul(up[c % 2][:, :], w[:, k, c * P:(c + 1) * P], h[:, T, k, :],
                                                      start=(k == 0), stop=(k == KC - 1))
                        mm.then_inc(s_h, 1)
                        if c:
                            down(T, c - 1)
                    down(T, FC - 1)

        @block.scalar
        def _(act):
            with nc.scalar.Fori(0, B) as b:
                for half in range(NH):
                    T = 2 * b + half
                    for c in range(FC):
                        act.wait_ge(s_h, T * FC + (c + 1))
                        act.wait_ge(s_hid if gated else s_mul, T * FC + (c - 1 + CR))
                        nc.scalar.activation(act_t[c % 2][:, :], UP0[c % 2][:, :], ACT.Silu).then_inc(s_act, 1)

        @block.vector
        def _(dve):
            nc.vector.sem_inc(s_mul, CR)
            nc.vector.sem_inc(s_tmp, CR)
            nc.vector.sem_inc(s_xa, CR)
            if not gated:
                nc.vector.sem_inc(s_hid, CR)
            with nc.vector.Fori(0, B) as b:
                for half in range(NH):
                    T = 2 * b + half
                    for c in range(FC):
                        dve.wait_ge(s_act, T * FC + (c + 1))
                        if gated:
                            nc.vector.tensor_tensor(act_t[c % 2][:, :], act_t[c % 2][:, :], UP1[c % 2][:, :],
                                                    ALU.mult).then_inc(s_mul, 1)
                        else:
                            dve.wait_ge(s_down, T * FC + (c - 1 + CR))
                            nc.vector.tensor_tensor(hid[c % 2][:, :], act_t[c % 2][:, :], UP1[c % 2][:, :],
                                                    ALU.mult).then_inc(s_hid, 1)
                            dve.wait_ge(s_hid, T * FC + (c + 1 + CR))
                            nc.vector.sem_inc(s_mul, 1)
                    dve.wait_ge(s_down, T * FC + (FC + CR))
                    for sub in range(SUB):
                        dve.wait_ge(s_xa, T * SUB + (sub - 1 + CR))
                        nc.vector.tensor_tensor(tmp[:, sub % 2, :], ACC[sub][:, :], t.gate[:, layer, 1, b, :],
                                                ALU.mult).then_inc(s_tmp, 1)
                        dve.wait_ge(s_tmp, T * SUB + (sub + 1 + CR))
                        nc.vector.tensor_tensor(x[:, T * SUB + sub, :], x[:, T * SUB + sub, :], tmp[:, sub % 2, :],
                                                ALU.add).then_inc(s_xa, 1)

        if gated:
            @block.gpsimd
            def _(pool):
                nc.gpsimd.sem_inc(s_hid, CR)
                with nc.gpsimd.Fori(0, B) as b:
                    for half in range(NH):
                        T = 2 * b + half
                        for c in range(FC):
                            e = c // 2
                            pool.wait_ge(s_mul, T * FC + (c + 1 + CR))
                            pool.wait_ge(s_g[e % 4], T * 32 + 16 * (e // 4 + 1))
                            pool.wait_ge(s_down, T * FC + (c - 1 + CR))
                            nc.gpsimd.tensor_tensor(hid[c % 2][:, :], act_t[c % 2][:, :], gb[e % 4][:, :],
                                                    ALU.mult).then_inc(s_hid, 1)


def ffn_weights(nc, ctx, t, sem, psum, w1, w3, wd, spare):
    ring = [t.at(f"fw_ring{i}", [P, 4, D], F32, 160 + 8 * i) for i in range(2)]
    s_ld = [sem(f"fw_ld{i}") for i in range(2)]
    s_tr, s_ev, s_had, s_hev, s_bd, s_bp = (sem(f"fw_{n}") for n in ("tr", "ev", "had", "hev", "bd", "bp"))
    NLD = 12
    with nc.Block() as block:
        @block.sync
        def _(sp):
            for n in range(NLD):
                which, j = divmod(n, 4)
                if n >= 2:
                    sp.wait_ge(s_tr, 4 * (n - 1))
                if which < 2:
                    src = (t.d_W1, t.d_W3)[which].rearrange("(c p) d -> p c d", p=P)[:, 4 * j:4 * j + 4, :]
                else:
                    src = t.d_W2[j * P:(j + 1) * P, :].rearrange("p (c d) -> p c d", c=4)
                sp.dma_start(ring[n % 2][:, :, :], src).then_inc(s_ld[n % 2], 16)

        @block.tensor
        def _(pe):
            for n in range(NLD):
                which, j = divmod(n, 4)
                pe.wait_ge(s_ld[n % 2], 16 * (n // 2 + 1))
                for k in range(KC):
                    m = 4 * n + k
                    if m >= 8:
                        pe.wait_ge(s_ev, m - 7)
                    for i in range(4):
                        src = ring[n % 2][:, i, k * P:(k + 1) * P] if which < 2 else \
                            ring[n % 2][:, k, i * P:(i + 1) * P]
                        mm = nc.tensor.transpose(psum[m % 8][:, i * P:(i + 1) * P], src, t.ident)
                    mm.then_inc(s_tr, 1)
            for c in range(FC):
                pe.wait_ge(s_ev, 48 if c == 0 else 48)
                if c >= 8:
                    pe.wait_ge(s_hev, c - 7)
                nc.tensor.matmul(psum[c % 8][:, :], t.had, wd[:, c, :], start=True, stop=True).then_inc(s_had, 1)

        @block.scalar
        def _(act):
            for m in range(48):
                n, k = divmod(m, 4)
                which, j = divmod(n, 4)
                act.wait_ge(s_tr, m + 1)
                if which < 2:
                    dst = (w1, w3)[which][:, k, j * QC:(j + 1) * QC]
                    src = psum[m % 8][:, :]
                else:
                    dst = wd[:, 4 * k:4 * k + 4, j * P:(j + 1) * P]
                    src = psum[m % 8][:, :].rearrange("p (c d) -> p c d", c=4)
                nc.scalar.activation(dst, src, ACT.Copy).then_inc(s_ev, 1)
            for c in range(FC):
                act.wait_ge(s_had, c + 1)
                nc.scalar.activation(wd[:, c, :], psum[c % 8][:, :], ACT.Copy).then_inc(s_hev, 1)

        def butterfly(eng, mine, other, which):
            cols = slice(0, 320) if which == 0 else slice(320, D)
            eng.wait_ge(s_hev, FC)
            for st in range(4):
                src, dst = (wd, spare) if st % 2 == 0 else (spare, wd)
                d = 1 << st
                if st:
                    eng.wait_ge(mine, 2 * d_count[which][st - 1])
                v = lambda z: z[:, :, cols].rearrange("p (a two b) n -> p a two b n", two=2, b=d)
                for a in range(FC // (2 * d)):
                    lo, hi = src[:, 2 * d * a:2 * d * a + d, cols], src[:, 2 * d * a + d:2 * d * a + 2 * d, cols]
                    eng.tensor_tensor(dst[:, 2 * d * a:2 * d * a + d, cols], lo, hi, ALU.add).then_inc(mine, 1)
                    eng.tensor_tensor(dst[:, 2 * d * a + d:2 * d * a + 2 * d, cols], lo, hi,
                                      ALU.subtract).then_inc(mine, 1)

        d_count = [[sum(FC // (2 << s) for s in range(st + 1)) for st in range(4)]] * 2

        @block.vector
        def _(dve):
            butterfly(dve, s_bd, s_bp, 0)

        @block.gpsimd
        def _(pool):
            butterfly(pool, s_bp, s_bd, 1)


def build(nc, d, d_const, d_out, stop=99):
    ctx = ExitStack()
    with ctx:
        t = Shared()

        def sb(name, shape, dt=F32):
            return ctx.enter_context(nc.sbuf_tensor(name, shape, dt))

        sems = ExitStack()

        used = []

        def sem(name):
            used.append(sems.enter_context(nc.semaphore(name)))
            return used[-1]

        psum = [ctx.enter_context(nc.psum_tensor(f"bank{i}", [P, QC], F32)) for i in range(8)]

        t.const = sb("const", [P, C_SEL])
        t.ident, t.blk = t.const[:, C_ID:C_ID + P], t.const[:, C_BLK:C_BLK + P]
        t.had, t.neg = t.const[:, C_HAD:C_HAD + P], t.const[:, C_NEG:C_NEG + P]
        t.blk4 = t.const[:, C_BLK:C_BLK + P:HD]
        t.ident_bf, t.neg_bf = sb("ident_bf", [P, P], BF16), sb("neg_bf", [P, P], BF16)
        t.avg = sb("avg", [P, P])
        t.mod = sb("mod", [P, 2, 4, KC * B])
        t.gate = sb("gate", [P, 2, 2, B, D])
        t.bd_m, t.bd_k, t.bd_v = (sb(n, [P, D]) for n in ("bd_m", "bd_k", "bd_v"))
        t.kb, t.vb = sb("kb", [P, KC]), sb("vb", [P, KC])
        t.eps = sb("eps", [P, 1])
        base = 43 * 1024

        def at(name, shape, dt, kib):
            return nc.alloc_sbuf_tensor_at(name, shape, dt, offset=base + int(kib * 1024))
        t.at = at

        t.d_const = d_const[:, 0:C_SEL]
        t.d_c = [d["L0_c"], d["L1_c"]]
        t.d_wmod = [d["L0_wmod"], d["L1_wmod"]]
        t.d_Wdkv, t.d_Wuk, t.d_Wuv = d["L0_attn_Wdkv"], d["L0_attn_Wuk"], d["L0_attn_Wuv"]
        t.d_Wq, t.d_Woh, t.d_lng, t.d_lnb = d["L0_attn_Wq"], d["L0_attn_Wo_h"], d["L0_attn_ln_g"], d["L0_attn_ln_b"]
        t.d_Wqkv, t.d_bqkv = d["L1_attn_Wqkv"], d["L1_attn_bqkv"]
        t.d_W1, t.d_W2, t.d_W3 = d["L1_ffn_W1"], d["L1_ffn_W2"], d["L1_ffn_W3"]
        d_x = d["L0_attn_x"].rearrange("b (n p) d -> p (b n) d", p=P)
        d_res = nc.dram_tensor("x_mid", [P, NT, D], F32, kind="Internal").ap()
        d_gates = nc.dram_tensor("gates", [NT, E, P], F32, kind="Internal").ap()
        d_y = d_out.rearrange("b (n p) d -> p (b n) d", p=P)

        def region(name, kib, shape):
            return at(name, shape, F32, kib)

        def finish(x):
            s = sem("stored")
            with nc.Block() as block:
                @block.sync
                def _(sp):
                    sp.dma_start(d_y, x[:, :, :]).then_inc(s, 16)
                    sp.wait_ge(s, 16)

        s_eps = sem("eps_set")
        with nc.Block() as block:
            @block.vector
            def _(dve):
                nc.vector.memset(t.eps[:, :], EPS).then_inc(s_eps, 1)
                dve.wait_ge(s_eps, 1)

        modulation(nc, ctx, t, sem, psum)
        latent_weights(nc, ctx, t, sem, psum)

        x = region("x_l0a", 0, [P, NT, D])
        h = region("h_l0a", 32, [P, B, KC, S])
        layer_norm(nc, ctx, t, sem, psum, x, h, 0, 0, "ln0a", load=d_x)
        k_all = region("k_l0", 64, [P, B * KC, S])
        v_all = region("v_l0", 96, [P, B * KC, QB, P])
        latent_keys_values(nc, ctx, t, sem, psum, h, k_all, v_all)
        q_all = h[:, :, :, :].rearrange("p b k s -> p (b k) s")
        if stop == 1:
            return finish(h_as_x(h, t, at))
        attention(nc, ctx, t, sem, psum, q_all, k_all, v_all, q_all, 0, "at0")
        x = region("x_l0b", 0, [P, NT, D])
        output_projection(nc, ctx, t, sem, psum, q_all, x, d_x, 0, d["L0_attn_Wo"], d["L0_attn_bo"], "op0")
        if stop == 2:
            return finish(x)
        h = region("h_l0b", 32, [P, NT // 4, KC, QC])
        layer_norm(nc, ctx, t, sem, psum, x, h, 0, 1, "ln0b")
        route(nc, ctx, t, sem, psum, h, d["L0_ffn_w_gate"], d_gates)
        w0, w1 = region("moe_w0", 64, [P, KC, F]), region("moe_w1", 96, [P, KC, F])
        wd = region("moe_wd", 128, [P, FC, D])
        loads = []
        for w, src in ((w0, d["L0_ffn_wi_0"]), (w1, d["L0_ffn_wi_1"])):
            for e in range(E):
                loads.append((w[:, :, e * M:(e + 1) * M], src[e, :, :].rearrange("(k p) m -> p k m", p=P)))
        for j in range(4):
            loads.append((wd[:, 4 * j:4 * j + 4, :],
                          d["L0_ffn_wo"].rearrange("e (m p) d -> p (e m) d", p=P)[:, 4 * j:4 * j + 4, :]))
        feed_forward(nc, ctx, t, sem, psum, h, x, w0, w1, wd, 0, "moe", loads=loads, d_gates=d_gates)
        if stop == 3:
            return finish(x)

        numbers = sorted(s.num for s in used)
        assert numbers == list(range(numbers[0], numbers[-1] + 1))
        with nc.Block() as block:
            @block.sync
            def _(sp):
                sp.sem_clear(range(numbers[0], numbers[-1] + 1))
        sems.close()
        h = region("h_l1a", 32, [P, B, KC, S])
        layer_norm(nc, ctx, t, sem, psum, x, h, 1, 0, "ln1a", save=d_res)
        q_all, k_all = region("q_l1", 0, [P, B * KC, S]), region("k_l1", 64, [P, B * KC, S])
        v_all = region("v_l1", 96, [P, B * KC, QB, P])
        project_qkv(nc, ctx, t, sem, psum, h, q_all, k_all, v_all)
        attention(nc, ctx, t, sem, psum, q_all[:, :, :], k_all, v_all, q_all[:, :, :], 32, "at1")
        w1, w3 = region("ffn_w1", 64, [P, KC, F]), region("ffn_w3", 96, [P, KC, F])
        wd, spare = region("ffn_wd", 128, [P, FC, D]), region("ffn_spare", 32, [P, FC, D])
        ffn_weights(nc, ctx, t, sem, psum, w1, w3, wd, spare)
        x = region("x_l1b", 32, [P, NT, D])
        output_projection(nc, ctx, t, sem, psum, q_all, x, d_res, 1, d["L1_attn_Wo"], d["L1_attn_bo"], "op1")
        if stop == 4:
            return finish(x)
        h = region("h_l1b", 0, [P, NT // 4, KC, QC])
        layer_norm(nc, ctx, t, sem, psum, x, h, 1, 1, "ln1b", tmp=160)
        feed_forward(nc, ctx, t, sem, psum, h, x, w1, w3, wd, 1, "ffn")
        finish(x)


_INS = ["L0_attn_x", "L0_attn_Wq", "L0_attn_Wdkv", "L0_attn_Wuk", "L0_attn_Wuv", "L0_attn_ln_g", "L0_attn_ln_b",
        "L0_attn_Wo_h", "L0_attn_Wo", "L0_attn_bo", "L0_ffn_w_gate", "L0_ffn_wi_0", "L0_ffn_wi_1", "L0_ffn_wo",
        "L0_c", "L0_wmod", "L1_attn_Wqkv", "L1_attn_bqkv", "L1_attn_Wo", "L1_attn_bo", "L1_ffn_W1", "L1_ffn_W2",
        "L1_ffn_W3", "L1_c", "L1_wmod"]


def kernel(**inputs):
    import numpy as _np
    import concourse.bacc as _bacc
    from concourse import mybir as _mybir
    from concourse.bass_utils import run_bass_kernel_spmd as _run

    nc = _bacc.Bacc("TRN2", target_bir_lowering=False, num_devices=1)
    arrays, aps = {}, {}
    for name in _INS:
        a = _np.ascontiguousarray(inputs[name])
        arrays[f"in_{name}"] = a
        aps[name] = nc.dram_tensor(f"in_{name}", a.shape, _mybir.dt.from_np(a.dtype), kind="ExternalInput").ap()
    table = constant_table()
    arrays["in_constants"] = table
    consts = nc.dram_tensor("in_constants", table.shape, F32, kind="ExternalInput").ap()
    out = nc.dram_tensor("out_x", (B, S, D), F32, kind="ExternalOutput").ap()
    build(nc, aps, consts, out)
    r = _run(nc, [arrays], core_ids=[0])
    return r.results[0]["out_x"]
```

```python
from contextlib import ExitStack

import concourse.bass as bass
import numpy as np
from concourse import mybir

P = 128
B, S, D = 2, 1024, 512
TOK = B * S
NT = TOK // P
KC = D // P
H, HD, LAT = 16, 32, 128
HG = P // HD
QB = S // P
QC = 512
NH = S // QC
E, M = 8, 256
F = 2048
FC = F // P
EPS = 1e-5
NEG = -1e30

ALU = mybir.AluOpType
ACT = mybir.ActivationFunctionType
AX = mybir.AxisListType
F32 = mybir.dt.float32
FR = mybir.dt.float32r
BF16 = mybir.dt.bfloat16


class Shared:
    pass


C_ID, C_BLK, C_HAD, C_NEG, C_NEGT, C_END = 0, P, 2 * P, 3 * P, 4 * P, 5 * P


def constant_table():
    t = np.zeros((P, C_END), np.float32)
    t[:, C_ID:C_ID + P] = np.eye(P)
    blk = np.arange(P) // HD
    t[:, C_BLK:C_BLK + P] = blk[:, None] == blk[None, :]
    had = np.ones((1, 1))
    while had.shape[0] < P:
        had = np.block([[had, had], [had, -had]])
    t[:, C_HAD:C_HAD + P] = had / np.sqrt(F)
    t[:, C_NEG:C_NEG + P] = np.where(np.arange(P)[None, :] > np.arange(P)[:, None], NEG, 0.0)
    t[:, C_NEGT:C_NEGT + P] = t[:, C_NEG:C_NEG + P].T
    return t


def chained(eng, sem):
    count = [0]

    def link(ins):
        count[0] += 1
        ins.then_inc(sem, 1)
        eng.wait_ge(sem, count[0])
    return link


def spread(ap, shape):
    return ap.broadcast_to(shape)


def modulation(nc, ctx, t, sem, psum):
    cT = t.at("cT", [P, 2, KC, B], F32, 64)
    sT = t.at("sT", [P, 2 * KC * B], F32, 65)
    sB = t.at("sB", [P, 2 * KC * B, P], F32, 66)
    ring = [t.at(f"wmod_ring{i}", [P, KC, D], F32, 76 + 8 * i) for i in range(4)]
    masks = t.at("masks", [P, 2 * P], F32, 108)
    t1 = t.at("gate_abs", [P, D], F32, 110)
    t2 = t.at("gate_sign", [P, D], F32, 112)
    s_const, s_c, s_w = sem("mod_const"), sem("mod_c"), [sem(f"mod_w{i}") for i in range(4)]
    s_silu, s_sb, s_ps, s_ev, s_chain = (sem(n) for n in
                                         ("mod_silu", "mod_sb", "mod_ps", "mod_ev", "mod_chain"))
    sections = [(layer, s) for layer in range(2) for s in range(6)]

    with nc.Block() as block:
        @block.sync
        def _(sp):
            sp.dma_start(t.const[:, :], t.d_const[:, 0:C_NEG]).then_inc(s_const, 16)
            sp.dma_start(masks[:, :], t.d_const[:, C_NEG:C_END]).then_inc(s_const, 16)
            for layer in range(2):
                for b in range(B):
                    src = t.d_c[layer][b, :].rearrange("(k p) -> p k", p=P)
                    sp.dma_start(cT[:, layer, :, b], src, allow_slow_non_contiguous=True).then_inc(s_c, 16)
            for n, (layer, s) in enumerate(sections):
                if n >= 4:
                    sp.wait_ge(s_ps, n - 3)
                src = t.d_wmod[layer].rearrange("(k p) n -> p k n", p=P)[:, :, s * D:(s + 1) * D]
                sp.dma_start(ring[n % 4][:, :, :], src).then_inc(s_w[n % 4], 16)

        @block.scalar
        def _(act):
            act.wait_ge(s_c, 64)
            nc.scalar.activation(sT[:, :], cT[:, :, :, :].rearrange("p l k b -> p (l k b)"),
                                 ACT.Silu).then_inc(s_silu, 1)

        @block.vector
        def _(dve):
            link = chained(dve, s_chain)
            dve.wait_ge(s_const, 32)
            link(nc.vector.tensor_copy(t.ident_bf[:, :], t.ident))
            link(nc.vector.tensor_copy(t.neg_bf[:, :], masks[:, 0:P]))
            link(nc.vector.tensor_copy(t.negt_bf[:, :], masks[:, P:2 * P]))
            link(nc.vector.memset(t.avg[:, :], 1.0 / P))
            dve.wait_ge(s_silu, 1)
            nc.vector.tensor_copy(sB[:, :, :], spread(sT[:, :].unsqueeze(2), [P, 2 * KC * B, P])).then_inc(s_sb, 1)
            for n, (layer, s) in enumerate(sections):
                dve.wait_ge(s_ps, n + 1)
                bank = psum[2 * (n % 2)]
                if s in (2, 5):
                    for b in range(B):
                        ps = psum[2 * (n % 2) + b]
                        link(nc.vector.tensor_scalar(t2[:, :], ps[:, :], 0.25, None, ALU.max))
                        link(nc.vector.scalar_tensor_tensor(out=t1[:, :], in0=ps[:, :], scalar=-1.0, in1=t2[:, :],
                                                            op0=ALU.mult, op1=ALU.max))
                        link(nc.vector.tensor_scalar(t2[:, :], ps[:, :], 0.0, 2.0, ALU.is_ge, ALU.mult))
                        ins = nc.vector.scalar_tensor_tensor(
                            out=t.gate[:, layer, s // 3, b, :], in0=t2[:, :], scalar=-1.0, in1=t1[:, :],
                            op0=ALU.add, op1=ALU.mult)
                        if b == 0:
                            link(ins)
                        else:
                            ins.then_inc(s_ev, 1)
                            dve.wait_ge(s_ev, n + 1)
                else:
                    one = 1.0 if s in (1, 4) else 0.0
                    nc.vector.tensor_scalar(
                        t.mod[:, layer, 2 * (s // 3) + s % 3, :], bank[:, 0:KC * B], one, None,
                        ALU.add).then_inc(s_ev, 1)

        @block.tensor
        def _(pe):
            pe.wait_ge(s_sb, 1)
            for n, (layer, s) in enumerate(sections):
                pe.wait_ge(s_w[n % 4], 16 * (n // 4 + 1))
                if n >= 2:
                    pe.wait_ge(s_ev, n - 1)
                w = ring[n % 4]
                if s in (2, 5):
                    for b in range(B):
                        for k in range(KC):
                            mm = nc.tensor.matmul(psum[2 * (n % 2) + b][:, :], sB[:, (layer * KC + k) * B + b, :],
                                                  w[:, k, :], start=(k == 0), stop=(k == KC - 1))
                else:
                    for j in range(KC):
                        for k in range(KC):
                            at = (layer * KC + k) * B
                            mm = nc.tensor.matmul(psum[2 * (n % 2)][:, j * B:(j + 1) * B],
                                                  w[:, k, j * P:(j + 1) * P], sT[:, at:at + B],
                                                  start=(k == 0), stop=(k == KC - 1))
                mm.then_inc(s_ps, 1)


def latent_weights(nc, ctx, t, sem, psum):
    W = {n: t.at("nat_" + n, [P, H * HD], F32, 116 + 2 * i) for i, n in enumerate(("dkv", "uk", "uv"))}
    S2 = {n: t.at("nat_" + n, [P, KC, HD], F32, 122 + i) for i, n in enumerate(("q", "o"))}
    lng = t.at("lngT", [P, H], F32, 124)
    lnb = t.at("lnbT", [P, H], F32, 125)
    wc = t.at("wc", [P, D], F32, 126)
    wg = t.at("wg", [P, D], F32, 128)
    mt = {n: t.at("mid_" + n, [P, D], F32, 130 + 2 * i) for i, n in enumerate(("uk", "uv"))}
    nat = {n: t.at("bdn_" + n, [P, D], F32, 134 + 2 * i) for i, n in enumerate(("q", "o"))}
    bdt = {n: t.at("bdt_" + n, [P, D], F32, 138 + 2 * i) for i, n in enumerate(("q", "o"))}
    own = t.at("own_head", [P, KC, HG], F32, 142)
    col = {n: t.at("col_" + n, [P, KC], F32, 143 + i) for i, n in enumerate(("uk", "uv"))}
    s_w, s_pe, s_dve, s_chain = sem("lat_w"), sem("lat_pe"), sem("lat_dve"), sem("lat_chain")
    pairs = (("uk", "q"), ("uv", "o"))

    def blk4(ap):
        return ap.rearrange("p (g c) -> p g c", g=KC)

    with nc.Block() as block:
        @block.sync
        def _(sp):
            for n, src in (("dkv", t.d_Wdkv), ("uk", t.d_Wuk), ("uv", t.d_Wuv)):
                sp.dma_start(W[n][:, :].rearrange("l (h d) -> l h d", h=H),
                             src.rearrange("h l d -> l h d")).then_inc(s_w, 16)
            for n, src in (("q", t.d_Wq), ("o", t.d_Woh)):
                sp.dma_start(S2[n][:, :, :], src.rearrange("(g a) i j -> (a i) g j", a=HG)).then_inc(s_w, 16)
            for dst, src in ((lng, t.d_lng), (lnb, t.d_lnb)):
                sp.dma_start(dst[:, :], src.rearrange("h l -> l h"),
                             allow_slow_non_contiguous=True).then_inc(s_w, 16)

        @block.tensor
        def _(pe):
            pe.wait_ge(s_w, 16 * 7)
            nc.tensor.matmul(psum[0][:, :], t.avg[:, :], W["dkv"][:, :], start=True, stop=True).then_inc(s_pe, 1)
            pe.wait_ge(s_dve, 1)
            for g in range(KC):
                c = slice(g * P, (g + 1) * P)
                nc.tensor.matmul(psum[1][:, c], wc[:, c], wc[:, c], start=True, stop=True)
                for i, (n, m) in enumerate(pairs):
                    nc.tensor.matmul(psum[2 + i][:, c], W[n][:, c], wg[:, c], start=True, stop=True)
                    nc.tensor.transpose(psum[4 + i][:, c], nat[m][:, c], t.ident)
                    mm = nc.tensor.matmul(psum[6][:, (i * KC + g) * HG:(i * KC + g + 1) * HG], W[n][:, c],
                                          lnb[:, g * HG:(g + 1) * HG], start=True, stop=True)
            mm.then_inc(s_pe, 1)
            pe.wait_ge(s_dve, 2)
            for i, (n, m) in enumerate(pairs):
                for g in range(KC):
                    c = slice(g * P, (g + 1) * P)
                    nc.tensor.matmul(psum[2 + i][:, c], mt[n][:, c], bdt[m][:, c], start=True, stop=True)
                    mm = nc.tensor.matmul(psum[7][:, i * KC + g:i * KC + g + 1], bdt[m][:, c],
                                          col[n][:, g:g + 1], start=True, stop=True)
            mm.then_inc(s_pe, 1)

        @block.vector
        def _(dve):
            link = chained(dve, s_chain)
            blk = t.blk.unsqueeze(1).broadcast_to([P, KC, P])
            dve.wait_ge(s_w, 16 * 7)
            dve.wait_ge(s_pe, 1)
            link(nc.vector.tensor_tensor(wc[:, :], W["dkv"][:, :], psum[0][:, :], ALU.subtract))
            link(nc.vector.tensor_tensor(wg[:, :].rearrange("l (h d) -> l h d", h=H),
                                         wc[:, :].rearrange("l (h d) -> l h d", h=H),
                                         lng[:, :].unsqueeze(2).broadcast_to([P, H, HD]), ALU.mult))
            for _, m in pairs:
                for g in range(KC):
                    ins = nc.vector.tensor_tensor(
                        nat[m][:, g * P:(g + 1) * P].rearrange("p (a j) -> p a j", a=HG),
                        S2[m][:, g, :].unsqueeze(1).broadcast_to([P, HG, HD]),
                        t.blk.rearrange("p (a j) -> p a j", a=HG), ALU.mult)
            ins.then_inc(s_dve, 1)
            dve.wait_ge(s_pe, 2)
            nc.vector.scalar_tensor_tensor(out=blk4(t.bd_m[:, :]), in0=blk4(psum[1][:, :]), scalar=1.0 / LAT,
                                           in1=blk, op0=ALU.mult, op1=ALU.mult)
            for i, (n, m) in enumerate(pairs):
                nc.vector.tensor_tensor(blk4(mt[n][:, :]), blk4(psum[2 + i][:, :]), blk, ALU.mult)
                nc.vector.tensor_copy(bdt[m][:, :], psum[4 + i][:, :])
                part = psum[6][:, i * KC * HG:(i + 1) * KC * HG].rearrange("p (g a) -> p g a", a=HG)
                link(nc.vector.tensor_tensor(own[:, :, :], part,
                                             t.blk4.unsqueeze(1).broadcast_to([P, KC, HG]), ALU.mult))
                link(nc.vector.tensor_reduce(col[n][:, :], own[:, :, :], AX.X, ALU.add))
            dve.wait_ge(s_chain, 6)
            nc.vector.memset(own[:, 0, 0:1], 0.0).then_inc(s_dve, 1)
            dve.wait_ge(s_pe, 3)
            scale = float(LAT) ** -0.5
            link(nc.vector.tensor_scalar(t.bd_k[:, :], psum[2][:, :], scale, None, ALU.mult))
            link(nc.vector.tensor_copy(t.bd_v[:, :], psum[3][:, :]))
            link(nc.vector.tensor_scalar(t.kb[:, :], psum[7][:, 0:KC], scale, None, ALU.mult))
            link(nc.vector.tensor_copy(t.vb[:, :], psum[7][:, KC:2 * KC]))


def layer_norm(nc, ctx, t, sem, psum, x, h, layer, half, name, load=None, save=None, tmp=128, prefetch=None):
    xn = [t.at(f"{name}_xn{i}", [P, 4, D], F32, tmp + 8 * i) for i in range(2)]
    stats = t.at(f"{name}_stats", [P, NT, 6], F32, tmp + 16)
    mv = t.at(f"{name}_mv", [P, NT, 2], F32, tmp + 17)
    std = t.at(f"{name}_std", [P, NT], F32, tmp + 18)
    s_x, s_chain, s_var, s_std, s_xn, s_tr, s_ev, s_sv = (
        sem(f"{name}_{n}") for n in ("x", "chain", "var", "std", "xn", "tr", "ev", "sv"))
    GR = NT // 4
    with nc.Block() as block:
        @block.sync
        def _(sp):
            if load is not None:
                for g in range(GR):
                    sp.dma_start(x[:, 4 * g:4 * g + 4, :], load[:, 4 * g:4 * g + 4, :]).then_inc(s_x, 16)
            if save is not None:
                sp.dma_start(save, x[:, :, :]).then_inc(s_sv, 16)
                sp.wait_ge(s_sv, 16)
            if prefetch is not None:
                prefetch()

        @block.vector
        def _(dve):
            link = chained(dve, s_chain)
            if load is not None:
                dve.wait_ge(s_x, 16 * GR)
            for i in range(NT):
                ins = nc.vector.bn_stats(stats[:, i, :], x[:, i, :])
            link(ins)
            for i in range(NT):
                ins = nc.vector.bn_aggr(mv[:, i, :], stats[:, i, :])
            link(ins)
            nc.vector.tensor_scalar(std[:, :], mv[:, :, 1], EPS, None, ALU.add).then_inc(s_var, 1)
            dve.wait_ge(s_std, 1)
            link(nc.vector.reciprocal(std[:, :], std[:, :]))
            for g in range(GR):
                if g >= 2:
                    dve.wait_ge(s_tr, g - 1)
                for i in range(4):
                    n = 4 * g + i
                    ins = nc.vector.tensor_scalar(xn[g % 2][:, i, :], x[:, n, :], mv[:, n, 0:1], std[:, n:n + 1],
                                                  ALU.subtract, ALU.mult)
                ins.then_inc(s_xn, 1)

        @block.tensor
        def _(pe):
            for g in range(GR):
                pe.wait_ge(s_xn, g + 1)
                if g >= 2:
                    pe.wait_ge(s_ev, 4 * (g - 1))
                for k in range(KC):
                    for i in range(4):
                        mm = nc.tensor.transpose(psum[4 * (g % 2) + k][:, i * P:(i + 1) * P],
                                                 xn[g % 2][:, i, k * P:(k + 1) * P], t.ident)
                mm.then_inc(s_tr, 1)

        @block.scalar
        def _(act):
            act.wait_ge(s_var, 1)
            nc.scalar.activation(std[:, :], std[:, :], ACT.Sqrt).then_inc(s_std, 1)
            for g in range(GR):
                act.wait_ge(s_tr, g + 1)
                b = g // NH
                for k in range(KC):
                    at = k * B + b
                    dst = h[:, b, k, (g % NH) * QC:(g % NH + 1) * QC] if half == 0 else h[:, g, k, :]
                    nc.scalar.activation(dst, psum[4 * (g % 2) + k][:, :],
                                         ACT.Identity, scale=t.mod[:, layer, 2 * half + 1, at:at + 1],
                                         bias=t.mod[:, layer, 2 * half, at:at + 1]).then_inc(s_ev, 1)


def latent_keys_values(nc, ctx, t, sem, psum, h, k_all, v_all):
    prod = [t.at(f"lat_prod{i}", [P, QC], F32, 128 + 2 * i) for i in range(4)]
    wide = [t.at(f"lat_wide{i}", [P, QC // P, HG, HD], F32, 136 + 2 * i) for i in range(2)]
    turned = [t.at(f"lat_turned{i}", [P, QC], F32, 140 + 2 * i) for i in range(2)]
    tmp = [t.at(f"lat_tmp{i}", [P, QC], F32, 144 + 2 * i) for i in range(2)]
    rt = t.at("lat_rt", [P, B * KC, QB, HG], F32, 148)
    s_y, s_prod, s_vt, s_rt, s_rtd, s_wide, s_turn, s_rb, s_kraw, s_mul, s_add, s_v, s_vev = (
        sem(f"lkv_{n}") for n in ("y", "prod", "vt", "rt", "rtd", "wide", "turn", "rb", "kraw", "mul", "add", "v",
                                  "vev"))
    N = B * KC * NH
    SUB = QC // P
    VT, PY = psum[0], psum[4:8]
    PT, PK, PV = psum[1:3], psum[3:5], psum[5:8]

    def place(n):
        i, c = divmod(n, NH)
        b, g = divmod(i, KC)
        return i, c, b, g

    with nc.Block() as block:
        @block.tensor
        def _(pe):
            def variance(n):
                i, c, _, _ = place(n)
                pe.wait_ge(s_prod, n + 1)
                for q in range(SUB):
                    at = (i * QB + c * SUB + q) * HG
                    mm = nc.tensor.matmul(VT[:, at:at + HG], prod[n % 4][:, q * P:(q + 1) * P], t.blk4,
                                          start=True, stop=True)
                mm.then_inc(s_vt, 1)

            for n in range(N):
                i, c, b, g = place(n)
                if n >= 4:
                    pe.wait_ge(s_prod, n - 3)
                nc.tensor.matmul(PY[n % 4][:, :], t.bd_m[:, g * P:(g + 1) * P], h[:, b, g, c * QC:(c + 1) * QC],
                                 start=True, stop=True).then_inc(s_y, 1)
                if n >= 2:
                    variance(n - 2)
            variance(N - 2)
            variance(N - 1)
            pe.wait_ge(s_prod, N)
            for n in range(N):
                i, c, b, g = place(n)
                gs = slice(g * P, (g + 1) * P)
                if n >= 3:
                    pe.wait_ge(s_vev, n - 2)
                for q in range(SUB):
                    at = c * QC + q * P
                    mm = nc.tensor.matmul(PV[n % 3][:, q * P:(q + 1) * P], h[:, b, g, at:at + P], t.bd_v[:, gs],
                                          start=True, stop=True)
                mm.then_inc(s_v, 1)
                if n >= 2:
                    pe.wait_ge(s_mul, n - 1)
                nc.tensor.matmul(PK[n % 2][:, :], t.bd_k[:, gs], h[:, b, g, c * QC:(c + 1) * QC], start=True,
                                 stop=True).then_inc(s_kraw, 1)
                pe.wait_ge(s_wide, n + 1)
                if n >= 2:
                    pe.wait_ge(s_rb, n - 1)
                for q in range(SUB):
                    mm = nc.tensor.transpose(PT[n % 2][:, q * P:(q + 1) * P],
                                             wide[n % 2][:, q, :, :].rearrange("p a c -> p (a c)"), t.ident)
                mm.then_inc(s_turn, 1)

        @block.vector
        def _(dve):
            for n in range(N):
                i, c, b, g = place(n)
                dve.wait_ge(s_y, n + 1)
                if n >= 4:
                    dve.wait_ge(s_vt, n - 3)
                nc.vector.tensor_tensor(prod[n % 4][:, :], PY[n % 4][:, :], h[:, b, g, c * QC:(c + 1) * QC],
                                        ALU.mult).then_inc(s_prod, 1)
            dve.wait_ge(s_vt, N)
            nc.vector.tensor_scalar(rt[:, :, :, :].rearrange("p i q a -> p (i q a)"), VT[:, 0:N * SUB * HG], EPS,
                                    None, ALU.add).then_inc(s_rt, 1)
            dve.wait_ge(s_rtd, 1)
            nc.vector.reciprocal(rt[:, :, :, :], rt[:, :, :, :]).then_inc(s_rt, 1)
            dve.wait_ge(s_rt, 2)

            def widen(n):
                i, c, _, _ = place(n)
                if n >= 2:
                    dve.wait_ge(s_turn, n - 1)
                at = rt[:, i, c * SUB:(c + 1) * SUB, :].rearrange("p q a -> p (q a)")
                nc.vector.tensor_copy(wide[n % 2][:, :, :, :].rearrange("p q a c -> p (q a) c"),
                                      at.unsqueeze(2).broadcast_to([P, SUB * HG, HD])).then_inc(s_wide, 1)

            widen(0)
            for n in range(N):
                i, c, _, _ = place(n)
                if n + 1 < N:
                    widen(n + 1)
                dve.wait_ge(s_v, n + 1)
                q = slice(c * SUB, (c + 1) * SUB)
                nc.vector.tensor_tensor(
                    v_all[:, i, q, :].rearrange("p q (a d) -> p (q a) d", a=HG),
                    PV[n % 3][:, :].rearrange("p (c d) -> p c d", d=HD),
                    rt[:, i, q, :].rearrange("p q a -> p (q a)").unsqueeze(2).broadcast_to([P, QC // HD, HD]),
                    ALU.mult).then_inc(s_vev, 1)
                dve.wait_ge(s_rb, n + 1)
                dve.wait_ge(s_kraw, n + 1)
                if n >= 2:
                    dve.wait_ge(s_add, n - 1)
                nc.vector.tensor_tensor(tmp[n % 2][:, :], PK[n % 2][:, :], turned[n % 2][:, :],
                                        ALU.mult).then_inc(s_mul, 1)

        @block.scalar
        def _(act):
            act.wait_ge(s_rt, 1)
            nc.scalar.activation(rt[:, :, :, :], rt[:, :, :, :], ACT.Sqrt).then_inc(s_rtd, 1)
            for n in range(N):
                act.wait_ge(s_turn, n + 1)
                if n >= 2:
                    act.wait_ge(s_mul, n - 1)
                nc.scalar.activation(turned[n % 2][:, :], PT[n % 2][:, :], ACT.Copy).then_inc(s_rb, 1)
                i, c, _, g = place(n)
                act.wait_ge(s_mul, n + 1)
                nc.scalar.activation(k_all[:, i, c * QC:(c + 1) * QC], tmp[n % 2][:, :], ACT.Identity,
                                     bias=t.kb[:, g:g + 1]).then_inc(s_add, 1)


def project_qkv(nc, ctx, t, sem, psum, h, q_all, k_all, v_all):
    w = t.at("wqkv", [P, KC, 3 * D], F32, 128)
    bias = t.at("bqkv", [P, 3 * KC], F32, 152)
    s_w, s_ps, s_ev, s_b, s_chain = (sem(f"qkv_{n}") for n in ("w", "ps", "ev", "b", "chain"))
    NG = B * KC * NH
    with nc.Block() as block:
        @block.sync
        def _(sp):
            for k in range(KC):
                sp.dma_start(w[:, k, :], t.d_Wqkv[k * P:(k + 1) * P, :]).then_inc(s_w, 16)
            sp.dma_start(bias[:, :], t.d_bqkv.rearrange("(c p) -> p c", p=P),
                         allow_slow_non_contiguous=True).then_inc(s_b, 16)

        @block.tensor
        def _(pe):
            pe.wait_ge(s_w, 16 * KC)
            n = 0
            for i in range(B * KC):
                b, g = divmod(i, KC)
                for c in range(NH):
                    for part in range(2):
                        if n >= 8:
                            pe.wait_ge(s_ev, n - 7)
                        for k in range(KC):
                            mm = nc.tensor.matmul(psum[n % 8][:, :],
                                                  w[:, k, part * D + g * P:part * D + (g + 1) * P],
                                                  h[:, b, k, c * QC:(c + 1) * QC],
                                                  start=(k == 0), stop=(k == KC - 1))
                        mm.then_inc(s_ps, 1)
                        n += 1
            for tile in range(NT):
                b, q = divmod(tile, QB)
                pe.wait_ge(s_ev, n - 7)
                for k in range(KC):
                    mm = nc.tensor.matmul(psum[n % 8][:, :], h[:, b, k, q * P:(q + 1) * P], w[:, k, 2 * D:3 * D],
                                          start=(k == 0), stop=(k == KC - 1))
                mm.then_inc(s_ps, 1)
                n += 1

        @block.vector
        def _(dve):
            scale = float(HD) ** -0.5
            dve.wait_ge(s_b, 16)
            nc.vector.tensor_copy(t.vb[:, :], bias[:, 2 * KC:3 * KC]).then_inc(s_chain, 1)
            n = 0
            for i in range(B * KC):
                g = i % KC
                for c in range(NH):
                    for part, dst in enumerate((q_all, k_all)):
                        dve.wait_ge(s_ps, n + 1)
                        nc.vector.tensor_scalar(dst[:, i, c * QC:(c + 1) * QC], psum[n % 8][:, :],
                                                bias[:, part * KC + g:part * KC + g + 1],
                                                scale if part == 0 else 1.0, ALU.add, ALU.mult).then_inc(s_ev, 1)
                        n += 1
            for tile in range(NT):
                b, q = divmod(tile, QB)
                dve.wait_ge(s_ps, n + 1)
                nc.vector.tensor_copy(v_all[:, b * KC:(b + 1) * KC, q, :],
                                      psum[n % 8][:, :].rearrange("p (g c) -> p g c", g=KC)).then_inc(s_ev, 1)
                n += 1


HP = 2
STEPS = [(c, tb) for c in range(NH) for tb in range(4 * c + 4)]
NSTEP = len(STEPS)
S1_UNITS = [[(q, 0, a) for q in range(4) for a in range(HP)],
            [(q, c, a) for q in range(4, QB) for c in range(NH) for a in range(HP)]]
N_S1 = len(S1_UNITS[0]) + len(S1_UNITS[1])
N_S2 = NSTEP * HP
DIAG = [tb >= 4 * c for c, tb in STEPS]
S1_NEXT = [0, 0, 0, 0, 0, 2, 3, 2, 3, 3, 3, 2]
S1_OWNS = [3, 3, 0, 0, 0, 0, 0, 0, 0, 0, 0, 0]
S1_OWN = sum(S1_OWNS)
assert S1_OWN + sum(S1_NEXT) == N_S1
TURN_OWN, TURN_NEXT = 3, 10
PTS = 4
LAG = 2


def attention(nc, ctx, t, sem, psum, q_all, k_all, v_all, stack_at, name):
    TAIL = 128
    qs = [t.at(f"{name}_qs{p}", [P, HP, S], FR, stack_at + 16 * p) for p in range(2)]
    ks = [t.at(f"{name}_ks{p}", [P, HP, S], FR, stack_at + 16 * p + 8) for p in range(2)]
    qh, ql, kh, kl = (t.at(f"{name}_{n}", [P, S], FR, TAIL + 4 * i) for i, n in enumerate(("qh", "ql", "kh", "kl")))
    ve = [t.at(f"{name}_ve{p}", [P, QB, HP, 2 * HD], F32, TAIL + 16 + 4 * p) for p in range(2)]
    pt = [t.at(f"{name}_pt{p}", [P, HP, QC], F32, TAIL + 24 + 4 * p) for p in range(PTS)]
    nm = [t.at(f"{name}_nm{p}", [P, 4, 4, HD], F32, TAIL + 40 + 2 * p) for p in range(2)]
    raw = t.at(f"{name}_raw", [P, 2, N_S1], F32, TAIL + 44)
    neg = t.at(f"{name}_negmax", [P, 2, 4, HP], F32, TAIL + 44.25)
    res = [t.at(f"{name}_res{p}", [P, S], F32, TAIL + 44.5 + 4 * p) for p in range(2)]
    PS1, PS2, POD, PMT = psum[0:2], psum[2:5], psum[5:7], psum[7]
    s_st = [sem(f"{name}_stack{p}") for p in range(2)]
    s_res = [sem(f"{name}_res{p}") for p in range(2)]
    (s_seen, s_split, s_ve, s_init, s_s1, s_max, s_nm, s_mt, s_row, s_s2, s_exp, s_pv, s_od, s_nch) = (sem(f"{name}_{n}") for n in (
         "seen", "split", "ve", "init", "s1", "max", "nm", "mt", "row", "s2", "exp", "pv", "od", "nch"))
    NI = B * KC
    DMAS = 12

    def item_base(i, p, per):
        return i * (2 * per) + p * per

    with nc.Block() as block:
        @block.sync
        def _(sp):
            def stack(i, p):
                sp.wait_ge(s_split, i * 4 + 4)
                for r, (x, y) in enumerate(((qh, kh), (qh, kl), (ql, kh))):
                    for part, to in ((x, qs[p]), (y, ks[p])):
                        for a in range(HP):
                            src = part[64 * p + HD * a:64 * p + HD * a + HD, :].bitcast(F32)
                            sp.dma_start(to[HD * r:HD * r + HD, a, :].bitcast(F32), src).then_inc(s_st[p], 16)

            def result(i, p):
                sp.wait_ge(s_od, item_base(i, p, NH) + NH)
                for r, dst in enumerate((q_all, k_all)):
                    for a in range(HP):
                        sp.dma_start(dst[64 * p + HD * a:64 * p + HD * a + HD, i, :],
                                     res[p][64 * a + HD * r:64 * a + HD * r + HD, :]).then_inc(s_res[p], 16)

            stack(0, 0)
            stack(0, 1)
            with nc.sync.Fori(1, NI) as i:
                for p in range(2):
                    sp.wait_ge(s_s2, item_base(i, p, N_S2) - N_S2)
                    stack(i, p)
                    result(i - 1, p)
            for p in range(2):
                result(NI - 1, p)
            for p in range(2):
                sp.wait_ge(s_res[p], NI * 4 * 16)

        @block.gpsimd
        def _(pool):
            def held():
                nc.gpsimd.sem_inc(s_seen, 1)

            def split(i):
                held()
                for x, hi, lo in ((q_all, qh, ql), (k_all, kh, kl)):
                    nc.gpsimd.tensor_copy(hi[:, :], x[:, i, :]).then_inc(s_split, 1)
                pool.wait_ge(s_split, i * 4 + 2)
                held()
                for x, hi, lo in ((q_all, qh, ql), (k_all, kh, kl)):
                    nc.gpsimd.tensor_tensor(lo[:, :], x[:, i, :], hi[:, :].bitcast(F32),
                                            ALU.subtract).then_inc(s_split, 1)

            def values(i, p):
                held()
                for a in range(HP):
                    at = 64 * p + HD * a
                    ins = nc.gpsimd.tensor_copy(ve[p][:, :, a, 0:HD], v_all[:, i, :, at:at + HD])
                ins.then_inc(s_ve, 1)

            for p in range(2):
                nc.gpsimd.memset(ve[p][:, :, :, HD:2 * HD], 1.0).then_inc(s_init, 1)
                nc.gpsimd.memset(nm[p][:, :, :, :], 0.0).then_inc(s_init, 1)
            split(0)
            values(0, 0)

            def body(i, first, last):
                if not first:
                    pool.wait_ge(s_pv, item_base(i, 0, NSTEP))
                values(i, 1)
                if not last:
                    for q in range(2):
                        pool.wait_ge(s_st[q], i * (16 * DMAS) + 16 * DMAS)
                    split(i + 1)
                    pool.wait_ge(s_pv, item_base(i, 1, NSTEP))
                    values(i + 1, 0)

            body(0, True, False)
            with nc.gpsimd.Fori(1, NI - 1) as i:
                body(i, False, False)
            body(NI - 1, False, True)

        @block.tensor
        def _(pe):
            def score1(i, p, u0, u1):
                units = S1_UNITS[0] + S1_UNITS[1]
                for u in range(u0, u1):
                    q, c, a = units[u]
                    n = min(QC, (q + 1) * P - c * QC)
                    diag = c == q // 4
                    pe.wait_ge(s_max, item_base(i, p, N_S1) + u - 1)
                    mm = nc.tensor.matmul(PS1[u % 2][:, 0:n], qs[p][0:3 * HD, a, q * P:(q + 1) * P],
                                          ks[p][0:3 * HD, a, c * QC:c * QC + n], start=True, stop=not diag)
                    if diag:
                        mm = nc.tensor.matmul(PS1[u % 2][:, n - P:n], t.ident_bf[:, :], t.neg_bf[:, :],
                                              start=False, stop=True)
                    mm.then_inc(s_s1, 1)

            def turn(i, p, hf):
                pe.wait_ge(s_nm, item_base(i, p, 2) + hf + 1)
                if hf or not isinstance(i, int) or i or p:
                    pe.wait_ge(s_row, item_base(i, p, 2) + hf)
                for q in range(4):
                    mm = nc.tensor.transpose(PMT[:, q * P:(q + 1) * P],
                                             nm[hf][:, q, :, :].rearrange("p a c -> p (a c)"), t.ident)
                mm.then_inc(s_mt, 1)

            def pv(i, p, s):
                c, tb = STEPS[s]
                at = max(0, tb * P - c * QC)
                if tb == 0:
                    if c == 0:
                        pe.wait_ge(s_ve, item_base(i, p, 1) + 1)
                    if not (isinstance(i, int) and i == 0 and p == 0):
                        pe.wait_ge(s_od, item_base(i, p, 2) + c - 1)
                pe.wait_ge(s_exp, item_base(i, p, N_S2) + HP * s + HP)
                for a in range(HP):
                    mm = nc.tensor.matmul(POD[c][64 * a:64 * a + 64, at:QC], ve[p][:, tb, a, :],
                                          pt[s % PTS][:, a, at:QC], start=(tb == 0), stop=(tb == 4 * c + 3))
                mm.then_inc(s_pv, 1)

            def score2(i, p, s, a):
                c, tb = STEPS[s]
                at = max(0, tb * P - c * QC)
                u = HP * s + a
                if u >= 3 or not (isinstance(i, int) and i == 0 and p == 0):
                    pe.wait_ge(s_exp, item_base(i, p, N_S2) + u - 2)
                mm = nc.tensor.matmul(PS2[u % 3][:, at:QC], ks[p][:, a, tb * P:(tb + 1) * P],
                                      qs[p][:, a, c * QC + at:(c + 1) * QC], start=True, stop=not DIAG[s])
                if DIAG[s]:
                    mm = nc.tensor.matmul(PS2[u % 3][:, at:at + P], t.ident_bf[:, :], t.negt_bf[:, :],
                                          start=False, stop=True)
                mm.then_inc(s_s2, 1)

            def item(i, p, prev, nxt):
                k = 0
                for s, (c, tb) in enumerate(STEPS):
                    if tb == 0:
                        pe.wait_ge(s_row, item_base(i, p, 2) + c + 1)
                    ahead = [(nxt, k + m) for m in range(S1_NEXT[s])] if nxt is not None else []
                    k += len(ahead)
                    if S1_OWNS[s]:
                        ahead = [((i, p), N_S1 - S1_OWN + sum(S1_OWNS[:s]) + m) for m in range(S1_OWNS[s])]
                    if nxt is not None and S1_NEXT[s] and k == S1_NEXT[s]:
                        pe.wait_ge(s_st[nxt[1]], nxt[0] * (16 * DMAS) + 16 * DMAS)
                    for a in range(HP):
                        score2(i, p, s, a)
                        if ahead:
                            (it, u), ahead = ahead[0], ahead[1:]
                            score1(*it, u, u + 1)
                    if s == TURN_OWN:
                        turn(i, p, 1)
                    if nxt is not None and s == TURN_NEXT:
                        turn(*nxt, 0)
                    if s >= LAG:
                        pv(i, p, s - LAG)
                    elif prev is not None:
                        pv(*prev, NSTEP + s - LAG)
                    for it, u in ahead:
                        score1(*it, u, u + 1)

            pe.wait_ge(s_init, 6)
            pe.wait_ge(s_st[0], 16 * DMAS)
            for u, (q, c, a) in enumerate((S1_UNITS[0] + S1_UNITS[1])[:2]):
                nc.tensor.matmul(PS1[u][:, 0:P], qs[0][0:3 * HD, a, 0:P], ks[0][0:3 * HD, a, 0:P],
                                 start=True, stop=False)
                nc.tensor.matmul(PS1[u][:, 0:P], t.ident_bf[:, :], t.neg_bf[:, :], start=False,
                                 stop=True).then_inc(s_s1, 1)
            score1(0, 0, 2, N_S1 - S1_OWN)
            turn(0, 0, 0)

            def body(i, first, last):
                item(i, 0, None if first else (i - 1, 1), (i, 1))
                item(i, 1, (i, 0), None if last else (i + 1, 0))

            body(0, True, False)
            with nc.tensor.Fori(1, NI - 1) as i:
                body(i, False, False)
            body(NI - 1, False, True)
            for s in range(NSTEP - LAG, NSTEP):
                pv(NI - 1, 1, s)

        @block.scalar
        def _(act):
            def rows(i, p, hf):
                act.wait_ge(s_mt, item_base(i, p, 2) + hf + 1)
                for a in range(HP):
                    ins = nc.scalar.activation(qs[p][3 * HD:P, a, hf * QC:(hf + 1) * QC],
                                               PMT[64 + HD * a:64 + HD * a + HD, :], ACT.Copy)
                ins.then_inc(s_row, 1)

            def store(i, p, c):
                act.wait_ge(s_pv, item_base(i, p, NSTEP) + (4, 12)[c])
                if c == 0 and not (isinstance(i, int) and i == 0):
                    act.wait_ge(s_res[p], i * 64)
                nc.scalar.activation(res[p][:, c * QC:(c + 1) * QC], POD[c][:, :], ACT.Copy).then_inc(s_od, 1)

            def item(i, p, prev, nxt):
                for s, (c, tb) in enumerate(STEPS):
                    at = max(0, tb * P - c * QC)
                    if s >= PTS or prev is not None:
                        act.wait_ge(s_pv, item_base(i, p, NSTEP) + s - PTS + 1)
                    for a in range(HP):
                        u = HP * s + a
                        act.wait_ge(s_s2, item_base(i, p, N_S2) + u + 1)
                        nc.scalar.activation(pt[s % PTS][:, a, at:QC], PS2[u % 3][:, at:QC],
                                             ACT.Exp).then_inc(s_exp, 1)
                    if s == 1 and prev is not None:
                        store(*prev, 1)
                    if s == TURN_OWN:
                        rows(i, p, 1)
                    if s == 3 + LAG:
                        store(i, p, 0)
                    if nxt is not None and s == TURN_NEXT:
                        rows(*nxt, 0)

            rows(0, 0, 0)

            def body(i, first, last):
                item(i, 0, None if first else (i - 1, 1), (i, 1))
                item(i, 1, (i, 0), None if last else (i + 1, 0))

            body(0, True, False)
            with nc.scalar.Fori(1, NI - 1) as i:
                body(i, False, False)
            body(NI - 1, False, True)
            store(NI - 1, 1, 1)

        @block.vector
        def _(dve):
            def maxima(i, p, u0, u1):
                units = S1_UNITS[0] + S1_UNITS[1]
                for u in range(u0, u1):
                    q, c, a = units[u]
                    n = min(QC, (q + 1) * P - c * QC)
                    dve.wait_ge(s_s1, item_base(i, p, N_S1) + u + 1)
                    nc.vector.tensor_reduce(raw[:, p, u:u + 1], PS1[u % 2][:, 0:n], AX.X, ALU.max,
                                            negate=True).then_inc(s_max, 1)
                    for hf, end in enumerate((8, 24)):
                        if u + 1 == end:
                            parts(i, p, hf)

            def parts(i, p, hf):
                dve.wait_ge(s_max, item_base(i, p, N_S1) + (8, 24)[hf])
                if hf == 0:
                    m = raw[:, p, 0:8].rearrange("p (q a) -> p q a", a=HP)
                else:
                    m = neg[:, p, :, :]
                    both = raw[:, p, 8:24].rearrange("p (q c a) -> p q c a", c=NH, a=HP)
                    nc.vector.tensor_tensor(m, both[:, :, 0, :], both[:, :, 1, :], ALU.min).then_inc(s_nch, 1)
                    dve.wait_ge(s_nch, item_base(i, p, 3) + 2)
                if not (isinstance(i, int) and i == 0 and p == 0):
                    dve.wait_ge(s_mt, item_base(i, p, 2) + hf - 1)
                hi, lo = nm[hf][:, :, 2:4, 0], nm[hf][:, :, 2:4, 1]
                nc.vector.tensor_copy(hi.bitcast(FR), m).then_inc(s_nch, 1)
                dve.wait_ge(s_nch, item_base(i, p, 3) + (1, 3)[hf])
                nc.vector.tensor_tensor(lo, m, hi, ALU.subtract).then_inc(s_nm, 1)

            for p in range(2):
                nc.vector.memset(ks[p][3 * HD:P, :, :].bitcast(F32), 1.0).then_inc(s_init, 1)
            dve.wait_ge(s_init, 6)
            maxima(0, 0, 0, N_S1 - S1_OWN)

            def body(i, last):
                for it, nxt in (((i, 0), (i, 1)), ((i, 1), None if last else (i + 1, 0))):
                    maxima(*it, N_S1 - S1_OWN, N_S1)
                    if nxt is not None:
                        maxima(*nxt, 0, N_S1 - S1_OWN)

            body(0, False)
            with nc.vector.Fori(1, NI - 1) as i:
                body(i, False)
            body(NI - 1, True)


def divide(nc, ctx, t, sem, psum, o_all, den, name):
    inv = [t.at(f"{name}_inv{i}", [P, QC // P, HG], F32, 128 + i) for i in range(2)]
    wide = [t.at(f"{name}_wide{i}", [P, QC // P, HG, HD], F32, 130 + 2 * i) for i in range(2)]
    s_t1, s_inv, s_wide, s_t2, s_div = (sem(f"{name}_{n}") for n in ("t1", "inv", "wide", "t2", "div"))
    N = B * KC * NH
    SUB = QC // P
    T1, T2 = psum[0:4], psum[4:8]
    with nc.Block() as block:
        @block.tensor
        def _(pe):
            def back(n):
                pe.wait_ge(s_wide, n + 1)
                if n >= 4:
                    pe.wait_ge(s_div, n - 3)
                for q in range(SUB):
                    mm = nc.tensor.transpose(T2[n % 4][:, q * P:(q + 1) * P],
                                             wide[n % 2][:, q, :, :].rearrange("p a c -> p (a c)"), t.ident)
                mm.then_inc(s_t2, 1)

            for n in range(N):
                i, c = divmod(n, NH)
                if n >= 4:
                    pe.wait_ge(s_inv, n - 3)
                for q in range(SUB):
                    at = c * QC + q * P
                    mm = nc.tensor.transpose(T1[n % 4][:, q * P:(q + 1) * P], den[:, i, at:at + P], t.ident)
                mm.then_inc(s_t1, 1)
                if n >= 2:
                    back(n - 2)
            back(N - 2)
            back(N - 1)

        @block.vector
        def _(dve):
            def product(n):
                i, c = divmod(n, NH)
                dve.wait_ge(s_t2, n + 1)
                here = o_all[:, i, c * QC:(c + 1) * QC]
                nc.vector.tensor_tensor(here, here, T2[n % 4][:, :], ALU.mult).then_inc(s_div, 1)

            for n in range(N):
                dve.wait_ge(s_t1, n + 1)
                if n >= 2:
                    dve.wait_ge(s_wide, n - 1)
                nc.vector.reciprocal(inv[n % 2][:, :, :],
                                     T1[n % 4][:, :].rearrange("p (q a c) -> p q a c", q=SUB, a=HG)[:, :, :, 0]
                                     ).then_inc(s_inv, 1)
                dve.wait_ge(s_inv, n + 1)
                if n >= 2:
                    dve.wait_ge(s_t2, n - 1)
                nc.vector.tensor_copy(wide[n % 2][:, :, :, :].rearrange("p q a c -> p (q a) c"),
                                      inv[n % 2][:, :, :].rearrange("p q a -> p (q a)").unsqueeze(2)
                                      .broadcast_to([P, SUB * HG, HD])).then_inc(s_wide, 1)
                if n >= 3:
                    product(n - 3)
            for n in range(N - 3, N):
                product(n)


def output_projection(nc, ctx, t, sem, psum, o_all, x, x_src, layer, d_Wo, d_bo, name):
    wo = t.at(f"{name}_wo", [P, KC, D], F32, 160)
    bo = t.at(f"{name}_bo", [P, D], F32, 168)
    bg = t.at(f"{name}_bg", [P, B, D], F32, 170)
    vbb = t.at(f"{name}_vbb", [P, KC, P], F32, 174)
    tmp = [t.at(f"{name}_tmp{i}", [P, D], F32, 176 + 2 * i) for i in range(2)]
    nat = t.at(f"{name}_nat", [P, KC, D], F32, 128) if layer == 0 else None
    s_w, s_x, s_tr, s_ev, s_vbb, s_bp, s_bg, s_xb, s_ps, s_tmp, s_add, s_chain = (
        sem(f"{name}_{n}") for n in ("w", "x", "tr", "ev", "vbb", "bp", "bg", "xb", "ps", "tmp", "add", "chain"))
    with nc.Block() as block:
        @block.sync
        def _(sp):
            sp.dma_start((nat if layer == 0 else wo)[:, :, :],
                         d_Wo.rearrange("(k p) n -> p k n", p=P)).then_inc(s_w, 16)
            sp.dma_start(bo[:, :], d_bo.rearrange("(o n) -> o n", o=1).broadcast_to([P, D])).then_inc(s_w, 16)
            for g in range(NT // 4):
                sp.dma_start(x[:, 4 * g:4 * g + 4, :], x_src[:, 4 * g:4 * g + 4, :]).then_inc(s_x, 16)

        @block.tensor
        def _(pe):
            pe.wait_ge(s_w, 32)
            if layer == 0:
                for k in range(KC):
                    for j in range(KC):
                        mm = nc.tensor.transpose(psum[k][:, j * P:(j + 1) * P], nat[:, j, k * P:(k + 1) * P],
                                                 t.ident)
                    mm.then_inc(s_tr, 1)
                pe.wait_ge(s_ev, KC)
            pe.wait_ge(s_vbb, 1)
            for k in range(KC):
                mm = nc.tensor.matmul(psum[4][:, :], vbb[:, k, :], wo[:, k, :], start=(k == 0), stop=(k == KC - 1))
            mm.then_inc(s_bp, 1)
            for n in range(NT):
                b, q = divmod(n, QB)
                if n >= 4:
                    pe.wait_ge(s_tmp, n - 3)
                for k in range(KC):
                    mm = nc.tensor.matmul(psum[n % 4][:, :], o_all[:, b * KC + k, q * P:(q + 1) * P], wo[:, k, :],
                                          start=(k == 0), stop=(k == KC - 1))
                mm.then_inc(s_ps, 1)

        @block.scalar
        def _(act):
            if layer == 0:
                for k in range(KC):
                    act.wait_ge(s_tr, k + 1)
                    nc.scalar.activation(wo[:, k, :], psum[k][:, :], ACT.Copy).then_inc(s_ev, 1)

        @block.vector
        def _(dve):
            nc.vector.tensor_copy(vbb[:, :, :], t.vb[:, :].unsqueeze(2).broadcast_to([P, KC, P])).then_inc(s_vbb, 1)
            dve.wait_ge(s_bp, 1)
            dve.wait_ge(s_w, 32)
            nc.vector.tensor_tensor(tmp[0][:, :], psum[4][:, :], bo[:, :], ALU.add).then_inc(s_chain, 1)
            dve.wait_ge(s_chain, 1)
            for b in range(B):
                ins = nc.vector.tensor_tensor(bg[:, b, :], tmp[0][:, :], t.gate[:, layer, 0, b, :], ALU.mult)
            ins.then_inc(s_bg, 1)
            dve.wait_ge(s_bg, 1)
            for n in range(NT):
                dve.wait_ge(s_ps, n + 1)
                if n >= 2:
                    dve.wait_ge(s_add, n - 1)
                nc.vector.tensor_tensor(tmp[n % 2][:, :], psum[n % 4][:, :], t.gate[:, layer, 0, n // QB, :],
                                        ALU.mult).then_inc(s_tmp, 1)

        @block.gpsimd
        def _(pool):
            pool.wait_ge(s_bg, 1)
            pool.wait_ge(s_x, 16 * (NT // 4))
            for n in range(NT):
                ins = nc.gpsimd.tensor_tensor(x[:, n, :], x[:, n, :], bg[:, n // QB, :], ALU.add)
            ins.then_inc(s_xb, 1)
            pool.wait_ge(s_xb, 1)
            for n in range(NT):
                pool.wait_ge(s_tmp, n + 1)
                nc.gpsimd.tensor_tensor(x[:, n, :], x[:, n, :], tmp[n % 2][:, :], ALU.add).then_inc(s_add, 1)


def route(nc, ctx, t, sem, psum, h, d_wgate, d_gates, prefetch):
    wg = t.at("rt_wg", [P, KC, E], F32, 160)
    lg = t.at("rt_logits", [P, NT, E], F32, 161)
    cmp_ = t.at("rt_cmp", [P, NT, E], F32, 162)
    rank = t.at("rt_rank", [P, NT, E], F32, 163)
    second = t.at("rt_second", [P, NT, E], F32, 164)
    m1, m2, ex, w1 = (t.at(f"rt_{n}", [P, NT], F32, 165 + 0.25 * i) for i, n in enumerate(("m1", "m2", "ex", "w1")))
    gt = t.at("rt_gt", [P, P], F32, 166)
    s_w, s_lg, s_d, s_e, s_g, s_t, s_gt, s_out, s_chain = (
        sem(f"rt_{n}") for n in ("w", "lg", "d", "e", "g", "t", "gt", "out", "chain"))
    with nc.Block() as block:
        @block.sync
        def _(sp):
            sp.dma_start(wg[:, :, :], d_wgate.rearrange("(k p) e -> p k e", p=P)).then_inc(s_w, 16)
            prefetch()
            sp.wait_ge(s_gt, 1)
            sp.dma_start(d_gates.rearrange("n e q -> (n e) q"), gt[:, :]).then_inc(s_out, 16)
            sp.wait_ge(s_out, 16)

        @block.tensor
        def _(pe):
            pe.wait_ge(s_w, 16)
            for n in range(NT):
                for k in range(KC):
                    mm = nc.tensor.matmul(psum[0][:, n * E:(n + 1) * E],
                                          h[:, n // 4, k, (n % 4) * P:(n % 4 + 1) * P], wg[:, k, :],
                                          start=(k == 0), stop=(k == KC - 1))
            mm.then_inc(s_lg, 1)
            pe.wait_ge(s_g, 1)
            nc.tensor.transpose(psum[1][:, 0:P], rank[:, :, :].rearrange("p n e -> p (n e)"), t.ident).then_inc(s_t, 1)

        @block.scalar
        def _(act):
            act.wait_ge(s_d, 1)
            nc.scalar.activation(ex[:, :], m2[:, :], ACT.Exp).then_inc(s_e, 1)

        @block.vector
        def _(dve):
            link = chained(dve, s_chain)
            tt, v = nc.vector.tensor_tensor, nc.vector
            dve.wait_ge(s_lg, 1)
            link(v.tensor_copy(lg[:, :, :].rearrange("p n e -> p (n e)"), psum[0][:, 0:NT * E]))
            link(v.memset(rank[:, :, :], 0.0))
            for e in range(E):
                one = lg[:, :, e:e + 1]
                ins = tt(cmp_[:, :, 0:e + 1], one.broadcast_to([P, NT, e + 1]), lg[:, :, 0:e + 1], ALU.is_gt)
                if e + 1 < E:
                    ins = tt(cmp_[:, :, e + 1:E], one.broadcast_to([P, NT, E - e - 1]), lg[:, :, e + 1:E], ALU.is_ge)
                link(ins)
                link(tt(rank[:, :, :], rank[:, :, :], cmp_[:, :, :], ALU.add))
            link(v.tensor_scalar(second[:, :, :], rank[:, :, :], 1.0, None, ALU.is_equal))
            link(v.tensor_scalar(rank[:, :, :], rank[:, :, :], 0.0, None, ALU.is_equal))
            link(v.tensor_reduce(m1[:, :], lg[:, :, :], AX.X, ALU.max))
            link(tt(cmp_[:, :, :], lg[:, :, :], second[:, :, :], ALU.mult))
            link(v.tensor_reduce(m2[:, :], cmp_[:, :, :], AX.X, ALU.add))
            tt(m2[:, :], m2[:, :], m1[:, :], ALU.subtract).then_inc(s_d, 1)
            dve.wait_ge(s_e, 1)
            link(v.tensor_scalar(w1[:, :], ex[:, :], 1.0, None, ALU.add))
            link(v.reciprocal(w1[:, :], w1[:, :]))
            link(tt(ex[:, :], ex[:, :], w1[:, :], ALU.mult))
            link(tt(rank[:, :, :], rank[:, :, :], w1[:, :].unsqueeze(2).broadcast_to([P, NT, E]), ALU.mult))
            link(tt(second[:, :, :], second[:, :, :], ex[:, :].unsqueeze(2).broadcast_to([P, NT, E]), ALU.mult))
            tt(rank[:, :, :], rank[:, :, :], second[:, :, :], ALU.add).then_inc(s_g, 1)
            dve.wait_ge(s_t, 1)
            v.tensor_copy(gt[:, :], psum[1][:, 0:P]).then_inc(s_gt, 1)


class FeedForwardBuffers:
    BLK = 2 * P
    NB = F // BLK

    def __init__(self, t, sem, name, kib):
        self.raw = [t.at(f"{name}_w{i}", [P, 3, KC * self.BLK], F32, kib + 24 * i) for i in range(2)]
        self.lo = [t.at(f"{name}_wlo{i}", [P, 3, KC * self.BLK], FR, kib + 24 * i) for i in range(2)]
        self.hi = [t.at(f"{name}_whi{i}", [P, 3, KC * self.BLK], FR, kib + 24 * i + 12) for i in range(2)]
        self.s_w = [sem(f"{name}_w{i}") for i in range(2)]

    def load(self, nc, slot, srcs):
        for which, src in enumerate(srcs):
            to = self.raw[slot][:, which, :]
            dst = to.rearrange("p (k m) -> p k m", k=KC) if which < 2 else to.rearrange("p (m d) -> p m d", d=D)
            nc.sync.dma_start(dst, src).then_inc(self.s_w[slot], 16)


def feed_forward(nc, ctx, t, sem, psum, h, h_lo, h_hi, x, bufs, sources, layer, name, at0, d_gates=None):
    BLK, NB = bufs.BLK, bufs.NB
    act_t = [t.at(f"{name}_act{i}", [P, QC], F32, at0 + 2 * i) for i in range(2)]
    hid = [t.at(f"{name}_hid{i}", [P, QC], F32, at0 + 4 + 2 * i) for i in range(2)]
    hid_lo = [t.at(f"{name}_hidlo{i}", [P, QC], FR, at0 + 4 + 2 * i) for i in range(2)]
    hid_hi = [t.at(f"{name}_hidhi{i}", [P, QC], FR, at0 + 8 + 2 * i) for i in range(2)]
    tmp = t.at(f"{name}_tmp", [P, 4, D], F32, at0 + 12)
    gb = [t.at(f"{name}_gb{i}", [P, QC], F32, at0 + 20 + 2 * i) for i in range(4)]
    (s_hh, s_h_split, s_whi, s_wlo, s_up, s_act, s_mul, s_prod, s_hi, s_lo, s_down, s_tmp, s_xa, s_seen) = (
        sem(f"{name}_{n}") for n in ("hh", "h_split", "whi", "wlo", "up", "act", "mul", "prod", "hi", "lo",
                                     "down", "tmp", "xa", "seen"))
    s_g = [sem(f"{name}_g{i}") for i in range(4)]
    UP0, UP1, ACC = psum[0:2], psum[2:4], psum[4:8]
    gated = d_gates is not None
    SUB = QC // P
    GR = TOK // QC
    PER = 2 * GR
    at_first = lambda i, g: isinstance(i, int) and i == 0 and g == 0

    def chunk(i, g, c):
        return i * (2 * PER) + (2 * g + c)

    def parts(tile, which, slot):
        w = tile[slot][:, which, :]
        return w.rearrange("p (k m) -> p k m", k=KC) if which < 2 else w.rearrange("p (m d) -> p m d", d=D)

    def loop(eng, body):
        body(0, True, False)
        with eng.Fori(1, NB // 2 - 1) as i:
            body(i, False, False)
        body(NB // 2 - 1, False, True)

    with nc.Block() as block:
        @block.sync
        def _(sp):
            def gates(i, jj, T):
                if not (isinstance(i, int) and i == 0 and jj == 0):
                    sp.wait_ge(s_prod, chunk(i, GR * jj + T, 0) - 6)
                src = d_gates.rearrange("(t n) e q -> e t n q", n=SUB)[2 * i + jj, T:T + 1, :, :]
                sp.dma_start(gb[T][:, :].rearrange("p (n q) -> p n q", n=SUB),
                             src.broadcast_to([P, SUB, P])).then_inc(s_g[T], 16)

            def body(i, first, last):
                for jj in range(2):
                    if gated:
                        for T in range(GR):
                            gates(i, jj, T)
                    if not (first and jj == 0) and not (last and jj == 1):
                        sp.wait_ge(s_down, chunk(i, GR * jj, 0))
                        bufs.load(nc, 1 - jj, sources(2 * i + jj + 1))

            loop(nc.sync, body)

        @block.tensor
        def _(pe):
            def up(i, g, c):
                jj, T = divmod(g, GR)
                if c == 0:
                    if T == 0:
                        pe.wait_ge(s_wlo, (i * 2 + jj) * 3 + 3)
                    if at_first(i, 0) and jj == 0:
                        pe.wait_ge(s_h_split, T + 1)
                if not (at_first(i, g)):
                    pe.wait_ge(s_mul, chunk(i, g, c) - 1)
                for which, bank in ((0, UP0), (1, UP1)):
                    whi, wlo = parts(bufs.hi, which, jj), parts(bufs.lo, which, jj)
                    for k in range(KC):
                        col = slice(c * P, (c + 1) * P)
                        for r, (w, z) in enumerate(((whi, h_hi), (whi, h_lo), (wlo, h_hi))):
                            mm = nc.tensor.matmul(bank[c][:, :], w[:, k, col], z[:, T, k, :],
                                                  start=(k == 0 and r == 0), stop=(k == KC - 1 and r == 2))
                mm.then_inc(s_up, 1)

            def down(i, g, c):
                jj, T = divmod(g, GR)
                pe.wait_ge(s_lo, chunk(i, g, c) + 1)
                whi, wlo = parts(bufs.hi, 2, jj), parts(bufs.lo, 2, jj)
                for sub in range(SUB):
                    if c == 0 and not at_first(i, g):
                        pe.wait_ge(s_tmp, i * (SUB * PER) + SUB * (g - 1) + sub + 1)
                    col = slice(sub * P, (sub + 1) * P)
                    for r, (z, w) in enumerate(((hid_hi, whi), (hid_hi, wlo), (hid_lo, whi))):
                        mm = nc.tensor.matmul(ACC[sub][:, :], z[c][:, col], w[:, c, :],
                                              start=(c == 0 and r == 0), stop=(c == 1 and r == 2))
                mm.then_inc(s_down, 1)

            def body(i, first, last):
                for g in range(PER):
                    up(i, g, 0)
                    if g:
                        down(i, g - 1, 1)
                    elif not first:
                        down(i - 1, PER - 1, 1)
                    up(i, g, 1)
                    down(i, g, 0)

            loop(nc.tensor, body)
            down(NB // 2 - 1, PER - 1, 1)

        @block.scalar
        def _(act):
            def weights(i, jj, which):
                if which == 0:
                    act.wait_ge(bufs.s_w[jj], i * 48 + 48)
                nc.scalar.activation(bufs.hi[jj][:, which, :], bufs.raw[jj][:, which, :],
                                     ACT.Copy).then_inc(s_whi, 1)

            def silu(i, g, c):
                act.wait_ge(s_up, chunk(i, g, c) + 1)
                if not at_first(i, g):
                    act.wait_ge(s_mul, chunk(i, g, c) - 1)
                nc.scalar.activation(act_t[c][:, :], UP0[c][:, :], ACT.Silu).then_inc(s_act, 1)

            def high(i, g, c):
                act.wait_ge(s_prod if gated else s_mul, chunk(i, g, c) + 1)
                nc.scalar.activation(hid_hi[c][:, :], hid[c][:, :], ACT.Copy).then_inc(s_hi, 1)

            def body(i, first, last):
                for g in range(PER):
                    for c in range(2):
                        silu(i, g, c)
                        high(i, g, c)
                    jj, T = divmod(g, GR)
                    if T and not (last and jj):
                        weights(i + jj, 1 - jj, T - 1)

            for which in range(3):
                weights(0, 0, which)
            for T in range(GR):
                nc.scalar.activation(h_hi[:, T, :, :], h[:, T, :, :], ACT.Copy).then_inc(s_hh, 1)
            loop(nc.scalar, body)

        @block.vector
        def _(dve):
            def weights(i, jj, which):
                dve.wait_ge(s_whi, (i * 2 + jj) * 3 + which + 1)
                nc.vector.tensor_tensor(bufs.lo[jj][:, which, :], bufs.raw[jj][:, which, :], bufs.hi[jj][:, which, :].bitcast(F32),
                                        ALU.subtract).then_inc(s_wlo, 1)

            def product(i, g, c):
                n = chunk(i, g, c)
                dve.wait_ge(s_act, n + 1)
                if not at_first(i, g):
                    dve.wait_ge(s_down, n - 1)
                here = hid[c][:, :]
                nc.vector.tensor_tensor(here, act_t[c][:, :], UP1[c][:, :], ALU.mult).then_inc(s_mul, 1)
                if gated:
                    jj, T = divmod(g, GR)
                    if c == 0:
                        dve.wait_ge(s_g[T], (i * 2 + jj) * 16 + 16)
                    dve.wait_ge(s_mul, n + 1)
                    nc.vector.tensor_tensor(here, here, gb[T][:, :], ALU.mult).then_inc(s_prod, 1)

            def residual(i, g):
                T = g % GR
                dve.wait_ge(s_down, chunk(i, g, 1) + 1)
                for sub in range(SUB):
                    m = i * (SUB * PER) + (SUB * g + sub)
                    if not at_first(i, g):
                        dve.wait_ge(s_xa, m - 3)
                    nc.vector.tensor_tensor(tmp[:, sub, :], ACC[sub][:, :], t.gate[:, layer, 1, T // NH, :],
                                            ALU.mult).then_inc(s_tmp, 1)
                for sub in range(SUB):
                    m = i * (SUB * PER) + (SUB * g + sub)
                    dve.wait_ge(s_tmp, m + 1)
                    here = x[:, T * SUB + sub, :]
                    nc.vector.tensor_tensor(here, here, tmp[:, sub, :], ALU.add).then_inc(s_xa, 1)

            def body(i, first, last):
                for g in range(PER):
                    product(i, g, 0)
                    if g:
                        residual(i, g - 1)
                    elif not first:
                        residual(i - 1, PER - 1)
                    product(i, g, 1)
                    jj, T = divmod(g, GR)
                    if T and not (last and jj):
                        weights(i + jj, 1 - jj, T - 1)

            for which in range(3):
                weights(0, 0, which)
            for T in range(GR):
                dve.wait_ge(s_hh, T + 1)
                nc.vector.tensor_tensor(h_lo[:, T, :, :], h[:, T, :, :], h_hi[:, T, :, :].bitcast(F32),
                                        ALU.subtract).then_inc(s_h_split, 1)
            loop(nc.vector, body)
            residual(NB // 2 - 1, PER - 1)

        @block.gpsimd
        def _(pool):
            def body(i, first, last):
                for g in range(PER):
                    for c in range(2):
                        pool.wait_ge(s_hi, chunk(i, g, c) + 1)
                        nc.gpsimd.sem_inc(s_seen, 1)
                        nc.gpsimd.tensor_tensor(hid_lo[c][:, :], hid[c][:, :],
                                                hid_hi[c][:, :].bitcast(F32), ALU.subtract).then_inc(s_lo, 1)

            loop(nc.gpsimd, body)


def ffn_weights(nc, ctx, t, sem, psum, w1, w3, wd, spare, stores):
    ring = [t.at(f"fw_ring{i}", [P, 4, D], F32, 160 + 8 * i) for i in range(2)]
    s_ld = [sem(f"fw_ld{i}") for i in range(2)]
    s_tr, s_ev, s_had, s_hev, s_bd, s_bp, s_st = (
        sem(f"fw_{n}") for n in ("tr", "ev", "had", "hev", "bd", "bp", "st"))
    NLD = 12
    d_count = [[sum(FC // (2 << s) for s in range(st + 1)) for st in range(4)]] * 2
    with nc.Block() as block:
        @block.sync
        def _(sp):
            for n in range(NLD):
                which, j = divmod(n, 4)
                if n >= 2:
                    sp.wait_ge(s_tr, 4 * (n - 1))
                if which < 2:
                    src = (t.d_W1, t.d_W3)[which].rearrange("(c p) d -> p c d", p=P)[:, 4 * j:4 * j + 4, :]
                else:
                    src = t.d_W2[j * P:(j + 1) * P, :].rearrange("p (c d) -> p c d", c=4)
                sp.dma_start(ring[n % 2][:, :, :], src).then_inc(s_ld[n % 2], 16)
            for which, w in enumerate((w1, w3)):
                sp.wait_ge(s_ev, 16 * which + 16)
                for j in range(F // (2 * P)):
                    sp.dma_start(stores[which][j, :, :, :], w[:, :, j * 2 * P:(j + 1) * 2 * P]).then_inc(s_st, 16)
            sp.wait_ge(s_bd, d_count[0][3] * 2)
            sp.wait_ge(s_bp, d_count[1][3] * 2)
            sp.dma_start(stores[2].rearrange("j p m d -> p j m d"),
                         wd[:, :, :].rearrange("p (j m) d -> p j m d", m=2)).then_inc(s_st, 16)
            sp.wait_ge(s_st, 16 * (2 * F // (2 * P) + 1))

        @block.tensor
        def _(pe):
            for n in range(NLD):
                which, j = divmod(n, 4)
                pe.wait_ge(s_ld[n % 2], 16 * (n // 2 + 1))
                for k in range(KC):
                    m = 4 * n + k
                    if m >= 8:
                        pe.wait_ge(s_ev, m - 7)
                    for i in range(4):
                        src = ring[n % 2][:, i, k * P:(k + 1) * P] if which < 2 else \
                            ring[n % 2][:, k, i * P:(i + 1) * P]
                        mm = nc.tensor.transpose(psum[m % 8][:, i * P:(i + 1) * P], src, t.ident)
                    mm.then_inc(s_tr, 1)
            for c in range(FC):
                pe.wait_ge(s_ev, 48 if c == 0 else 48)
                if c >= 8:
                    pe.wait_ge(s_hev, c - 7)
                nc.tensor.matmul(psum[c % 8][:, :], t.had, wd[:, c, :], start=True, stop=True).then_inc(s_had, 1)

        @block.scalar
        def _(act):
            for m in range(48):
                n, k = divmod(m, 4)
                which, j = divmod(n, 4)
                act.wait_ge(s_tr, m + 1)
                if which < 2:
                    dst = (w1, w3)[which][:, k, j * QC:(j + 1) * QC]
                    src = psum[m % 8][:, :]
                else:
                    dst = wd[:, 4 * k:4 * k + 4, j * P:(j + 1) * P]
                    src = psum[m % 8][:, :].rearrange("p (c d) -> p c d", c=4)
                nc.scalar.activation(dst, src, ACT.Copy).then_inc(s_ev, 1)
            for c in range(FC):
                act.wait_ge(s_had, c + 1)
                nc.scalar.activation(wd[:, c, :], psum[c % 8][:, :], ACT.Copy).then_inc(s_hev, 1)

        def butterfly(eng, mine, other, which):
            cols = slice(0, 320) if which == 0 else slice(320, D)
            eng.wait_ge(s_hev, FC)
            for st in range(4):
                src, dst = (wd, spare) if st % 2 == 0 else (spare, wd)
                d = 1 << st
                if st:
                    eng.wait_ge(mine, 2 * d_count[which][st - 1])
                v = lambda z: z[:, :, cols].rearrange("p (a two b) n -> p a two b n", two=2, b=d)
                for a in range(FC // (2 * d)):
                    lo, hi = src[:, 2 * d * a:2 * d * a + d, cols], src[:, 2 * d * a + d:2 * d * a + 2 * d, cols]
                    eng.tensor_tensor(dst[:, 2 * d * a:2 * d * a + d, cols], lo, hi, ALU.add).then_inc(mine, 1)
                    eng.tensor_tensor(dst[:, 2 * d * a + d:2 * d * a + 2 * d, cols], lo, hi,
                                      ALU.subtract).then_inc(mine, 1)

        @block.vector
        def _(dve):
            butterfly(dve, s_bd, s_bp, 0)

        @block.gpsimd
        def _(pool):
            butterfly(pool, s_bp, s_bd, 1)


def build(nc, d, d_const, d_out, stop=99):
    ctx = ExitStack()
    with ctx:
        t = Shared()

        def sb(name, shape, dt=F32):
            return ctx.enter_context(nc.sbuf_tensor(name, shape, dt))

        sems = ExitStack()

        used = []

        def sem(name):
            used.append(sems.enter_context(nc.semaphore(name)))
            return used[-1]

        psum = [ctx.enter_context(nc.psum_tensor(f"bank{i}", [P, QC], F32)) for i in range(8)]

        t.const = sb("const", [P, C_NEG])
        t.ident, t.blk = t.const[:, C_ID:C_ID + P], t.const[:, C_BLK:C_BLK + P]
        t.had = t.const[:, C_HAD:C_HAD + P]
        t.blk4 = t.const[:, C_BLK:C_BLK + P:HD]
        t.ident_bf, t.neg_bf, t.negt_bf = (sb(n, [P, P], BF16) for n in ("ident_bf", "neg_bf", "negt_bf"))
        t.avg = sb("avg", [P, P])
        t.mod = sb("mod", [P, 2, 4, KC * B])
        t.gate = sb("gate", [P, 2, 2, B, D])
        t.bd_m, t.bd_k, t.bd_v = (sb(n, [P, D]) for n in ("bd_m", "bd_k", "bd_v"))
        t.kb, t.vb = sb("kb", [P, KC]), sb("vb", [P, KC])
        t.eps = sb("eps", [P, 1])
        base = 43 * 1024

        def at(name, shape, dt, kib):
            return nc.alloc_sbuf_tensor_at(name, shape, dt, offset=base + int(kib * 1024))
        t.at = at

        t.d_const = d_const
        t.d_c = [d["L0_c"], d["L1_c"]]
        t.d_wmod = [d["L0_wmod"], d["L1_wmod"]]
        t.d_Wdkv, t.d_Wuk, t.d_Wuv = d["L0_attn_Wdkv"], d["L0_attn_Wuk"], d["L0_attn_Wuv"]
        t.d_Wq, t.d_Woh, t.d_lng, t.d_lnb = d["L0_attn_Wq"], d["L0_attn_Wo_h"], d["L0_attn_ln_g"], d["L0_attn_ln_b"]
        t.d_Wqkv, t.d_bqkv = d["L1_attn_Wqkv"], d["L1_attn_bqkv"]
        t.d_W1, t.d_W2, t.d_W3 = d["L1_ffn_W1"], d["L1_ffn_W2"], d["L1_ffn_W3"]
        d_x = d["L0_attn_x"].rearrange("b (n p) d -> p (b n) d", p=P)
        d_res = nc.dram_tensor("x_mid", [P, NT, D], F32, kind="Internal").ap()
        d_gates = nc.dram_tensor("gates", [NT, E, P], F32, kind="Internal").ap()
        d_y = d_out.rearrange("b (n p) d -> p (b n) d", p=P)

        def region(name, kib, shape):
            return at(name, shape, F32, kib)

        def finish(x):
            s = sem("stored")
            with nc.Block() as block:
                @block.sync
                def _(sp):
                    sp.dma_start(d_y, x[:, :, :]).then_inc(s, 16)
                    sp.wait_ge(s, 16)

        s_eps = sem("eps_set")
        with nc.Block() as block:
            @block.vector
            def _(dve):
                nc.vector.memset(t.eps[:, :], EPS).then_inc(s_eps, 1)
                dve.wait_ge(s_eps, 1)

        modulation(nc, ctx, t, sem, psum)
        latent_weights(nc, ctx, t, sem, psum)

        x = region("x_l0a", 0, [P, NT, D])
        h = region("h_l0a", 32, [P, B, KC, S])
        layer_norm(nc, ctx, t, sem, psum, x, h, 0, 0, "ln0a", load=d_x)
        k_all = region("k_l0", 64, [P, B * KC, S])
        v_all = region("v_l0", 96, [P, B * KC, QB, P])
        latent_keys_values(nc, ctx, t, sem, psum, h, k_all, v_all)
        q_all = h[:, :, :, :].rearrange("p b k s -> p (b k) s")
        if stop == 1:
            return finish(h_as_x(h, t, at))
        attention(nc, ctx, t, sem, psum, q_all, k_all, v_all, 0, "at0")
        divide(nc, ctx, t, sem, psum, q_all, k_all, "dv0")
        x = region("x_l0b", 0, [P, NT, D])
        output_projection(nc, ctx, t, sem, psum, q_all, x, d_x, 0, d["L0_attn_Wo"], d["L0_attn_bo"], "op0")
        if stop == 2:
            return finish(x)
        h = region("h_l0b", 32, [P, NT // 4, KC, QC])
        h_lo, h_hi = (at(f"h_l0b_{n}", [P, NT // 4, KC, QC], FR, kib) for n, kib in (("lo", 32), ("hi", 64)))
        layer_norm(nc, ctx, t, sem, psum, x, h, 0, 1, "ln0b", tmp=144)
        ups = [d[n].rearrange("e (k p) m -> e p k m", p=P) for n in ("L0_ffn_wi_0", "L0_ffn_wi_1")]
        downs = d["L0_ffn_wo"].rearrange("e (m p) d -> e p m d", p=P)
        bufs = FeedForwardBuffers(t, sem, "moe", 96)

        def expert(j):
            return [w[j, :, :, :] for w in (*ups, downs)]

        route(nc, ctx, t, sem, psum, h, d["L0_ffn_w_gate"], d_gates,
              prefetch=lambda: [bufs.load(nc, j, expert(j)) for j in range(2)])
        feed_forward(nc, ctx, t, sem, psum, h, h_lo, h_hi, x, bufs, expert, 0, "moe", 144, d_gates=d_gates)
        if stop == 3:
            return finish(x)

        numbers = sorted(s.num for s in used)
        assert numbers == list(range(numbers[0], numbers[-1] + 1))
        with nc.Block() as block:
            @block.sync
            def _(sp):
                sp.sem_clear(range(numbers[0], numbers[-1] + 1))
        sems.close()
        h = region("h_l1a", 32, [P, B, KC, S])
        layer_norm(nc, ctx, t, sem, psum, x, h, 1, 0, "ln1a", save=d_res)
        q_all, k_all = region("q_l1", 0, [P, B * KC, S]), region("k_l1", 64, [P, B * KC, S])
        v_all = region("v_l1", 96, [P, B * KC, QB, P])
        project_qkv(nc, ctx, t, sem, psum, h, q_all, k_all, v_all)
        attention(nc, ctx, t, sem, psum, q_all, k_all, v_all, 32, "at1")
        divide(nc, ctx, t, sem, psum, q_all, k_all, "dv1")
        w1, w3 = region("ffn_w1", 64, [P, KC, F]), region("ffn_w3", 96, [P, KC, F])
        wd, spare = region("ffn_wd", 128, [P, FC, D]), region("ffn_spare", 32, [P, FC, D])
        blocks = [nc.dram_tensor(f"ffn_blocks{n}", [F // (2 * P), P, *m], F32, kind="Internal").ap()
                  for n, m in enumerate(((KC, 2 * P), (KC, 2 * P), (2, D)))]
        ffn_weights(nc, ctx, t, sem, psum, w1, w3, wd, spare, blocks)
        x = region("x_l1b", 32, [P, NT, D])
        output_projection(nc, ctx, t, sem, psum, q_all, x, d_res, 1, d["L1_attn_Wo"], d["L1_attn_bo"], "op1")
        if stop == 4:
            return finish(x)
        h = region("h_l1b", 0, [P, NT // 4, KC, QC])
        h_lo, h_hi = (at(f"h_l1b_{n}", [P, NT // 4, KC, QC], FR, kib) for n, kib in (("lo", 0), ("hi", 64)))
        bufs = FeedForwardBuffers(t, sem, "ffn", 96)

        def hidden_block(j):
            return [w[j, :, :, :] for w in blocks]

        layer_norm(nc, ctx, t, sem, psum, x, h, 1, 1, "ln1b", tmp=144,
                   prefetch=lambda: [bufs.load(nc, j, hidden_block(j)) for j in range(2)])
        feed_forward(nc, ctx, t, sem, psum, h, h_lo, h_hi, x, bufs, hidden_block, 1, "ffn", 144)
        finish(x)


_INS = ["L0_attn_x", "L0_attn_Wq", "L0_attn_Wdkv", "L0_attn_Wuk", "L0_attn_Wuv", "L0_attn_ln_g", "L0_attn_ln_b",
        "L0_attn_Wo_h", "L0_attn_Wo", "L0_attn_bo", "L0_ffn_w_gate", "L0_ffn_wi_0", "L0_ffn_wi_1", "L0_ffn_wo",
        "L0_c", "L0_wmod", "L1_attn_Wqkv", "L1_attn_bqkv", "L1_attn_Wo", "L1_attn_bo", "L1_ffn_W1", "L1_ffn_W2",
        "L1_ffn_W3", "L1_c", "L1_wmod"]


def kernel(**inputs):
    import numpy as _np
    import concourse.bacc as _bacc
    from concourse import mybir as _mybir
    from concourse.bass_utils import run_bass_kernel_spmd as _run

    nc = _bacc.Bacc("TRN2", target_bir_lowering=False, num_devices=1)
    arrays, aps = {}, {}
    for name in _INS:
        a = _np.ascontiguousarray(inputs[name])
        arrays[f"in_{name}"] = a
        aps[name] = nc.dram_tensor(f"in_{name}", a.shape, _mybir.dt.from_np(a.dtype), kind="ExternalInput").ap()
    table = constant_table()
    arrays["in_constants"] = table
    consts = nc.dram_tensor("in_constants", table.shape, F32, kind="ExternalInput").ap()
    out = nc.dram_tensor("out_x", (B, S, D), F32, kind="ExternalOutput").ap()
    build(nc, aps, consts, out)
    r = _run(nc, [arrays], core_ids=[0])
    return r.results[0]["out_x"]
```

```python
from contextlib import ExitStack

import concourse.bass as bass
import numpy as np
from concourse import mybir

P = 128
B, S, D = 2, 1024, 512
TOK = B * S
NT = TOK // P
KC = D // P
H, HD, LAT = 16, 32, 128
HG = P // HD
QB = S // P
QC = 512
NH = S // QC
E, M = 8, 256
F = 2048
FC = F // P
EPS = 1e-5
NEG = -1e30

ALU = mybir.AluOpType
ACT = mybir.ActivationFunctionType
AX = mybir.AxisListType
F32 = mybir.dt.float32
FR = mybir.dt.float32r
BF16 = mybir.dt.bfloat16


class Shared:
    pass


C_ID, C_BLK, C_HAD, C_NEG, C_NEGT, C_END = 0, P, 2 * P, 3 * P, 4 * P, 5 * P


def constant_table():
    t = np.zeros((P, C_END), np.float32)
    t[:, C_ID:C_ID + P] = np.eye(P)
    blk = np.arange(P) // HD
    t[:, C_BLK:C_BLK + P] = blk[:, None] == blk[None, :]
    had = np.ones((1, 1))
    while had.shape[0] < P:
        had = np.block([[had, had], [had, -had]])
    t[:, C_HAD:C_HAD + P] = had / np.sqrt(F)
    t[:, C_NEG:C_NEG + P] = np.where(np.arange(P)[None, :] > np.arange(P)[:, None], NEG, 0.0)
    t[:, C_NEGT:C_NEGT + P] = t[:, C_NEG:C_NEG + P].T
    return t


def chained(eng, sem):
    count = [0]

    def link(ins):
        count[0] += 1
        ins.then_inc(sem, 1)
        eng.wait_ge(sem, count[0])
    return link


class Modulation:
    SLOTS = 8

    def __init__(self, t, sem):
        self.cT = t.at("cT", [P, 2, KC, B], F32, 128)
        self.sT = t.at("sT", [P, 2 * KC * B], F32, 129)
        self.wide = t.at("mod_wide", [P, 2 * KC, HD], F32, 130)
        self.rows = [t.at(f"mod_rows{layer}", [P, 6, D], F32, (32, 144)[layer]) for layer in range(2)]
        self.pick = t.at("mod_pick", [P, B, P], F32, 143)
        self.masks = t.at("masks", [P, 2 * P], F32, 138)
        self.sel = t.at("mod_sel", [P, B], F32, 131)
        self.t1 = t.at("gate_abs", [P, D], F32, 139)
        self.t2 = t.at("gate_sign", [P, D], F32, 141)
        self.ring = [t.at(f"wmod_ring{i}", [P, KC, D], F32, 64 + 8 * i) for i in range(self.SLOTS)]
        self.s_w = [sem(f"mod_w{i}") for i in range(self.SLOTS)]
        self.s_const, self.s_c = sem("mod_const"), sem("mod_c")
        self.s_silu, self.s_pick, self.s_ps = (sem(n) for n in ("mod_silu", "mod_pick", "mod_ps"))
        self.s_ev, self.s_tr, self.s_chain, self.s_out = (
            [sem(f"mod_{n}{layer}") for layer in range(2)] for n in ("ev", "tr", "chain", "out"))

    def load(self, nc, sp, t, layer):
        for s in range(6):
            n = 6 * layer + s
            if n >= self.SLOTS:
                sp.wait_ge(self.s_ps, n - self.SLOTS + 1)
            src = t.d_wmod[layer].rearrange("(k p) n -> p k n", p=P)[:, :, s * D:(s + 1) * D]
            sp.dma_start(self.ring[n % self.SLOTS][:, :, :], src).then_inc(self.s_w[n % self.SLOTS], 16)


def modulation(nc, t, m, psum, layer, prefetch=None):
    wide, sel = m.wide, m.sel
    cT, sT, t1, t2, masks, ring, s_w, rows, pick = m.cT, m.sT, m.t1, m.t2, m.masks, m.ring, m.s_w, m.rows[layer], m.pick
    s_const, s_c, s_silu, s_pick, s_ps = m.s_const, m.s_c, m.s_silu, m.s_pick, m.s_ps
    s_ev, s_tr, s_out = m.s_ev[layer], m.s_tr[layer], m.s_out[layer]
    SLOTS = m.SLOTS
    COLS, GATES = (0, 1, 3, 4), (2, 5)
    TURNED, SPREAD = psum[2], psum[4:8]

    with nc.Block() as block:
        if layer == 0:
            @block.sync
            def _(sp):
                sp.dma_start(t.const[:, :], t.d_const[:, 0:C_NEG]).then_inc(s_const, 16)
                sp.dma_start(masks[:, :], t.d_const[:, C_NEG:C_END]).then_inc(s_const, 16)
                for l in range(2):
                    for b in range(B):
                        src = t.d_c[l][b, :].rearrange("(k p) -> p k", p=P)
                        sp.dma_start(cT[:, l, :, b], src, allow_slow_non_contiguous=True).then_inc(s_c, 16)
                m.load(nc, sp, t, 0)
                prefetch(sp)
                m.load(nc, sp, t, 1)

            @block.scalar
            def _(act):
                act.wait_ge(s_c, 64)
                nc.scalar.activation(sT[:, :], cT[:, :, :, :].rearrange("p l k b -> p (l k b)"),
                                     ACT.Silu).then_inc(s_silu, 1)

        @block.vector
        def _(dve):
            link = chained(dve, m.s_chain[layer])
            if layer == 0:
                dve.wait_ge(s_const, 32)
                link(nc.vector.tensor_copy(t.ident_bf[:, :], t.ident))
                link(nc.vector.tensor_copy(t.neg_bf[:, :], masks[:, 0:P]))
                link(nc.vector.tensor_copy(t.negt_bf[:, :], masks[:, P:2 * P]))
                link(nc.vector.memset(t.avg[:, :], 1.0 / P))
                link(nc.vector.memset(wide[:, :, :], 0.0))
                for b in range(B):
                    ins = nc.vector.tensor_reduce(sel[:, b:b + 1],
                                                  t.ident.rearrange("p (k c) -> p c k", k=KC)[:, b:b + 1, :],
                                                  AX.X, ALU.add)
                link(ins)
                for b in range(B):
                    ins = nc.vector.tensor_copy(pick[:, b, :], sel[:, b:b + 1].broadcast_to([P, P]))
                link(ins)
                dve.wait_ge(s_silu, 1)
                nc.vector.tensor_copy(wide[:, :, 0:B], sT[:, :].rearrange("p (n b) -> p n b", b=B)).then_inc(s_pick, 1)
            for s in range(6):
                dve.wait_ge(s_ps, 6 * layer + s + 1)
                nc.vector.tensor_copy(rows[:, s, :], psum[s % 2][:, :]).then_inc(s_ev, 1)
            for n in range(2 * B):
                dve.wait_ge(s_tr, n + 1)
                ps = SPREAD[n][:, :]
                link(nc.vector.tensor_scalar(t2[:, :], ps, 0.25, None, ALU.max))
                link(nc.vector.scalar_tensor_tensor(out=t1[:, :], in0=ps, scalar=-1.0, in1=t2[:, :],
                                                    op0=ALU.mult, op1=ALU.max))
                link(nc.vector.tensor_scalar(t2[:, :], ps, 0.0, 2.0, ALU.is_ge, ALU.mult))
                link(nc.vector.scalar_tensor_tensor(out=t.gate[:, layer, n // B, n % B, :], in0=t2[:, :],
                                                    scalar=-1.0, in1=t1[:, :], op0=ALU.add, op1=ALU.mult))
            dve.wait_ge(s_tr, 2 * B + 1)
            for i in range(4):
                nc.vector.tensor_scalar(t.mod[:, layer, i, :], TURNED[:, i * KC * B:(i + 1) * KC * B],
                                        float(i % 2), None, ALU.add).then_inc(s_out, 1)
            dve.wait_ge(s_out, 4)

        @block.tensor
        def _(pe):
            if layer == 0:
                pe.wait_ge(s_pick, 1)
            for s in range(6):
                n = 6 * layer + s
                pe.wait_ge(s_w[n % SLOTS], 16 * (n // SLOTS + 1))
                if s >= 2:
                    pe.wait_ge(s_ev, s - 1)
                for k in range(KC):
                    mm = nc.tensor.matmul(psum[s % 2][HD * k:HD * (k + 1), :], wide[:, layer * KC + k, :],
                                          ring[n % SLOTS][:, k, :], start=True, stop=True)
                mm.then_inc(s_ps, 1)
            for n in range(2 * B):
                s = GATES[n // B]
                pe.wait_ge(s_ev, s + 1)
                nc.tensor.matmul(SPREAD[n][:, :], pick[:, n % B, :], rows[:, s, :],
                                 start=True, stop=True).then_inc(s_tr, 1)
            for i, s in enumerate(COLS):
                for j in range(KC):
                    at = (i * KC + j) * B
                    mm = nc.tensor.matmul(TURNED[:, at:at + B], rows[:, s, j * P:(j + 1) * P], pick[:, :, 0],
                                          start=True, stop=True)
            mm.then_inc(s_tr, 1)


class LatentLoads:

    def __init__(self, t, sem):
        self.W = {n: t.at("nat_" + n, [P, H * HD], F32, 144 + 2 * i) for i, n in enumerate(("dkv", "uk", "uv"))}
        self.S2 = {n: t.at("nat_" + n, [P, KC, HD], F32, 150 + i) for i, n in enumerate(("q", "o"))}
        self.lng = t.at("lngT", [P, H], F32, 152)
        self.lnb = t.at("lnbT", [P, H], F32, 153)
        self.s_w = sem("lat_w")

    def load(self, sp, t):
        for n, src in (("dkv", t.d_Wdkv), ("uk", t.d_Wuk), ("uv", t.d_Wuv)):
            sp.dma_start(self.W[n][:, :].rearrange("l (h d) -> l h d", h=H),
                         src.rearrange("h l d -> l h d")).then_inc(self.s_w, 16)
        for n, src in (("q", t.d_Wq), ("o", t.d_Woh)):
            sp.dma_start(self.S2[n][:, :, :], src.rearrange("(g a) i j -> (a i) g j", a=HG)).then_inc(self.s_w, 16)
        for dst, src in ((self.lng, t.d_lng), (self.lnb, t.d_lnb)):
            sp.dma_start(dst[:, :], src.rearrange("h l -> l h"),
                         allow_slow_non_contiguous=True).then_inc(self.s_w, 16)


def latent_weights(nc, t, lat, sem, psum):
    W, S2, lng, lnb, s_w = lat.W, lat.S2, lat.lng, lat.lnb, lat.s_w
    wc = t.at("wc", [P, D], F32, 154)
    wg = t.at("wg", [P, D], F32, 156)
    mt = {n: t.at("mid_" + n, [P, D], F32, 158 + 2 * i) for i, n in enumerate(("uk", "uv"))}
    nat = {n: t.at("bdn_" + n, [P, D], F32, 162 + 2 * i) for i, n in enumerate(("q", "o"))}
    bdt = {n: t.at("bdt_" + n, [P, D], F32, 166 + 2 * i) for i, n in enumerate(("q", "o"))}
    own = t.at("own_head", [P, KC, HG], F32, 170)
    col = {n: t.at("col_" + n, [P, KC], F32, 171 + i) for i, n in enumerate(("uk", "uv"))}
    s_pe, s_dve, s_chain = sem("lat_pe"), sem("lat_dve"), sem("lat_chain")
    pairs = (("uk", "q"), ("uv", "o"))

    def blk4(ap):
        return ap.rearrange("p (g c) -> p g c", g=KC)

    with nc.Block() as block:
        @block.tensor
        def _(pe):
            pe.wait_ge(s_w, 16 * 7)
            nc.tensor.matmul(psum[0][:, :], t.avg[:, :], W["dkv"][:, :], start=True, stop=True).then_inc(s_pe, 1)
            pe.wait_ge(s_dve, 1)
            for g in range(KC):
                c = slice(g * P, (g + 1) * P)
                nc.tensor.matmul(psum[1][:, c], wc[:, c], wc[:, c], start=True, stop=True)
                for i, (n, m) in enumerate(pairs):
                    nc.tensor.matmul(psum[2 + i][:, c], W[n][:, c], wg[:, c], start=True, stop=True)
                    nc.tensor.transpose(psum[4 + i][:, c], nat[m][:, c], t.ident)
                    mm = nc.tensor.matmul(psum[6][:, (i * KC + g) * HG:(i * KC + g + 1) * HG], W[n][:, c],
                                          lnb[:, g * HG:(g + 1) * HG], start=True, stop=True)
            mm.then_inc(s_pe, 1)
            pe.wait_ge(s_dve, 2)
            for i, (n, m) in enumerate(pairs):
                for g in range(KC):
                    c = slice(g * P, (g + 1) * P)
                    nc.tensor.matmul(psum[2 + i][:, c], mt[n][:, c], bdt[m][:, c], start=True, stop=True)
                    mm = nc.tensor.matmul(psum[7][:, i * KC + g:i * KC + g + 1], bdt[m][:, c],
                                          col[n][:, g:g + 1], start=True, stop=True)
            mm.then_inc(s_pe, 1)

        @block.vector
        def _(dve):
            link = chained(dve, s_chain)
            blk = t.blk.unsqueeze(1).broadcast_to([P, KC, P])
            dve.wait_ge(s_w, 16 * 7)
            dve.wait_ge(s_pe, 1)
            link(nc.vector.tensor_tensor(wc[:, :], W["dkv"][:, :], psum[0][:, :], ALU.subtract))
            link(nc.vector.tensor_tensor(wg[:, :].rearrange("l (h d) -> l h d", h=H),
                                         wc[:, :].rearrange("l (h d) -> l h d", h=H),
                                         lng[:, :].unsqueeze(2).broadcast_to([P, H, HD]), ALU.mult))
            for _, m in pairs:
                for g in range(KC):
                    ins = nc.vector.tensor_tensor(
                        nat[m][:, g * P:(g + 1) * P].rearrange("p (a j) -> p a j", a=HG),
                        S2[m][:, g, :].unsqueeze(1).broadcast_to([P, HG, HD]),
                        t.blk.rearrange("p (a j) -> p a j", a=HG), ALU.mult)
            ins.then_inc(s_dve, 1)
            dve.wait_ge(s_pe, 2)
            nc.vector.scalar_tensor_tensor(out=blk4(t.bd_m[:, :]), in0=blk4(psum[1][:, :]), scalar=1.0 / LAT,
                                           in1=blk, op0=ALU.mult, op1=ALU.mult)
            for i, (n, m) in enumerate(pairs):
                nc.vector.tensor_tensor(blk4(mt[n][:, :]), blk4(psum[2 + i][:, :]), blk, ALU.mult)
                nc.vector.tensor_copy(bdt[m][:, :], psum[4 + i][:, :])
                part = psum[6][:, i * KC * HG:(i + 1) * KC * HG].rearrange("p (g a) -> p g a", a=HG)
                link(nc.vector.tensor_tensor(own[:, :, :], part,
                                             t.blk4.unsqueeze(1).broadcast_to([P, KC, HG]), ALU.mult))
                link(nc.vector.tensor_reduce(col[n][:, :], own[:, :, :], AX.X, ALU.add))
            dve.wait_ge(s_chain, 6)
            nc.vector.memset(own[:, 0, 0:1], 0.0).then_inc(s_dve, 1)
            dve.wait_ge(s_pe, 3)
            scale = float(LAT) ** -0.5
            link(nc.vector.tensor_scalar(t.bd_k[:, :], psum[2][:, :], scale, None, ALU.mult))
            link(nc.vector.tensor_copy(t.bd_v[:, :], psum[3][:, :]))
            link(nc.vector.tensor_scalar(t.kb[:, :], psum[7][:, 0:KC], scale, None, ALU.mult))
            link(nc.vector.tensor_copy(t.vb[:, :], psum[7][:, KC:2 * KC]))


def layer_norm(nc, ctx, t, sem, psum, x, h, layer, half, name, loaded=None, save=None, tmp=128, prefetch=None, stats_done=False):
    xn = [t.at(f"{name}_xn{i}", [P, 4, D], F32, tmp + 8 * i) for i in range(2)]
    stats = t.stats
    mv = t.at(f"{name}_mv", [P, NT, 2], F32, tmp + 17)
    std = t.at(f"{name}_std", [P, NT], F32, tmp + 18)
    s_chain, s_var, s_std, s_xn, s_tr, s_ev, s_sv = (
        sem(f"{name}_{n}") for n in ("chain", "var", "std", "xn", "tr", "ev", "sv"))
    GR = NT // 4
    with nc.Block() as block:
        @block.sync
        def _(sp):
            if prefetch is not None:
                prefetch()
            if save is not None:
                sp.dma_start(save, x[:, :, :]).then_inc(s_sv, 16)
                sp.wait_ge(s_sv, 16)

        @block.vector
        def _(dve):
            link = chained(dve, s_chain)
            if loaded is not None:
                dve.wait_ge(loaded, 16 * GR)
            if not stats_done:
                for i in range(NT):
                    ins = nc.vector.bn_stats(stats[:, i, :], x[:, i, :])
                link(ins)
            for i in range(NT):
                ins = nc.vector.bn_aggr(mv[:, i, :], stats[:, i, :])
            link(ins)
            nc.vector.tensor_scalar(std[:, :], mv[:, :, 1], EPS, None, ALU.add).then_inc(s_var, 1)
            dve.wait_ge(s_std, 1)
            link(nc.vector.reciprocal(std[:, :], std[:, :]))
            for g in range(GR):
                if g >= 2:
                    dve.wait_ge(s_tr, g - 1)
                for i in range(4):
                    n = 4 * g + i
                    ins = nc.vector.tensor_scalar(xn[g % 2][:, i, :], x[:, n, :], mv[:, n, 0:1], std[:, n:n + 1],
                                                  ALU.subtract, ALU.mult)
                ins.then_inc(s_xn, 1)

        @block.tensor
        def _(pe):
            for g in range(GR):
                pe.wait_ge(s_xn, g + 1)
                if g >= 2:
                    pe.wait_ge(s_ev, 4 * (g - 1))
                for k in range(KC):
                    for i in range(4):
                        mm = nc.tensor.transpose(psum[4 * (g % 2) + k][:, i * P:(i + 1) * P],
                                                 xn[g % 2][:, i, k * P:(k + 1) * P], t.ident)
                mm.then_inc(s_tr, 1)

        @block.scalar
        def _(act):
            act.wait_ge(s_var, 1)
            nc.scalar.activation(std[:, :], std[:, :], ACT.Sqrt).then_inc(s_std, 1)
            for g in range(GR):
                act.wait_ge(s_tr, g + 1)
                b = g // NH
                for k in range(KC):
                    at = k * B + b
                    dst = h[:, b, k, (g % NH) * QC:(g % NH + 1) * QC] if half == 0 else h[:, g, k, :]
                    nc.scalar.activation(dst, psum[4 * (g % 2) + k][:, :],
                                         ACT.Identity, scale=t.mod[:, layer, 2 * half + 1, at:at + 1],
                                         bias=t.mod[:, layer, 2 * half, at:at + 1]).then_inc(s_ev, 1)


def latent_keys_values(nc, ctx, t, sem, psum, h, k_all, v_all):
    prod = [t.at(f"lat_prod{i}", [P, QC], F32, 128 + 2 * i) for i in range(4)]
    wide = [t.at(f"lat_wide{i}", [P, QC // P, HG, HD], F32, 136 + 2 * i) for i in range(2)]
    turned = [t.at(f"lat_turned{i}", [P, QC], F32, 140 + 2 * i) for i in range(2)]
    tmp = [t.at(f"lat_tmp{i}", [P, QC], F32, 144 + 2 * i) for i in range(2)]
    rt = t.at("lat_rt", [P, B * KC, QB, HG], F32, 148)
    s_y, s_prod, s_vt, s_rt, s_rtd, s_wide, s_turn, s_rb, s_kraw, s_mul, s_add, s_v, s_vev = (
        sem(f"lkv_{n}") for n in ("y", "prod", "vt", "rt", "rtd", "wide", "turn", "rb", "kraw", "mul", "add", "v",
                                  "vev"))
    N = B * KC * NH
    SUB = QC // P
    VT, PY = psum[0], psum[4:8]
    PT, PK, PV = psum[1:3], psum[3:5], psum[5:8]

    def place(n):
        i, c = divmod(n, NH)
        b, g = divmod(i, KC)
        return i, c, b, g

    with nc.Block() as block:
        @block.tensor
        def _(pe):
            def variance(n):
                i, c, _, _ = place(n)
                pe.wait_ge(s_prod, n + 1)
                for q in range(SUB):
                    at = (i * QB + c * SUB + q) * HG
                    mm = nc.tensor.matmul(VT[:, at:at + HG], prod[n % 4][:, q * P:(q + 1) * P], t.blk4,
                                          start=True, stop=True)
                mm.then_inc(s_vt, 1)

            for n in range(N):
                i, c, b, g = place(n)
                if n >= 4:
                    pe.wait_ge(s_prod, n - 3)
                nc.tensor.matmul(PY[n % 4][:, :], t.bd_m[:, g * P:(g + 1) * P], h[:, b, g, c * QC:(c + 1) * QC],
                                 start=True, stop=True).then_inc(s_y, 1)
                if n >= 2:
                    variance(n - 2)
            variance(N - 2)
            variance(N - 1)
            pe.wait_ge(s_prod, N)
            for n in range(N):
                i, c, b, g = place(n)
                gs = slice(g * P, (g + 1) * P)
                if n >= 3:
                    pe.wait_ge(s_vev, n - 2)
                for q in range(SUB):
                    at = c * QC + q * P
                    mm = nc.tensor.matmul(PV[n % 3][:, q * P:(q + 1) * P], h[:, b, g, at:at + P], t.bd_v[:, gs],
                                          start=True, stop=True)
                mm.then_inc(s_v, 1)
                if n >= 2:
                    pe.wait_ge(s_mul, n - 1)
                nc.tensor.matmul(PK[n % 2][:, :], t.bd_k[:, gs], h[:, b, g, c * QC:(c + 1) * QC], start=True,
                                 stop=True).then_inc(s_kraw, 1)
                pe.wait_ge(s_wide, n + 1)
                if n >= 2:
                    pe.wait_ge(s_rb, n - 1)
                for q in range(SUB):
                    mm = nc.tensor.transpose(PT[n % 2][:, q * P:(q + 1) * P],
                                             wide[n % 2][:, q, :, :].rearrange("p a c -> p (a c)"), t.ident)
                mm.then_inc(s_turn, 1)

        @block.vector
        def _(dve):
            for n in range(N):
                i, c, b, g = place(n)
                dve.wait_ge(s_y, n + 1)
                if n >= 4:
                    dve.wait_ge(s_vt, n - 3)
                nc.vector.tensor_tensor(prod[n % 4][:, :], PY[n % 4][:, :], h[:, b, g, c * QC:(c + 1) * QC],
                                        ALU.mult).then_inc(s_prod, 1)
            dve.wait_ge(s_vt, N)
            nc.vector.tensor_scalar(rt[:, :, :, :].rearrange("p i q a -> p (i q a)"), VT[:, 0:N * SUB * HG], EPS,
                                    None, ALU.add).then_inc(s_rt, 1)
            dve.wait_ge(s_rtd, 1)
            nc.vector.reciprocal(rt[:, :, :, :], rt[:, :, :, :]).then_inc(s_rt, 1)
            dve.wait_ge(s_rt, 2)

            def widen(n):
                i, c, _, _ = place(n)
                if n >= 2:
                    dve.wait_ge(s_turn, n - 1)
                at = rt[:, i, c * SUB:(c + 1) * SUB, :].rearrange("p q a -> p (q a)")
                nc.vector.tensor_copy(wide[n % 2][:, :, :, :].rearrange("p q a c -> p (q a) c"),
                                      at.unsqueeze(2).broadcast_to([P, SUB * HG, HD])).then_inc(s_wide, 1)

            widen(0)
            for n in range(N):
                i, c, _, _ = place(n)
                if n + 1 < N:
                    widen(n + 1)
                dve.wait_ge(s_v, n + 1)
                q = slice(c * SUB, (c + 1) * SUB)
                nc.vector.tensor_tensor(
                    v_all[:, i, q, :].rearrange("p q (a d) -> p (q a) d", a=HG),
                    PV[n % 3][:, :].rearrange("p (c d) -> p c d", d=HD),
                    rt[:, i, q, :].rearrange("p q a -> p (q a)").unsqueeze(2).broadcast_to([P, QC // HD, HD]),
                    ALU.mult).then_inc(s_vev, 1)
                dve.wait_ge(s_rb, n + 1)
                dve.wait_ge(s_kraw, n + 1)
                if n >= 2:
                    dve.wait_ge(s_add, n - 1)
                nc.vector.tensor_tensor(tmp[n % 2][:, :], PK[n % 2][:, :], turned[n % 2][:, :],
                                        ALU.mult).then_inc(s_mul, 1)

        @block.scalar
        def _(act):
            act.wait_ge(s_rt, 1)
            nc.scalar.activation(rt[:, :, :, :], rt[:, :, :, :], ACT.Sqrt).then_inc(s_rtd, 1)
            for n in range(N):
                act.wait_ge(s_turn, n + 1)
                if n >= 2:
                    act.wait_ge(s_mul, n - 1)
                nc.scalar.activation(turned[n % 2][:, :], PT[n % 2][:, :], ACT.Copy).then_inc(s_rb, 1)
                i, c, _, g = place(n)
                act.wait_ge(s_mul, n + 1)
                nc.scalar.activation(k_all[:, i, c * QC:(c + 1) * QC], tmp[n % 2][:, :], ACT.Identity,
                                     bias=t.kb[:, g:g + 1]).then_inc(s_add, 1)


class QkvLoads:

    def __init__(self, t, sem):
        self.w = t.at("wqkv", [P, 3, KC, D], F32, 128)
        self.bias = t.at("bqkv", [P, 3 * KC], F32, 176)
        self.s_w = sem("qkv_w")

    def load(self, sp, t):
        for part in range(3):
            sp.dma_start(self.w[:, part, :, :],
                         t.d_Wqkv.rearrange("(k p) n -> p k n", p=P)[:, :, part * D:(part + 1) * D]
                         ).then_inc(self.s_w, 16)
        sp.dma_start(self.bias[:, :], t.d_bqkv.rearrange("(c p) -> p c", p=P),
                     allow_slow_non_contiguous=True).then_inc(self.s_w, 16)


def project_qkv(nc, t, ld, sem, psum, h, q_all, k_all, v_all):
    w, bias, s_w = ld.w, ld.bias, ld.s_w
    w_lo = t.at("qkv_wlo", [P, 3, KC, D], FR, 128)
    w_hi = t.at("qkv_whi", [P, 3, KC, D], FR, 152)
    h_lo = t.at("qkv_hlo", [P, B, KC, S], FR, 32)
    under_q = t.at("qkv_hhi", [P, B, KC, S], FR, 0)
    s_whi, s_wlo, s_hhi, s_hlo, s_ps, s_ev, s_vb = (
        sem(f"qkv_{n}") for n in ("whi", "wlo", "hhi", "hlo", "ps", "ev", "vb"))
    GR = B * NH
    OUTS = 2 * KC + QC // P
    parts = [(i % 2, i // 2) for i in range(2 * KC)]

    def here(x, T):
        return x[:, T // NH, :, (T % NH) * QC:(T % NH + 1) * QC]

    def high(T):
        return here(under_q, T + 1) if T + 1 < GR else here(h_lo, 0)

    with nc.Block() as block:
        @block.tensor
        def _(pe):
            for T in range(GR):
                pe.wait_ge(s_hlo, T + 1)
                hi, lo = high(T), here(h_lo, T)
                for o in range(OUTS):
                    n = T * OUTS + o
                    if T == 0 and o in (0, 1, 2 * KC):
                        pe.wait_ge(s_wlo, (1, 2, 3)[(0, 1, 2 * KC).index(o)])
                    if n >= 8:
                        pe.wait_ge(s_ev, n - 7)
                    for k in range(KC):
                        for r, (a, z) in enumerate(((w_hi, hi), (w_hi, lo), (w_lo, hi))):
                            if o < 2 * KC:
                                part, g = parts[o]
                                left, right = a[:, part, k, g * P:(g + 1) * P], z[:, k, :]
                            else:
                                at = (o - 2 * KC) * P
                                left, right = z[:, k, at:at + P], a[:, 2, k, :]
                            mm = nc.tensor.matmul(psum[n % 8][:, :], left, right,
                                                  start=(k == 0 and r == 0), stop=(k == KC - 1 and r == 2))
                    mm.then_inc(s_ps, 1)

        @block.scalar
        def _(act):
            act.wait_ge(s_w, 64)
            for T in range(GR):
                if T == GR - 1:
                    act.wait_ge(s_ps, OUTS)
                elif T:
                    act.wait_ge(s_ps, (T - 1) * OUTS + 1)
                nc.scalar.activation(high(T), here(h, T), ACT.Copy).then_inc(s_hhi, 1)
                if T == 0:
                    for part in range(3):
                        nc.scalar.activation(w_hi[:, part, :, :], w[:, part, :, :], ACT.Copy).then_inc(s_whi, 1)

        @block.vector
        def _(dve):
            def low(T):
                dve.wait_ge(s_hhi, T + 1)
                nc.vector.tensor_tensor(here(h_lo, T), here(h, T), high(T).bitcast(F32),
                                        ALU.subtract).then_inc(s_hlo, 1)

            def low_weights(part):
                dve.wait_ge(s_whi, part + 1)
                nc.vector.tensor_tensor(w_lo[:, part, :, :], w[:, part, :, :], w_hi[:, part, :, :].bitcast(F32),
                                        ALU.subtract).then_inc(s_wlo, 1)

            scale = float(HD) ** -0.5
            low(0)
            for part in range(3):
                low_weights(part)
            nc.vector.tensor_copy(t.vb[:, :], bias[:, 2 * KC:3 * KC]).then_inc(s_vb, 1)
            for T in range(GR):
                b, c = divmod(T, NH)
                for o in range(OUTS):
                    n = T * OUTS + o
                    dve.wait_ge(s_ps, n + 1)
                    if o < 2 * KC:
                        part, g = parts[o]
                        nc.vector.tensor_scalar((q_all, k_all)[part][:, b * KC + g, c * QC:(c + 1) * QC],
                                                psum[n % 8][:, :], bias[:, part * KC + g:part * KC + g + 1],
                                                scale if part == 0 else 1.0, ALU.add, ALU.mult).then_inc(s_ev, 1)
                    else:
                        nc.vector.tensor_copy(v_all[:, b * KC:(b + 1) * KC, c * 4 + o - 2 * KC, :],
                                              psum[n % 8][:, :].rearrange("p (g c) -> p g c", g=KC)
                                              ).then_inc(s_ev, 1)
                    if o == 2 and T + 1 < GR:
                        low(T + 1)


HP = 2
STEPS = [(c, tb) for c in range(NH) for tb in range(4 * c + 4)]
NSTEP = len(STEPS)
S1_UNITS = [[(q, 0, a) for q in range(4) for a in range(HP)],
            [(q, c, a) for q in range(4, QB) for c in range(NH) for a in range(HP)]]
N_S1 = len(S1_UNITS[0]) + len(S1_UNITS[1])
N_S2 = NSTEP * HP
DIAG = [tb >= 4 * c for c, tb in STEPS]
S1_NEXT = [0, 0, 0, 0, 0, 3, 3, 2, 3, 2, 2, 2]
S1_OWNS = [3, 2, 2, 0, 0, 0, 0, 0, 0, 0, 0, 0]
S1_OWN = sum(S1_OWNS)
assert S1_OWN + sum(S1_NEXT) == N_S1
TURN_OWN, TURN_NEXT = 3, 9
PTS = 4
LAG = 2


def attention(nc, ctx, t, sem, psum, q_all, k_all, v_all, stack_at, name):
    TAIL = 128
    qs = [t.at(f"{name}_qs{p}", [P, HP, S], FR, stack_at + 16 * p) for p in range(2)]
    ks = [t.at(f"{name}_ks{p}", [P, HP, S], FR, stack_at + 16 * p + 8) for p in range(2)]
    qh, ql, kh, kl = (t.at(f"{name}_{n}", [P, S], FR, TAIL + 4 * i) for i, n in enumerate(("qh", "ql", "kh", "kl")))
    ve = [t.at(f"{name}_ve{p}", [P, QB, HP, 2 * HD], F32, TAIL + 16 + 4 * p) for p in range(2)]
    pt = [t.at(f"{name}_pt{p}", [P, HP, QC], F32, TAIL + 24 + 4 * p) for p in range(PTS)]
    nm = [t.at(f"{name}_nm{p}", [P, 4, 4, HD], F32, TAIL + 40 + 2 * p) for p in range(2)]
    raw = t.at(f"{name}_raw", [P, 2, N_S1], F32, TAIL + 44)
    neg = t.at(f"{name}_negmax", [P, 2, 4, HP], F32, TAIL + 44.25)
    res = [t.at(f"{name}_res{p}", [P, S], F32, TAIL + 44.5 + 4 * p) for p in range(2)]
    PS1, PS2, POD, PMT = psum[0:2], psum[2:5], psum[5:7], psum[7]
    s_st = [sem(f"{name}_stack{p}") for p in range(2)]
    s_res = [sem(f"{name}_res{p}") for p in range(2)]
    (s_seen, s_split, s_ve, s_init, s_s1, s_max, s_nm, s_mt, s_row, s_s2, s_exp, s_pv, s_od, s_nch) = (sem(f"{name}_{n}") for n in (
         "seen", "split", "ve", "init", "s1", "max", "nm", "mt", "row", "s2", "exp", "pv", "od", "nch"))
    NI = B * KC
    DMAS = 12

    def item_base(i, p, per):
        return i * (2 * per) + p * per

    with nc.Block() as block:
        @block.sync
        def _(sp):
            def stack(i, p):
                sp.wait_ge(s_split, i * 4 + 4)
                for r, (x, y) in enumerate(((qh, kh), (qh, kl), (ql, kh))):
                    for part, to in ((x, qs[p]), (y, ks[p])):
                        for a in range(HP):
                            src = part[64 * p + HD * a:64 * p + HD * a + HD, :].bitcast(F32)
                            sp.dma_start(to[HD * r:HD * r + HD, a, :].bitcast(F32), src).then_inc(s_st[p], 16)

            def result(i, p):
                sp.wait_ge(s_od, item_base(i, p, NH) + NH)
                for r, dst in enumerate((q_all, k_all)):
                    for a in range(HP):
                        sp.dma_start(dst[64 * p + HD * a:64 * p + HD * a + HD, i, :],
                                     res[p][64 * a + HD * r:64 * a + HD * r + HD, :]).then_inc(s_res[p], 16)

            stack(0, 0)
            stack(0, 1)
            with nc.sync.Fori(1, NI) as i:
                for p in range(2):
                    sp.wait_ge(s_s2, item_base(i, p, N_S2) - N_S2)
                    stack(i, p)
                    result(i - 1, p)
            for p in range(2):
                result(NI - 1, p)
            for p in range(2):
                sp.wait_ge(s_res[p], NI * 4 * 16)

        @block.gpsimd
        def _(pool):
            def held():
                nc.gpsimd.sem_inc(s_seen, 1)

            def split(i):
                held()
                for x, hi, lo in ((q_all, qh, ql), (k_all, kh, kl)):
                    nc.gpsimd.tensor_copy(hi[:, :], x[:, i, :]).then_inc(s_split, 1)
                pool.wait_ge(s_split, i * 4 + 2)
                held()
                for x, hi, lo in ((q_all, qh, ql), (k_all, kh, kl)):
                    nc.gpsimd.tensor_tensor(lo[:, :], x[:, i, :], hi[:, :].bitcast(F32),
                                            ALU.subtract).then_inc(s_split, 1)

            def values(i, p):
                held()
                for a in range(HP):
                    at = 64 * p + HD * a
                    ins = nc.gpsimd.tensor_copy(ve[p][:, :, a, 0:HD], v_all[:, i, :, at:at + HD])
                ins.then_inc(s_ve, 1)

            for p in range(2):
                nc.gpsimd.memset(ve[p][:, :, :, HD:2 * HD], 1.0).then_inc(s_init, 1)
                nc.gpsimd.memset(nm[p][:, :, :, :], 0.0).then_inc(s_init, 1)
            values(0, 0)

            def body(i, first, last):
                if not first:
                    pool.wait_ge(s_pv, item_base(i, 0, NSTEP))
                values(i, 1)
                if not last:
                    for q in range(2):
                        pool.wait_ge(s_st[q], i * (16 * DMAS) + 16 * DMAS)
                    split(i + 1)
                    pool.wait_ge(s_pv, item_base(i, 1, NSTEP))
                    values(i + 1, 0)

            body(0, True, False)
            with nc.gpsimd.Fori(1, NI - 1) as i:
                body(i, False, False)
            body(NI - 1, False, True)

        @block.tensor
        def _(pe):
            def score1(i, p, u0, u1):
                units = S1_UNITS[0] + S1_UNITS[1]
                for u in range(u0, u1):
                    q, c, a = units[u]
                    n = min(QC, (q + 1) * P - c * QC)
                    diag = c == q // 4
                    pe.wait_ge(s_max, item_base(i, p, N_S1) + u - 1)
                    mm = nc.tensor.matmul(PS1[u % 2][:, 0:n], qs[p][0:3 * HD, a, q * P:(q + 1) * P],
                                          ks[p][0:3 * HD, a, c * QC:c * QC + n], start=True, stop=not diag)
                    if diag:
                        mm = nc.tensor.matmul(PS1[u % 2][:, n - P:n], t.ident_bf[:, :], t.neg_bf[:, :],
                                              start=False, stop=True)
                    mm.then_inc(s_s1, 1)

            def turn(i, p, hf):
                pe.wait_ge(s_nm, item_base(i, p, 2) + hf + 1)
                if hf or not isinstance(i, int) or i or p:
                    pe.wait_ge(s_row, item_base(i, p, 2) + hf)
                for q in range(4):
                    mm = nc.tensor.transpose(PMT[:, q * P:(q + 1) * P],
                                             nm[hf][:, q, :, :].rearrange("p a c -> p (a c)"), t.ident)
                mm.then_inc(s_mt, 1)

            def pv(i, p, s):
                c, tb = STEPS[s]
                at = max(0, tb * P - c * QC)
                if tb == 0:
                    if c == 0:
                        pe.wait_ge(s_ve, item_base(i, p, 1) + 1)
                    if not (isinstance(i, int) and i == 0 and p == 0):
                        pe.wait_ge(s_od, item_base(i, p, 2) + c - 1)
                pe.wait_ge(s_exp, item_base(i, p, N_S2) + HP * s + HP)
                for a in range(HP):
                    mm = nc.tensor.matmul(POD[c][64 * a:64 * a + 64, at:QC], ve[p][:, tb, a, :],
                                          pt[s % PTS][:, a, at:QC], start=(tb == 0), stop=(tb == 4 * c + 3))
                mm.then_inc(s_pv, 1)

            def score2(i, p, s, a):
                c, tb = STEPS[s]
                at = max(0, tb * P - c * QC)
                u = HP * s + a
                if u >= 3 or not (isinstance(i, int) and i == 0 and p == 0):
                    pe.wait_ge(s_exp, item_base(i, p, N_S2) + u - 2)
                mm = nc.tensor.matmul(PS2[u % 3][:, at:QC], ks[p][:, a, tb * P:(tb + 1) * P],
                                      qs[p][:, a, c * QC + at:(c + 1) * QC], start=True, stop=not DIAG[s])
                if DIAG[s]:
                    mm = nc.tensor.matmul(PS2[u % 3][:, at:at + P], t.ident_bf[:, :], t.negt_bf[:, :],
                                          start=False, stop=True)
                mm.then_inc(s_s2, 1)

            def item(i, p, prev, nxt):
                k = 0
                for s, (c, tb) in enumerate(STEPS):
                    if tb == 0:
                        pe.wait_ge(s_row, item_base(i, p, 2) + c + 1)
                    ahead = [(nxt, k + m) for m in range(S1_NEXT[s])] if nxt is not None else []
                    k += len(ahead)
                    if S1_OWNS[s]:
                        ahead = [((i, p), N_S1 - S1_OWN + sum(S1_OWNS[:s]) + m) for m in range(S1_OWNS[s])]
                    if nxt is not None and S1_NEXT[s] and k == S1_NEXT[s]:
                        pe.wait_ge(s_st[nxt[1]], nxt[0] * (16 * DMAS) + 16 * DMAS)
                    for a in range(HP):
                        score2(i, p, s, a)
                        if ahead:
                            (it, u), ahead = ahead[0], ahead[1:]
                            score1(*it, u, u + 1)
                    if s == TURN_OWN:
                        turn(i, p, 1)
                    if nxt is not None and s == TURN_NEXT:
                        turn(*nxt, 0)
                    if s >= LAG:
                        pv(i, p, s - LAG)
                    elif prev is not None:
                        pv(*prev, NSTEP + s - LAG)
                    for it, u in ahead:
                        score1(*it, u, u + 1)

            pe.wait_ge(s_init, 6)
            pe.wait_ge(s_st[0], 16 * DMAS)
            for u, (q, c, a) in enumerate((S1_UNITS[0] + S1_UNITS[1])[:2]):
                nc.tensor.matmul(PS1[u][:, 0:P], qs[0][0:3 * HD, a, 0:P], ks[0][0:3 * HD, a, 0:P],
                                 start=True, stop=False)
                nc.tensor.matmul(PS1[u][:, 0:P], t.ident_bf[:, :], t.neg_bf[:, :], start=False,
                                 stop=True).then_inc(s_s1, 1)
            score1(0, 0, 2, N_S1 - S1_OWN)
            turn(0, 0, 0)

            def body(i, first, last):
                item(i, 0, None if first else (i - 1, 1), (i, 1))
                item(i, 1, (i, 0), None if last else (i + 1, 0))

            body(0, True, False)
            with nc.tensor.Fori(1, NI - 1) as i:
                body(i, False, False)
            body(NI - 1, False, True)
            for s in range(NSTEP - LAG, NSTEP):
                pv(NI - 1, 1, s)

        @block.scalar
        def _(act):
            def rows(i, p, hf):
                act.wait_ge(s_mt, item_base(i, p, 2) + hf + 1)
                for a in range(HP):
                    ins = nc.scalar.activation(qs[p][3 * HD:P, a, hf * QC:(hf + 1) * QC],
                                               PMT[64 + HD * a:64 + HD * a + HD, :], ACT.Copy)
                ins.then_inc(s_row, 1)

            def store(i, p, c):
                act.wait_ge(s_pv, item_base(i, p, NSTEP) + (4, 12)[c])
                if c == 0 and not (isinstance(i, int) and i == 0):
                    act.wait_ge(s_res[p], i * 64)
                nc.scalar.activation(res[p][:, c * QC:(c + 1) * QC], POD[c][:, :], ACT.Copy).then_inc(s_od, 1)

            def item(i, p, prev, nxt):
                for s, (c, tb) in enumerate(STEPS):
                    at = max(0, tb * P - c * QC)
                    if s >= PTS or prev is not None:
                        act.wait_ge(s_pv, item_base(i, p, NSTEP) + s - PTS + 1)
                    for a in range(HP):
                        u = HP * s + a
                        act.wait_ge(s_s2, item_base(i, p, N_S2) + u + 1)
                        nc.scalar.activation(pt[s % PTS][:, a, at:QC], PS2[u % 3][:, at:QC],
                                             ACT.Exp).then_inc(s_exp, 1)
                    if s == 1 and prev is not None:
                        store(*prev, 1)
                    if s == TURN_OWN:
                        rows(i, p, 1)
                    if s == 3 + LAG:
                        store(i, p, 0)
                    if nxt is not None and s == TURN_NEXT:
                        rows(*nxt, 0)

            for x, hi in ((q_all, qh), (k_all, kh)):
                nc.scalar.activation(hi[:, :], x[:, 0, :], ACT.Copy).then_inc(s_split, 1)
            rows(0, 0, 0)

            def body(i, first, last):
                item(i, 0, None if first else (i - 1, 1), (i, 1))
                item(i, 1, (i, 0), None if last else (i + 1, 0))

            body(0, True, False)
            with nc.scalar.Fori(1, NI - 1) as i:
                body(i, False, False)
            body(NI - 1, False, True)
            store(NI - 1, 1, 1)

        @block.vector
        def _(dve):
            def maxima(i, p, u0, u1):
                units = S1_UNITS[0] + S1_UNITS[1]
                for u in range(u0, u1):
                    q, c, a = units[u]
                    n = min(QC, (q + 1) * P - c * QC)
                    dve.wait_ge(s_s1, item_base(i, p, N_S1) + u + 1)
                    nc.vector.tensor_reduce(raw[:, p, u:u + 1], PS1[u % 2][:, 0:n], AX.X, ALU.max,
                                            negate=True).then_inc(s_max, 1)
                    for hf, end in enumerate((8, 24)):
                        if u + 1 == end:
                            parts(i, p, hf)

            def parts(i, p, hf):
                dve.wait_ge(s_max, item_base(i, p, N_S1) + (8, 24)[hf])
                if hf == 0:
                    m = raw[:, p, 0:8].rearrange("p (q a) -> p q a", a=HP)
                else:
                    m = neg[:, p, :, :]
                    both = raw[:, p, 8:24].rearrange("p (q c a) -> p q c a", c=NH, a=HP)
                    nc.vector.tensor_tensor(m, both[:, :, 0, :], both[:, :, 1, :], ALU.min).then_inc(s_nch, 1)
                    dve.wait_ge(s_nch, item_base(i, p, 3) + 2)
                if not (isinstance(i, int) and i == 0 and p == 0):
                    dve.wait_ge(s_mt, item_base(i, p, 2) + hf - 1)
                hi, lo = nm[hf][:, :, 2:4, 0], nm[hf][:, :, 2:4, 1]
                nc.vector.tensor_copy(hi.bitcast(FR), m).then_inc(s_nch, 1)
                dve.wait_ge(s_nch, item_base(i, p, 3) + (1, 3)[hf])
                nc.vector.tensor_tensor(lo, m, hi, ALU.subtract).then_inc(s_nm, 1)

            dve.wait_ge(s_split, 2)
            for x, hi, lo in ((q_all, qh, ql), (k_all, kh, kl)):
                nc.vector.tensor_tensor(lo[:, :], x[:, 0, :], hi[:, :].bitcast(F32),
                                        ALU.subtract).then_inc(s_split, 1)
            for p in range(2):
                nc.vector.memset(ks[p][3 * HD:P, :, :].bitcast(F32), 1.0).then_inc(s_init, 1)
            dve.wait_ge(s_init, 6)
            maxima(0, 0, 0, N_S1 - S1_OWN)

            def body(i, last):
                for it, nxt in (((i, 0), (i, 1)), ((i, 1), None if last else (i + 1, 0))):
                    maxima(*it, N_S1 - S1_OWN, N_S1)
                    if nxt is not None:
                        maxima(*nxt, 0, N_S1 - S1_OWN)

            body(0, False)
            with nc.vector.Fori(1, NI - 1) as i:
                body(i, False)
            body(NI - 1, True)


def divide(nc, ctx, t, sem, psum, o_all, o_lo, o_hi, den, name, prefetch):
    inv = [t.at(f"{name}_inv{i}", [P, QC // P, HG], F32, 170 + i) for i in range(2)]
    wide = [t.at(f"{name}_wide{i}", [P, QC // P, HG, HD], F32, 172 + 2 * i) for i in range(2)]
    s_t1, s_inv, s_wide, s_t2, s_div, s_hi, s_lo = (
        sem(f"{name}_{n}") for n in ("t1", "inv", "wide", "t2", "div", "hi", "lo"))
    N = B * KC * NH
    SUB = QC // P
    T1, T2 = psum[0:4], psum[4:8]
    with nc.Block() as block:
        @block.sync
        def _(sp):
            prefetch(sp)

        @block.tensor
        def _(pe):
            def back(n):
                pe.wait_ge(s_wide, n + 1)
                if n >= 4:
                    pe.wait_ge(s_div, n - 3)
                for q in range(SUB):
                    mm = nc.tensor.transpose(T2[n % 4][:, q * P:(q + 1) * P],
                                             wide[n % 2][:, q, :, :].rearrange("p a c -> p (a c)"), t.ident)
                mm.then_inc(s_t2, 1)

            for n in range(N):
                i, c = divmod(n, NH)
                if n >= 4:
                    pe.wait_ge(s_inv, n - 3)
                for q in range(SUB):
                    at = c * QC + q * P
                    mm = nc.tensor.transpose(T1[n % 4][:, q * P:(q + 1) * P], den[:, i, at:at + P], t.ident)
                mm.then_inc(s_t1, 1)
                if n >= 2:
                    back(n - 2)
            back(N - 2)
            back(N - 1)

        @block.scalar
        def _(act):
            for n in range(N):
                i, c = divmod(n, NH)
                act.wait_ge(s_div, n + 1)
                nc.scalar.activation(o_hi[:, i, c * QC:(c + 1) * QC], o_all[:, i, c * QC:(c + 1) * QC],
                                     ACT.Copy).then_inc(s_hi, 1)

        @block.gpsimd
        def _(pool):
            for n in range(N):
                i, c = divmod(n, NH)
                part = slice(c * QC, (c + 1) * QC)
                pool.wait_ge(s_hi, n + 1)
                nc.gpsimd.tensor_tensor(o_lo[:, i, part], o_all[:, i, part], o_hi[:, i, part].bitcast(F32),
                                        ALU.subtract).then_inc(s_lo, 1)

        @block.vector
        def _(dve):
            def product(n):
                i, c = divmod(n, NH)
                dve.wait_ge(s_t2, n + 1)
                here = o_all[:, i, c * QC:(c + 1) * QC]
                nc.vector.tensor_tensor(here, here, T2[n % 4][:, :], ALU.mult).then_inc(s_div, 1)

            for n in range(N):
                dve.wait_ge(s_t1, n + 1)
                if n >= 2:
                    dve.wait_ge(s_wide, n - 1)
                nc.vector.reciprocal(inv[n % 2][:, :, :],
                                     T1[n % 4][:, :].rearrange("p (q a c) -> p q a c", q=SUB, a=HG)[:, :, :, 0]
                                     ).then_inc(s_inv, 1)
                dve.wait_ge(s_inv, n + 1)
                if n >= 2:
                    dve.wait_ge(s_t2, n - 1)
                nc.vector.tensor_copy(wide[n % 2][:, :, :, :].rearrange("p q a c -> p (q a) c"),
                                      inv[n % 2][:, :, :].rearrange("p q a -> p (q a)").unsqueeze(2)
                                      .broadcast_to([P, SUB * HG, HD])).then_inc(s_wide, 1)
                if n >= 3:
                    product(n - 3)
            for n in range(N - 3, N):
                product(n)


class ProjectionLoads:

    def __init__(self, t, sem, name, layer, d_Wo, d_bo, x, x_src):
        self.wo = t.at(f"{name}_wo", [P, KC, D], F32, 160)
        self.bo = t.at(f"{name}_bo", [P, D], F32, 168)
        self.nat = t.at(f"{name}_nat", [P, KC, D], F32, 128) if layer == 0 else None
        self.s_w, self.s_x = sem(f"{name}_w"), sem(f"{name}_x")
        self.x, self.x_src, self.d_Wo, self.d_bo = x, x_src, d_Wo, d_bo

    def load(self, sp):
        sp.dma_start((self.wo if self.nat is None else self.nat)[:, :, :],
                     self.d_Wo.rearrange("(k p) n -> p k n", p=P)).then_inc(self.s_w, 16)
        sp.dma_start(self.bo[:, :], self.d_bo.rearrange("(o n) -> o n", o=1).broadcast_to([P, D])
                     ).then_inc(self.s_w, 16)
        for g in range(NT // 4):
            sp.dma_start(self.x[:, 4 * g:4 * g + 4, :], self.x_src[:, 4 * g:4 * g + 4, :]).then_inc(self.s_x, 16)


def output_projection(nc, ctx, t, sem, psum, o_lo, o_hi, ld, layer, name, prefetch=None):
    wo, bo, nat, x, s_w, s_x = ld.wo, ld.bo, ld.nat, ld.x, ld.s_w, ld.s_x
    shift = t.at(f"{name}_shift", [P, D], F32, 170)
    vbb = t.at(f"{name}_vbb", [P, KC, P], F32, 174)
    TMPS = 4
    tmp = [t.at(f"{name}_tmp{i}", [P, D], F32, 152 + 2 * i) for i in range(TMPS)]
    wo_hi, wo_lo = (t.at(f"{name}_wo_{n}", [P, KC, D], FR, kib) for n, kib in (("hi", 136), ("lo", 144)))
    s_tr, s_ev, s_whi, s_wlo, s_stats, s_vbb, s_bp, s_shift, s_ps, s_sum, s_tmp, s_add = (
        sem(f"{name}_{n}") for n in ("tr", "ev", "whi", "wlo", "stats", "vbb", "bp", "shift", "ps", "sum", "tmp",
                                     "add"))
    with nc.Block() as block:
        @block.sync
        def _(sp):
            if prefetch is not None:
                prefetch(sp)

        @block.tensor
        def _(pe):
            pe.wait_ge(s_w, 32)
            if layer == 0:
                for k in range(KC):
                    for j in range(KC):
                        mm = nc.tensor.transpose(psum[k][:, j * P:(j + 1) * P], nat[:, j, k * P:(k + 1) * P],
                                                 t.ident)
                    mm.then_inc(s_tr, 1)
                pe.wait_ge(s_ev, KC)
            pe.wait_ge(s_vbb, 1)
            for k in range(KC):
                mm = nc.tensor.matmul(psum[4][:, :], vbb[:, k, :], wo[:, k, :], start=(k == 0), stop=(k == KC - 1))
            mm.then_inc(s_bp, 1)
            pe.wait_ge(s_wlo, 1)
            for n in range(NT):
                b, q = divmod(n, QB)
                if n >= 4:
                    pe.wait_ge(s_sum, n - 3)
                for k in range(KC):
                    for r, (o, w) in enumerate(((o_hi, wo_hi), (o_hi, wo_lo), (o_lo, wo_hi))):
                        mm = nc.tensor.matmul(psum[n % 4][:, :], o[:, b * KC + k, q * P:(q + 1) * P], w[:, k, :],
                                              start=(k == 0 and r == 0), stop=(k == KC - 1 and r == 2))
                mm.then_inc(s_ps, 1)

        @block.scalar
        def _(act):
            if layer == 0:
                for k in range(KC):
                    act.wait_ge(s_tr, k + 1)
                    nc.scalar.activation(wo[:, k, :], psum[k][:, :], ACT.Copy).then_inc(s_ev, 1)
                act.wait_ge(s_ev, KC)
            else:
                act.wait_ge(s_w, 32)
            nc.scalar.activation(wo_hi[:, :, :], wo[:, :, :], ACT.Copy).then_inc(s_whi, 1)

        @block.vector
        def _(dve):
            nc.vector.tensor_copy(vbb[:, :, :], t.vb[:, :].unsqueeze(2).broadcast_to([P, KC, P])).then_inc(s_vbb, 1)
            dve.wait_ge(s_whi, 1)
            nc.vector.tensor_tensor(wo_lo[:, :, :], wo[:, :, :], wo_hi[:, :, :].bitcast(F32),
                                    ALU.subtract).then_inc(s_wlo, 1)
            dve.wait_ge(s_bp, 1)
            dve.wait_ge(s_w, 32)
            nc.vector.tensor_tensor(shift[:, :], psum[4][:, :], bo[:, :], ALU.add).then_inc(s_shift, 1)
            dve.wait_ge(s_shift, 1)
            for n in range(NT):
                dve.wait_ge(s_ps, n + 1)
                if n >= TMPS:
                    dve.wait_ge(s_add, n - TMPS + 1)
                nc.vector.tensor_tensor(tmp[n % TMPS][:, :], psum[n % 4][:, :], shift[:, :], ALU.add).then_inc(s_sum, 1)
                dve.wait_ge(s_sum, n + 1)
                nc.vector.tensor_tensor(tmp[n % TMPS][:, :], tmp[n % TMPS][:, :], t.gate[:, layer, 0, n // QB, :],
                                        ALU.mult).then_inc(s_tmp, 1)
                if n >= 3:
                    dve.wait_ge(s_add, n - 2)
                    nc.vector.bn_stats(t.stats[:, n - 3, :], x[:, n - 3, :]).then_inc(s_stats, 1)
            dve.wait_ge(s_add, NT)
            for n in range(NT - 3, NT):
                nc.vector.bn_stats(t.stats[:, n, :], x[:, n, :]).then_inc(s_stats, 1)

        @block.gpsimd
        def _(pool):
            pool.wait_ge(s_x, 16 * (NT // 4))
            for n in range(NT):
                pool.wait_ge(s_tmp, n + 1)
                nc.gpsimd.tensor_tensor(x[:, n, :], x[:, n, :], tmp[n % TMPS][:, :], ALU.add).then_inc(s_add, 1)


def route(nc, ctx, t, sem, psum, h, d_wgate, d_gates, prefetch):
    wg = t.at("rt_wg", [P, KC, E], F32, 160)
    lg = t.at("rt_logits", [P, NT, E], F32, 161)
    cmp_ = t.at("rt_cmp", [P, NT, E], F32, 162)
    rank = t.at("rt_rank", [P, NT, E], F32, 163)
    second = t.at("rt_second", [P, NT, E], F32, 164)
    m1, m2, ex, w1 = (t.at(f"rt_{n}", [P, NT], F32, 165 + 0.25 * i) for i, n in enumerate(("m1", "m2", "ex", "w1")))
    gt = t.at("rt_gt", [P, P], F32, 166)
    rows = t.at("rt_rows", [E, TOK], F32, 168)
    s_w, s_lt, s_lrow, s_lg, s_d, s_e, s_g, s_t, s_gt, s_out, s_chain = (
        sem(f"rt_{n}") for n in ("w", "lt", "lrow", "lg", "d", "e", "g", "t", "gt", "out", "chain"))
    with nc.Block() as block:
        @block.sync
        def _(sp):
            sp.dma_start(wg[:, :, :], d_wgate.rearrange("(k p) e -> p k e", p=P)).then_inc(s_w, 16)
            prefetch()
            sp.wait_ge(s_gt, 1)
            sp.dma_start(d_gates.rearrange("n e q -> (n e) q"), gt[:, :]).then_inc(s_out, 16)
            sp.wait_ge(s_out, 16)

        @block.tensor
        def _(pe):
            pe.wait_ge(s_w, 16)
            for T in range(NT // 4):
                for k in range(KC):
                    mm = nc.tensor.matmul(psum[2 + T][0:E, :], wg[:, k, :], h[:, T, k, :],
                                          start=(k == 0), stop=(k == KC - 1))
                mm.then_inc(s_lt, 1)
            for T in range(NT // 4):
                pe.wait_ge(s_lrow, T + 1)
                for n in range(4 * T, 4 * T + 4):
                    mm = nc.tensor.transpose(psum[0][:, n * E:(n + 1) * E], rows[:, n * P:(n + 1) * P],
                                             t.ident[0:E, 0:E])
            mm.then_inc(s_lg, 1)
            pe.wait_ge(s_g, 1)
            nc.tensor.transpose(psum[1][:, 0:P], rank[:, :, :].rearrange("p n e -> p (n e)"), t.ident).then_inc(s_t, 1)

        @block.scalar
        def _(act):
            for T in range(NT // 4):
                act.wait_ge(s_lt, T + 1)
                nc.scalar.activation(rows[:, T * QC:(T + 1) * QC], psum[2 + T][0:E, :], ACT.Copy).then_inc(s_lrow, 1)
            act.wait_ge(s_d, 1)
            nc.scalar.activation(ex[:, :], m2[:, :], ACT.Exp).then_inc(s_e, 1)

        @block.vector
        def _(dve):
            link = chained(dve, s_chain)
            tt, v = nc.vector.tensor_tensor, nc.vector
            dve.wait_ge(s_lg, 1)
            link(v.tensor_copy(lg[:, :, :].rearrange("p n e -> p (n e)"), psum[0][:, 0:NT * E]))
            link(v.memset(rank[:, :, :], 0.0))
            for e in range(E):
                one = lg[:, :, e:e + 1]
                ins = tt(cmp_[:, :, 0:e + 1], one.broadcast_to([P, NT, e + 1]), lg[:, :, 0:e + 1], ALU.is_gt)
                if e + 1 < E:
                    ins = tt(cmp_[:, :, e + 1:E], one.broadcast_to([P, NT, E - e - 1]), lg[:, :, e + 1:E], ALU.is_ge)
                link(ins)
                link(tt(rank[:, :, :], rank[:, :, :], cmp_[:, :, :], ALU.add))
            link(v.tensor_scalar(second[:, :, :], rank[:, :, :], 1.0, None, ALU.is_equal))
            link(v.tensor_scalar(rank[:, :, :], rank[:, :, :], 0.0, None, ALU.is_equal))
            link(v.tensor_reduce(m1[:, :], lg[:, :, :], AX.X, ALU.max))
            link(tt(cmp_[:, :, :], lg[:, :, :], second[:, :, :], ALU.mult))
            link(v.tensor_reduce(m2[:, :], cmp_[:, :, :], AX.X, ALU.add))
            tt(m2[:, :], m2[:, :], m1[:, :], ALU.subtract).then_inc(s_d, 1)
            dve.wait_ge(s_e, 1)
            link(v.tensor_scalar(w1[:, :], ex[:, :], 1.0, None, ALU.add))
            link(v.reciprocal(w1[:, :], w1[:, :]))
            link(tt(ex[:, :], ex[:, :], w1[:, :], ALU.mult))
            link(tt(rank[:, :, :], rank[:, :, :], w1[:, :].unsqueeze(2).broadcast_to([P, NT, E]), ALU.mult))
            link(tt(second[:, :, :], second[:, :, :], ex[:, :].unsqueeze(2).broadcast_to([P, NT, E]), ALU.mult))
            tt(rank[:, :, :], rank[:, :, :], second[:, :, :], ALU.add).then_inc(s_g, 1)
            dve.wait_ge(s_t, 1)
            v.tensor_copy(gt[:, :], psum[1][:, 0:P]).then_inc(s_gt, 1)


class FeedForwardBuffers:
    BLK = 2 * P
    NB = F // BLK

    def __init__(self, t, sem, name, kib):
        self.raw = [t.at(f"{name}_w{i}", [P, 3, KC * self.BLK], F32, kib + 24 * i) for i in range(2)]
        self.lo = [t.at(f"{name}_wlo{i}", [P, 3, KC * self.BLK], FR, kib + 24 * i) for i in range(2)]
        self.hi = [t.at(f"{name}_whi{i}", [P, 3, KC * self.BLK], FR, kib + 24 * i + 12) for i in range(2)]
        self.s_w = [sem(f"{name}_w{i}") for i in range(2)]

    def load(self, nc, slot, srcs):
        for which, src in enumerate(srcs):
            to = self.raw[slot][:, which, :]
            dst = to.rearrange("p (k m) -> p k m", k=KC) if which < 2 else to.rearrange("p (m d) -> p m d", d=D)
            nc.sync.dma_start(dst, src).then_inc(self.s_w[slot], 16)


def feed_forward(nc, ctx, t, sem, psum, h, h_lo, h_hi, x, bufs, sources, layer, name, at0, d_gates=None):
    BLK, NB = bufs.BLK, bufs.NB
    act_t = [t.at(f"{name}_act{i}", [P, QC], F32, at0 + 2 * i) for i in range(2)]
    hid = [t.at(f"{name}_hid{i}", [P, QC], F32, at0 + 4 + 2 * i) for i in range(2)]
    hid_lo = [t.at(f"{name}_hidlo{i}", [P, QC], FR, at0 + 4 + 2 * i) for i in range(2)]
    hid_hi = [t.at(f"{name}_hidhi{i}", [P, QC], FR, at0 + 8 + 2 * i) for i in range(2)]
    tmp = t.at(f"{name}_tmp", [P, 4, D], F32, at0 + 12)
    gb = [t.at(f"{name}_gb{i}", [P, QC], F32, at0 + 20 + 2 * i) for i in range(4)]
    (s_hh, s_h_split, s_whi, s_wlo, s_up, s_act, s_mul, s_prod, s_hi, s_lo, s_down, s_tmp, s_xa, s_seen,
     s_stats) = (
        sem(f"{name}_{n}") for n in ("hh", "h_split", "whi", "wlo", "up", "act", "mul", "prod", "hi", "lo",
                                     "down", "tmp", "xa", "seen", "stats"))
    s_g = [sem(f"{name}_g{i}") for i in range(4)]
    UP0, UP1, ACC = psum[0:2], psum[2:4], psum[4:8]
    gated = d_gates is not None
    SUB = QC // P
    GR = TOK // QC
    PER = 2 * GR
    at_first = lambda i, g: isinstance(i, int) and i == 0 and g == 0

    def chunk(i, g, c):
        return i * (2 * PER) + (2 * g + c)

    def parts(tile, which, slot):
        w = tile[slot][:, which, :]
        return w.rearrange("p (k m) -> p k m", k=KC) if which < 2 else w.rearrange("p (m d) -> p m d", d=D)

    def loop(eng, body):
        body(0, True, False)
        with eng.Fori(1, NB // 2 - 1) as i:
            body(i, False, False)
        body(NB // 2 - 1, False, True)

    with nc.Block() as block:
        @block.sync
        def _(sp):
            def gates(i, jj, T):
                if not (isinstance(i, int) and i == 0 and jj == 0):
                    sp.wait_ge(s_prod, chunk(i, GR * jj + T, 0) - 6)
                src = d_gates.rearrange("(t n) e q -> e t n q", n=SUB)[2 * i + jj, T:T + 1, :, :]
                sp.dma_start(gb[T][:, :].rearrange("p (n q) -> p n q", n=SUB),
                             src.broadcast_to([P, SUB, P])).then_inc(s_g[T], 16)

            def body(i, first, last):
                for jj in range(2):
                    if gated:
                        for T in range(GR):
                            gates(i, jj, T)
                    if not (first and jj == 0) and not (last and jj == 1):
                        sp.wait_ge(s_down, chunk(i, GR * jj, 0))
                        bufs.load(nc, 1 - jj, sources(2 * i + jj + 1))

            loop(nc.sync, body)

        @block.tensor
        def _(pe):
            def up(i, g, c):
                jj, T = divmod(g, GR)
                if c == 0:
                    if T == 0:
                        pe.wait_ge(s_wlo, (i * 2 + jj) * 3 + 2)
                    if at_first(i, 0) and jj == 0:
                        pe.wait_ge(s_h_split, T + 1)
                if not (at_first(i, g)):
                    pe.wait_ge(s_mul, chunk(i, g, c) - 1)
                for which, bank in ((0, UP0), (1, UP1)):
                    whi, wlo = parts(bufs.hi, which, jj), parts(bufs.lo, which, jj)
                    for k in range(KC):
                        col = slice(c * P, (c + 1) * P)
                        for r, (w, z) in enumerate(((whi, h_hi), (whi, h_lo), (wlo, h_hi))):
                            mm = nc.tensor.matmul(bank[c][:, :], w[:, k, col], z[:, T, k, :],
                                                  start=(k == 0 and r == 0), stop=(k == KC - 1 and r == 2))
                mm.then_inc(s_up, 1)

            def down(i, g, c):
                jj, T = divmod(g, GR)
                pe.wait_ge(s_lo, chunk(i, g, c) + 1)
                if T == 0 and c == 0:
                    pe.wait_ge(s_wlo, (i * 2 + jj) * 3 + 3)
                whi, wlo = parts(bufs.hi, 2, jj), parts(bufs.lo, 2, jj)
                for sub in range(SUB):
                    if c == 0 and not at_first(i, g):
                        pe.wait_ge(s_tmp, i * (SUB * PER) + SUB * (g - 1) + sub + 1)
                    col = slice(sub * P, (sub + 1) * P)
                    for r, (z, w) in enumerate(((hid_hi, whi), (hid_hi, wlo), (hid_lo, whi))):
                        mm = nc.tensor.matmul(ACC[sub][:, :], z[c][:, col], w[:, c, :],
                                              start=(c == 0 and r == 0), stop=(c == 1 and r == 2))
                mm.then_inc(s_down, 1)

            def body(i, first, last):
                for g in range(PER):
                    up(i, g, 0)
                    if g:
                        down(i, g - 1, 1)
                    elif not first:
                        down(i - 1, PER - 1, 1)
                    up(i, g, 1)
                    down(i, g, 0)

            loop(nc.tensor, body)
            down(NB // 2 - 1, PER - 1, 1)

        @block.scalar
        def _(act):
            def weights(i, jj, which):
                if which == 0:
                    act.wait_ge(bufs.s_w[jj], i * 48 + 48)
                nc.scalar.activation(bufs.hi[jj][:, which, :], bufs.raw[jj][:, which, :],
                                     ACT.Copy).then_inc(s_whi, 1)

            def silu(i, g, c):
                act.wait_ge(s_up, chunk(i, g, c) + 1)
                if not at_first(i, g):
                    act.wait_ge(s_mul, chunk(i, g, c) - 1)
                nc.scalar.activation(act_t[c][:, :], UP0[c][:, :], ACT.Silu).then_inc(s_act, 1)

            def high(i, g, c):
                act.wait_ge(s_prod if gated else s_mul, chunk(i, g, c) + 1)
                nc.scalar.activation(hid_hi[c][:, :], hid[c][:, :], ACT.Copy).then_inc(s_hi, 1)

            def body(i, first, last):
                for g in range(PER):
                    for c in range(2):
                        silu(i, g, c)
                        high(i, g, c)
                    jj, T = divmod(g, GR)
                    if T and not (last and jj):
                        weights(i + jj, 1 - jj, T - 1)

            weights(0, 0, 0)
            weights(0, 0, 1)
            for T in range(GR):
                if T == 1:
                    weights(0, 0, 2)
                nc.scalar.activation(h_hi[:, T, :, :], h[:, T, :, :], ACT.Copy).then_inc(s_hh, 1)
            loop(nc.scalar, body)

        @block.vector
        def _(dve):
            def weights(i, jj, which):
                dve.wait_ge(s_whi, (i * 2 + jj) * 3 + which + 1)
                nc.vector.tensor_tensor(bufs.lo[jj][:, which, :], bufs.raw[jj][:, which, :], bufs.hi[jj][:, which, :].bitcast(F32),
                                        ALU.subtract).then_inc(s_wlo, 1)

            def product(i, g, c):
                n = chunk(i, g, c)
                dve.wait_ge(s_act, n + 1)
                if not at_first(i, g):
                    dve.wait_ge(s_down, n - 1)
                here = hid[c][:, :]
                nc.vector.tensor_tensor(here, act_t[c][:, :], UP1[c][:, :], ALU.mult).then_inc(s_mul, 1)
                if gated:
                    jj, T = divmod(g, GR)
                    if c == 0:
                        dve.wait_ge(s_g[T], (i * 2 + jj) * 16 + 16)
                    dve.wait_ge(s_mul, n + 1)
                    nc.vector.tensor_tensor(here, here, gb[T][:, :], ALU.mult).then_inc(s_prod, 1)

            def residual(i, g, final=False):
                T = g % GR
                dve.wait_ge(s_down, chunk(i, g, 1) + 1)
                for sub in range(SUB):
                    m = i * (SUB * PER) + (SUB * g + sub)
                    if not at_first(i, g):
                        dve.wait_ge(s_xa, m - 3)
                    nc.vector.tensor_tensor(tmp[:, sub, :], ACC[sub][:, :], t.gate[:, layer, 1, T // NH, :],
                                            ALU.mult).then_inc(s_tmp, 1)
                for sub in range(SUB):
                    m = i * (SUB * PER) + (SUB * g + sub)
                    dve.wait_ge(s_tmp, m + 1)
                    here = x[:, T * SUB + sub, :]
                    nc.vector.tensor_tensor(here, here, tmp[:, sub, :], ALU.add).then_inc(s_xa, 1)
                if final:
                    for sub in range(SUB):
                        dve.wait_ge(s_xa, i * (SUB * PER) + (SUB * g + sub) + 1)
                        nc.vector.bn_stats(t.stats[:, T * SUB + sub, :], x[:, T * SUB + sub, :]).then_inc(s_stats, 1)

            def body(i, first, last):
                for g in range(PER):
                    product(i, g, 0)
                    if g:
                        residual(i, g - 1, last and gated and g > GR)
                    elif not first:
                        residual(i - 1, PER - 1)
                    product(i, g, 1)
                    jj, T = divmod(g, GR)
                    if T and not (last and jj):
                        weights(i + jj, 1 - jj, T - 1)

            weights(0, 0, 0)
            weights(0, 0, 1)
            for T in range(GR):
                if T == 1:
                    weights(0, 0, 2)
                dve.wait_ge(s_hh, T + 1)
                nc.vector.tensor_tensor(h_lo[:, T, :, :], h[:, T, :, :], h_hi[:, T, :, :].bitcast(F32),
                                        ALU.subtract).then_inc(s_h_split, 1)
            loop(nc.vector, body)
            residual(NB // 2 - 1, PER - 1, gated)

        @block.gpsimd
        def _(pool):
            def body(i, first, last):
                for g in range(PER):
                    for c in range(2):
                        pool.wait_ge(s_hi, chunk(i, g, c) + 1)
                        nc.gpsimd.sem_inc(s_seen, 1)
                        nc.gpsimd.tensor_tensor(hid_lo[c][:, :], hid[c][:, :],
                                                hid_hi[c][:, :].bitcast(F32), ALU.subtract).then_inc(s_lo, 1)

            loop(nc.gpsimd, body)


def ffn_weights(nc, ctx, t, sem, psum, w1, w3, wd, nat, s_nat, spare, stores):
    ring = [t.at(f"fw_ring{i}", [P, 4, D], F32, kib) for i, kib in enumerate((160, 168, 112, 120))]
    s_ld = [sem(f"fw_ld{i}") for i in range(4)]

    def slot(n):
        return n if n < 4 else n % 2

    turned = [t.at(f"fw_turned{i}", [P, D], F32, 176 + 2 * i) for i in range(2)]
    s_tr, s_ev, s_had, s_hev, s_dev, s_bd, s_bp, s_t2, s_tev = (
        sem(f"fw_{n}") for n in ("tr", "ev", "had", "hev", "dev", "bd", "bp", "t2", "tev"))
    s_st = [sem(f"fw_stored{i}") for i in range(3)]
    d_count = [[sum(FC // (2 << s) for s in range(st + 1)) for st in range(4)]] * 2
    NW = 2 * (F // QC)
    NT2 = KC
    FINAL = 2 * d_count[0][3]
    NBL = F // (2 * P)
    with nc.Block() as block:
        @block.sync
        def _(sp):
            def load(n):
                which, j = divmod(n, 4)
                sp.dma_start(ring[slot(n)][:, :, :],
                             (t.d_W1, t.d_W3)[which].rearrange("(c p) d -> p c d", p=P)[:, 4 * j:4 * j + 4, :]
                             ).then_inc(s_ld[slot(n)], 16)

            def store(which, w):
                sp.wait_ge(s_ev, 16 * which + 16)
                for j in range(NBL):
                    sp.dma_start(stores[which][j, :, :, :], w[:, :, j * 2 * P:(j + 1) * 2 * P]).then_inc(s_st[which], 16)

            for n in range(NW):
                if n >= 4:
                    sp.wait_ge(s_tr, KC * (n % 2 + 1 if n < 6 else n - 1))
                load(n)
            store(0, w1)
            store(1, w3)
            for j in range(NBL):
                sp.wait_ge(s_hev, j + 1)
                sp.wait_ge(s_dev, j + 1)
                sp.dma_start(stores[2][j, :, :, :], wd[:, 2 * j:2 * j + 2, :]).then_inc(s_st[2], 16)
            sp.wait_ge(s_st[0], 16 * NBL)

        @block.tensor
        def _(pe):
            for n in range(NW):
                pe.wait_ge(s_ld[slot(n)], 16 if n < 4 else 16 * (n // 2))
                for k in range(KC):
                    m = KC * n + k
                    if m >= 8:
                        pe.wait_ge(s_ev, m - 7)
                    for i in range(4):
                        mm = nc.tensor.transpose(psum[m % 8][:, i * P:(i + 1) * P], ring[slot(n)][:, i, k * P:(k + 1) * P],
                                                 t.ident)
                    mm.then_inc(s_tr, 1)
            pe.wait_ge(s_bd, FINAL)
            pe.wait_ge(s_bp, FINAL)

            def hadamard(c):
                pe.wait_ge(s_tev, c + 1)
                if c >= 4:
                    pe.wait_ge(s_dev if c % 2 else s_hev, (c - 4) // 2 + 1)
                nc.tensor.matmul(psum[4 + c % 4][:, :], t.had, turned[c % 2][:, :], start=True, stop=True).then_inc(s_had, 1)

            for c in range(FC):
                pe.wait_ge(s_ev, KC * NW)
                if c >= 4:
                    pe.wait_ge(s_tev, c - 3)
                for j in range(NT2):
                    mm = nc.tensor.transpose(psum[c % 4][:, j * P:(j + 1) * P], nat[:, j, c, :], t.ident)
                mm.then_inc(s_t2, 1)
                if c:
                    hadamard(c - 1)
            hadamard(FC - 1)

        def product(eng, c):
            eng.wait_ge(s_had, c + 1)
            if c % 2 == 0:
                nc.scalar.activation(wd[:, c, :], psum[4 + c % 4][:, :], ACT.Copy).then_inc(s_hev, 1)
            else:
                nc.vector.tensor_copy(wd[:, c, :], psum[4 + c % 4][:, :]).then_inc(s_dev, 1)

        @block.scalar
        def _(act):
            for m in range(KC * NW):
                n, k = divmod(m, KC)
                which, j = divmod(n, 4)
                act.wait_ge(s_tr, m + 1)
                nc.scalar.activation((w1, w3)[which][:, k, j * QC:(j + 1) * QC], psum[m % 8][:, :],
                                     ACT.Copy).then_inc(s_ev, 1)
            for c in range(FC):
                act.wait_ge(s_t2, c + 1)
                if c >= 2:
                    act.wait_ge(s_had, c - 1)
                nc.scalar.activation(turned[c % 2][:, :], psum[c % 4][:, :], ACT.Copy).then_inc(s_tev, 1)
                if c >= 2 and c % 2 == 0:
                    product(act, c - 2)
            product(act, FC - 2)

        def butterfly(eng, mine, which):
            cols = slice(0, 80) if which == 0 else slice(80, P)
            eng.wait_ge(s_nat, 16 * NT2)
            for st in range(4):
                src, dst = (nat, spare) if st % 2 == 0 else (spare, nat)
                d = 1 << st
                if st:
                    eng.wait_ge(mine, 2 * d_count[which][st - 1])
                for a in range(FC // (2 * d)):
                    at = 2 * d * a
                    lo, hi = src[:, :, at:at + d, cols], src[:, :, at + d:at + 2 * d, cols]
                    eng.tensor_tensor(dst[:, :, at:at + d, cols], lo, hi, ALU.add).then_inc(mine, 1)
                    eng.tensor_tensor(dst[:, :, at + d:at + 2 * d, cols], lo, hi, ALU.subtract).then_inc(mine, 1)

        @block.vector
        def _(dve):
            butterfly(dve, s_bd, 0)
            for c in range(1, FC, 2):
                product(dve, c)

        @block.gpsimd
        def _(pool):
            butterfly(pool, s_bp, 1)

    def stored():
        for which in (1, 2):
            nc.sync.wait_ge(s_st[which], 16 * NBL)
    return stored


def build(nc, d, d_const, d_out):
    ctx = ExitStack()
    with ctx:
        t = Shared()

        def sb(name, shape, dt=F32):
            return ctx.enter_context(nc.sbuf_tensor(name, shape, dt))

        sems = ExitStack()

        used = []

        def sem(name):
            used.append(sems.enter_context(nc.semaphore(name)))
            return used[-1]

        psum = [ctx.enter_context(nc.psum_tensor(f"bank{i}", [P, QC], F32)) for i in range(8)]

        t.const = sb("const", [P, C_NEG])
        t.ident, t.blk = t.const[:, C_ID:C_ID + P], t.const[:, C_BLK:C_BLK + P]
        t.had = t.const[:, C_HAD:C_HAD + P]
        t.blk4 = t.const[:, C_BLK:C_BLK + P:HD]
        t.ident_bf, t.neg_bf, t.negt_bf = (sb(n, [P, P], BF16) for n in ("ident_bf", "neg_bf", "negt_bf"))
        t.avg = sb("avg", [P, P])
        t.mod = sb("mod", [P, 2, 4, KC * B])
        t.gate = sb("gate", [P, 2, 2, B, D])
        t.bd_m, t.bd_k, t.bd_v = (sb(n, [P, D]) for n in ("bd_m", "bd_k", "bd_v"))
        t.kb, t.vb = sb("kb", [P, KC]), sb("vb", [P, KC])
        t.eps = sb("eps", [P, 1])
        t.stats = sb("norm_stats", [P, NT, 6])
        base = 43 * 1024

        def at(name, shape, dt, kib):
            return nc.alloc_sbuf_tensor_at(name, shape, dt, offset=base + int(kib * 1024))
        t.at = at

        t.d_const = d_const
        t.d_c = [d["L0_c"], d["L1_c"]]
        t.d_wmod = [d["L0_wmod"], d["L1_wmod"]]
        t.d_Wdkv, t.d_Wuk, t.d_Wuv = d["L0_attn_Wdkv"], d["L0_attn_Wuk"], d["L0_attn_Wuv"]
        t.d_Wq, t.d_Woh, t.d_lng, t.d_lnb = d["L0_attn_Wq"], d["L0_attn_Wo_h"], d["L0_attn_ln_g"], d["L0_attn_ln_b"]
        t.d_Wqkv, t.d_bqkv = d["L1_attn_Wqkv"], d["L1_attn_bqkv"]
        t.d_W1, t.d_W2, t.d_W3 = d["L1_ffn_W1"], d["L1_ffn_W2"], d["L1_ffn_W3"]
        d_x = d["L0_attn_x"].rearrange("b (n p) d -> p (b n) d", p=P)
        d_res = nc.dram_tensor("x_mid", [P, NT, D], F32, kind="Internal").ap()
        d_gates = nc.dram_tensor("gates", [NT, E, P], F32, kind="Internal").ap()
        d_y = d_out.rearrange("b (n p) d -> p (b n) d", p=P)

        def region(name, kib, shape):
            return at(name, shape, F32, kib)

        def finish(x):
            s = sem("stored")
            with nc.Block() as block:
                @block.sync
                def _(sp):
                    sp.dma_start(d_y, x[:, :, :]).then_inc(s, 16)
                    sp.wait_ge(s, 16)

        s_eps = sem("eps_set")
        with nc.Block() as block:
            @block.vector
            def _(dve):
                nc.vector.memset(t.eps[:, :], EPS).then_inc(s_eps, 1)
                dve.wait_ge(s_eps, 1)

        x = region("x_l0a", 0, [P, NT, D])
        h = region("h_l0a", 32, [P, B, KC, S])
        mod, lat, s_x = Modulation(t, sem), LatentLoads(t, sem), sem("x_loaded")

        def load_x(sp, x, src, s):
            for g in range(NT // 4):
                sp.dma_start(x[:, 4 * g:4 * g + 4, :], src[:, 4 * g:4 * g + 4, :]).then_inc(s, 16)

        def first_loads(sp):
            lat.load(sp, t)
            load_x(sp, x, d_x, s_x)

        modulation(nc, t, mod, psum, 0, prefetch=first_loads)
        latent_weights(nc, t, lat, sem, psum)
        layer_norm(nc, ctx, t, sem, psum, x, h, 0, 0, "ln0a", loaded=s_x, tmp=144)
        modulation(nc, t, mod, psum, 1)
        k_all = region("k_l0", 64, [P, B * KC, S])
        v_all = region("v_l0", 96, [P, B * KC, QB, P])
        latent_keys_values(nc, ctx, t, sem, psum, h, k_all, v_all)
        q_all = h[:, :, :, :].rearrange("p b k s -> p (b k) s")
        attention(nc, ctx, t, sem, psum, q_all, k_all, v_all, 0, "at0")
        x = region("x_l0b", 0, [P, NT, D])
        ld = ProjectionLoads(t, sem, "op0", 0, d["L0_attn_Wo"], d["L0_attn_bo"], x, d_x)
        o_lo, o_hi = at("o_lo_l0", [P, B * KC, S], FR, 32), at("o_hi_l0", [P, B * KC, S], FR, 96)
        divide(nc, ctx, t, sem, psum, q_all, o_lo, o_hi, k_all, "dv0", ld.load)
        output_projection(nc, ctx, t, sem, psum, o_lo, o_hi, ld, 0, "op0")
        h = region("h_l0b", 32, [P, NT // 4, KC, QC])
        h_lo, h_hi = (at(f"h_l0b_{n}", [P, NT // 4, KC, QC], FR, kib) for n, kib in (("lo", 32), ("hi", 64)))
        layer_norm(nc, ctx, t, sem, psum, x, h, 0, 1, "ln0b", tmp=144, stats_done=True)
        ups = [d[n].rearrange("e (k p) m -> e p k m", p=P) for n in ("L0_ffn_wi_0", "L0_ffn_wi_1")]
        downs = d["L0_ffn_wo"].rearrange("e (m p) d -> e p m d", p=P)
        bufs = FeedForwardBuffers(t, sem, "moe", 96)

        def expert(j):
            return [w[j, :, :, :] for w in (*ups, downs)]

        route(nc, ctx, t, sem, psum, h, d["L0_ffn_w_gate"], d_gates,
              prefetch=lambda: [bufs.load(nc, j, expert(j)) for j in range(2)])
        feed_forward(nc, ctx, t, sem, psum, h, h_lo, h_hi, x, bufs, expert, 0, "moe", 144, d_gates=d_gates)

        numbers = sorted(s.num for s in used)
        assert numbers == list(range(numbers[0], numbers[-1] + 1))
        with nc.Block() as block:
            @block.sync
            def _(sp):
                sp.sem_clear(range(numbers[0], numbers[-1] + 1))
        sems.close()
        h = region("h_l1a", 32, [P, B, KC, S])
        qkv = QkvLoads(t, sem)
        layer_norm(nc, ctx, t, sem, psum, x, h, 1, 0, "ln1a", save=d_res, tmp=64, stats_done=True,
                   prefetch=lambda: qkv.load(nc.sync, t))
        q_all, k_all = region("q_l1", 0, [P, B * KC, S]), region("k_l1", 64, [P, B * KC, S])
        v_all = region("v_l1", 96, [P, B * KC, QB, P])
        project_qkv(nc, t, qkv, sem, psum, h, q_all, k_all, v_all)
        attention(nc, ctx, t, sem, psum, q_all, k_all, v_all, 32, "at1")
        x = region("x_l1b", 32, [P, NT, D])
        ld = ProjectionLoads(t, sem, "op1", 1, d["L1_attn_Wo"], d["L1_attn_bo"], x, d_res)
        o_lo, o_hi = at("o_lo_l1", [P, B * KC, S], FR, 0), at("o_hi_l1", [P, B * KC, S], FR, 96)
        divide(nc, ctx, t, sem, psum, q_all, o_lo, o_hi, k_all, "dv1", ld.load)
        nat, s_nat = region("ffn_nat", 64, [P, KC, FC, P]), sem("ffn_nat_loaded")

        def load_w2(sp):
            for j in range(KC):
                sp.dma_start(nat[:, j, :, :], d["L1_ffn_W2"][j * P:(j + 1) * P, :].rearrange("p (c f) -> p c f", c=FC)
                             ).then_inc(s_nat, 16)

        output_projection(nc, ctx, t, sem, psum, o_lo, o_hi, ld, 1, "op1", load_w2)
        w1, w3 = region("ffn_w1", 0, [P, KC, F]), region("ffn_w3", 96, [P, KC, F])
        wd, spare = region("ffn_wd", 128, [P, FC, D]), region("ffn_spare", 128, [P, KC, FC, P])
        blocks = [nc.dram_tensor(f"ffn_blocks{n}", [F // (2 * P), P, *m], F32, kind="Internal").ap()
                  for n, m in enumerate(((KC, 2 * P), (KC, 2 * P), (2, D)))]
        stored = ffn_weights(nc, ctx, t, sem, psum, w1, w3, wd, nat, s_nat, spare, blocks)
        h = region("h_l1b", 0, [P, NT // 4, KC, QC])
        h_lo, h_hi = (at(f"h_l1b_{n}", [P, NT // 4, KC, QC], FR, kib) for n, kib in (("lo", 0), ("hi", 64)))
        bufs = FeedForwardBuffers(t, sem, "ffn", 96)

        def hidden_block(j):
            return [w[j, :, :, :] for w in blocks]

        def first_blocks():
            stored()
            for j in range(2):
                bufs.load(nc, j, hidden_block(j))

        layer_norm(nc, ctx, t, sem, psum, x, h, 1, 1, "ln1b", tmp=64, stats_done=True, prefetch=first_blocks)
        feed_forward(nc, ctx, t, sem, psum, h, h_lo, h_hi, x, bufs, hidden_block, 1, "ffn", 144)
        finish(x)


_INS = ["L0_attn_x", "L0_attn_Wq", "L0_attn_Wdkv", "L0_attn_Wuk", "L0_attn_Wuv", "L0_attn_ln_g", "L0_attn_ln_b",
        "L0_attn_Wo_h", "L0_attn_Wo", "L0_attn_bo", "L0_ffn_w_gate", "L0_ffn_wi_0", "L0_ffn_wi_1", "L0_ffn_wo",
        "L0_c", "L0_wmod", "L1_attn_Wqkv", "L1_attn_bqkv", "L1_attn_Wo", "L1_attn_bo", "L1_ffn_W1", "L1_ffn_W2",
        "L1_ffn_W3", "L1_c", "L1_wmod"]


def kernel(**inputs):
    import numpy as _np
    import concourse.bacc as _bacc
    from concourse import mybir as _mybir
    from concourse.bass_utils import run_bass_kernel_spmd as _run

    nc = _bacc.Bacc("TRN2", target_bir_lowering=False, num_devices=1)
    arrays, aps = {}, {}
    for name in _INS:
        a = _np.ascontiguousarray(inputs[name])
        arrays[f"in_{name}"] = a
        aps[name] = nc.dram_tensor(f"in_{name}", a.shape, _mybir.dt.from_np(a.dtype), kind="ExternalInput").ap()
    table = constant_table()
    arrays["in_constants"] = table
    consts = nc.dram_tensor("in_constants", table.shape, F32, kind="ExternalInput").ap()
    out = nc.dram_tensor("out_x", (B, S, D), F32, kind="ExternalOutput").ap()
    build(nc, aps, consts, out)
    r = _run(nc, [arrays], core_ids=[0])
    return r.results[0]["out_x"]
```
